# Optimizing a Trainium2 kernel written in Bass

```python
import numpy as np
import jax
import jax.numpy as jnp

def _softmax(x, axis=-1):
    return jax.nn.softmax(x, axis=axis)

def _gelu(x):
    return jax.nn.gelu(x, approximate=True)

def _silu(x):
    return jax.nn.silu(x)

def _sigmoid(x):
    return jax.nn.sigmoid(x)

def _layernorm(x, axis=-1, eps=1e-05):
    m = jnp.mean(x, axis=axis, keepdims=True)
    v = jnp.var(x, axis=axis, keepdims=True)
    return (x - m) / jnp.sqrt(v + eps)

def _scatter_add(tgt, idx, src, axis=0):
    return tgt.at[idx].add(src)

def _segment_sum(src, seg, n):
    return jax.ops.segment_sum(src, seg, n)
kernel_name = 'mk_perceiver_d2_seqx_r4_0a54f1'

def setup_inputs(seed: int=0):
    np.random.seed(seed)
    _w = jnp.asarray

    def _rec_inputs():
        import jax
        import jax.numpy as jnp
        _rk = jax.random.key(seed)
        x = 4.136e-05 + 0.9999 * jax.random.normal(jax.random.fold_in(_rk, 1), (2, 256, 256), jnp.float32)
        _lenS = 256 - jax.random.randint(jax.random.fold_in(_rk, 7), (2,), 0, max(1, 256 // 4) + 1, jnp.int32)
        _lenS2 = 4096 - jax.random.randint(jax.random.fold_in(_rk, 8), (2,), 0, max(1, 4096 // 4) + 1, jnp.int32)
        _ctx_1024P = jax.random.normal(jax.random.fold_in(_rk, 11), (2, 16, 256), jnp.float32)
        _ctx_1024c = jax.random.dirichlet(jax.random.fold_in(_rk, 511), 0.3 * jnp.ones((16,), jnp.float32), (2, 4096))
        _ctx_1024t = jnp.einsum('bsk,bkd->bsd', _ctx_1024c, _ctx_1024P)
        _ctx_1024t = _ctx_1024t * jax.lax.rsqrt(jnp.mean(jnp.square(_ctx_1024t)) + 1e-12) * 0.953939
        ctx_1024 = 7.22013e-05 + 1.00017 * (_ctx_1024t + 0.3 * jax.random.normal(jax.random.fold_in(_rk, 611), (2, 4096, 256), jnp.float32))
        _validS = jnp.arange(256)[None, :] < _lenS[:, None]
        _validS2 = jnp.arange(4096)[None, :] < _lenS2[:, None]
        _causal = jnp.tril(jnp.ones((256, 256), dtype=bool))
        mask_BxS2_bk1 = jnp.broadcast_to(_validS2[:, :], (2, 4096))
        return (x, ctx_1024, mask_BxS2_bk1)
    x, ctx_1024, mask_BxS2_bk1 = _rec_inputs()

    def _L0_xattn_setup():
        import jax, jax.numpy as jnp
        import numpy as np
        B, S, T, D, H = (4, 512, 512, 256, 16)
        HD = D // H
        key = jax.random.key(seed)
        ks = jax.random.split(key, 7)
        src = jax.random.normal(ks[0], (B, S, D), dtype=jnp.float32)
        tgt = jax.random.normal(ks[1], (B, T, D), dtype=jnp.float32)
        attention_mask = jax.random.bernoulli(ks[2], 0.9, (B, S))
        scale = 1.0 / np.sqrt(D)
        Wq = jax.random.normal(ks[3], (D, D), dtype=jnp.float32) * scale
        Wk = jax.random.normal(ks[4], (D, D), dtype=jnp.float32) * scale
        Wv = jax.random.normal(ks[5], (D, D), dtype=jnp.float32) * scale
        Wo = jax.random.normal(ks[6], (D, D), dtype=jnp.float32) * scale
        return {'src': src, 'tgt': tgt, 'attention_mask': attention_mask, 'Wq': Wq, 'Wk': Wk, 'Wv': Wv, 'Wo': Wo}
    _L0_xattn_all = _L0_xattn_setup()
    _L0_xattn_in = {k: v for k, v in _L0_xattn_all.items() if k in ('Wq', 'Wk', 'Wv', 'Wo')}
    del _L0_xattn_all

    def _L0_attn_setup():
        import jax, jax.numpy as jnp
        from jax import lax
        import numpy as np
        DIM = 256
        HEADS = 16
        B, N = (2, 512)

        def sn_dense(x, W, u, sigma_param):
            v = lax.stop_gradient(W @ u)
            v = lax.stop_gradient(v / jnp.linalg.norm(v, ord=2))
            u2 = lax.stop_gradient(W.T @ v)
            u2 = lax.stop_gradient(u2 / jnp.linalg.norm(u2, ord=2))
            sigma = jnp.einsum('c,cd,d->', v, W, u2)
            return x @ (sigma_param[0] / sigma * W)
        key = jax.random.key(seed)
        ks = jax.random.split(key, 5)
        std = 0.1
        batch = jax.random.normal(ks[0], (B, N, DIM), dtype=jnp.float32)
        W_qkv = jax.random.normal(ks[1], (DIM, 3 * DIM), dtype=jnp.float32) * std
        W_proj = jax.random.normal(ks[2], (DIM, DIM), dtype=jnp.float32) * std
        u_qkv = jax.random.normal(ks[3], (3 * DIM,), dtype=jnp.float32)
        u_qkv = u_qkv / jnp.linalg.norm(u_qkv)
        u_proj = jax.random.normal(ks[4], (DIM,), dtype=jnp.float32)
        u_proj = u_proj / jnp.linalg.norm(u_proj)
        sigma_qkv = jnp.ones((1,), dtype=jnp.float32)
        sigma_proj = jnp.ones((1,), dtype=jnp.float32)
        return {'batch': batch, 'W_qkv': W_qkv, 'u_qkv': u_qkv, 'sigma_qkv': sigma_qkv, 'W_proj': W_proj, 'u_proj': u_proj, 'sigma_proj': sigma_proj}
    _L0_attn_all = _L0_attn_setup()
    _L0_attn_in = {k: v for k, v in _L0_attn_all.items() if k in ('W_qkv', 'u_qkv', 'sigma_qkv', 'W_proj', 'u_proj', 'sigma_proj')}
    del _L0_attn_all

    def _L0_ffn_setup():
        import jax, jax.numpy as jnp
        import numpy as np
        TAU = 1.0
        K_ROUTE = 3
        EPS = 1e-08

        def _route_combine_weights(x_addr, U, k, tau):
            z = x_addr @ U.T
            topv, topi = jax.lax.top_k(z, k)
            w = jax.nn.softmax(topv / (tau + EPS), axis=1)
            N, L = z.shape
            rows = jnp.arange(N)[:, None]
            return jnp.zeros((N, L), z.dtype).at[rows, topi].add(w)

        def _mixture(inp, C, W):
            L = W.shape[0]
            y = jnp.zeros((inp.shape[0], W.shape[1]), inp.dtype)
            for e in range(L):
                y = y + C[:, e:e + 1] * (inp @ W[e].T)
            return y
        key = jax.random.key(seed)
        ks = jax.random.split(key, 8)
        B, T, D_in, H, D_out, L, d_addr = (8, 2048, 256, 256, 256, 12, 64)

        def unit_rows(k, L_, d_):
            U = jax.random.normal(k, (L_, d_), dtype=jnp.float32)
            U = U - U.mean(axis=1, keepdims=True)
            return U / (jnp.linalg.norm(U, axis=1, keepdims=True) + EPS)

        def norm_tape(k, shape):
            W = jax.random.normal(k, shape, dtype=jnp.float32)
            n = jnp.sqrt(jnp.sum(W * W, axis=tuple(range(1, W.ndim)), keepdims=True)) + 1e-12
            return W / n
        x = jax.random.normal(ks[0], (B, T, D_in), dtype=jnp.float32)
        P_w = jax.random.normal(ks[1], (d_addr, D_in), dtype=jnp.float32) / np.sqrt(D_in)
        U1 = unit_rows(ks[2], L, d_addr)
        U2 = unit_rows(ks[3], L, d_addr)
        U3 = unit_rows(ks[4], L, d_addr)
        W1 = norm_tape(ks[5], (L, H, D_in))
        W2 = norm_tape(ks[6], (L, D_out, H))
        b2 = norm_tape(ks[7], (L, D_out))
        return {'x': x, 'P_w': P_w, 'U1': U1, 'U2': U2, 'U3': U3, 'W1': W1, 'W2': W2, 'b2': b2}
    _L0_ffn_all = _L0_ffn_setup()
    _L0_ffn_in = {k: v for k, v in _L0_ffn_all.items() if k in ('P_w', 'U1', 'U2', 'U3', 'W1', 'W2', 'b2')}
    del _L0_ffn_all

    def _L1_xattn_setup():
        import jax, jax.numpy as jnp
        import numpy as np
        N_HEAD, MODEL_DIM, KEY_DIM, VALUE_DIM = (16, 256, 64, 64)
        B, S = (4, 512)
        EPS = 1e-05
        TEMP = float(np.sqrt(KEY_DIM))
        key = jax.random.key(seed)
        ks = jax.random.split(key, 12)
        d = {'query': jax.random.normal(ks[0], (B, S, MODEL_DIM), jnp.float32), 'key': jax.random.normal(ks[1], (B, S, MODEL_DIM), jnp.float32), 'value': jax.random.normal(ks[2], (B, S, MODEL_DIM), jnp.float32), 'Wq': jax.random.normal(ks[3], (MODEL_DIM, N_HEAD * KEY_DIM), jnp.float32) * np.sqrt(2.0 / (MODEL_DIM + KEY_DIM)), 'bq': jnp.zeros((N_HEAD * KEY_DIM,), jnp.float32), 'Wk': jax.random.normal(ks[4], (MODEL_DIM, N_HEAD * KEY_DIM), jnp.float32) * np.sqrt(2.0 / (MODEL_DIM + KEY_DIM)), 'bk': jnp.zeros((N_HEAD * KEY_DIM,), jnp.float32), 'Wv': jax.random.normal(ks[5], (MODEL_DIM, N_HEAD * VALUE_DIM), jnp.float32) * np.sqrt(2.0 / (MODEL_DIM + VALUE_DIM)), 'bv': jnp.zeros((N_HEAD * VALUE_DIM,), jnp.float32), 'Wo': jax.random.normal(ks[6], (N_HEAD * VALUE_DIM, MODEL_DIM), jnp.float32) * np.sqrt(2.0 / (N_HEAD * VALUE_DIM + MODEL_DIM)), 'bo': jnp.zeros((MODEL_DIM,), jnp.float32), 'ln_gamma': jnp.ones((MODEL_DIM,), jnp.float32), 'ln_beta': jnp.zeros((MODEL_DIM,), jnp.float32)}
        return d
    _L1_xattn_all = _L1_xattn_setup()
    _L1_xattn_in = {k: v for k, v in _L1_xattn_all.items() if k in ('Wq', 'bq', 'Wk', 'bk', 'Wv', 'bv', 'Wo', 'bo', 'ln_gamma', 'ln_beta')}
    del _L1_xattn_all

    def _L1_attn_setup():
        import jax, jax.numpy as jnp
        import numpy as np
        B, S, E = (4, 256, 256)
        H = 16
        D = E // H
        key = jax.random.key(seed)
        kx, kq, kk, kv, ko = jax.random.split(key, 5)
        scale = 1.0 / np.sqrt(2.0 * E)
        return {'x': jax.random.normal(kx, (B, S, E), dtype=jnp.float32), 'Wq': jax.random.normal(kq, (E, E), dtype=jnp.float32) * scale, 'Wk': jax.random.normal(kk, (E, E), dtype=jnp.float32) * scale, 'Wv': jax.random.normal(kv, (E, E), dtype=jnp.float32) * scale, 'Wo': jax.random.normal(ko, (E, E), dtype=jnp.float32) * scale}
    _L1_attn_all = _L1_attn_setup()
    _L1_attn_in = {k: v for k, v in _L1_attn_all.items() if k in ('Wq', 'Wk', 'Wv', 'Wo')}
    del _L1_attn_all

    def _L1_ffn_setup():
        import jax, jax.numpy as jnp
        import numpy as np
        BLOCK = 32
        W_BITS = 4
        ACT_BITS = 16

        def act_qdq(x):
            qmax = 2.0 ** (ACT_BITS - 1) - 1.0
            scale = jnp.maximum(jnp.max(jnp.abs(x)) / qmax, 1e-12)
            return jnp.clip(jnp.round(x / scale), -qmax - 1.0, qmax) * scale

        def fixed_qdq_u16(x):
            scale = 1.0 / 65536.0
            return jnp.clip(jnp.round(x / scale), 0.0, 65535.0) * scale

        def lpbq_dequant(w):
            O, I = w.shape
            qmax = 2.0 ** (W_BITS - 1) - 1.0
            wb = w.reshape(O, I // BLOCK, BLOCK)
            s = jnp.maximum(jnp.max(jnp.abs(wb), axis=-1, keepdims=True) / qmax, 1e-12)
            wq = jnp.clip(jnp.round(wb / s), -qmax - 1.0, qmax) * s
            return wq.reshape(O, I)
        key = jax.random.key(seed)
        k1, k2, k3, k4 = jax.random.split(key, 4)
        B, S, H, I = (2, 1024, 256, 768)
        x = jax.random.normal(k1, (B, S, H), jnp.float32)
        w_gate = jax.random.normal(k2, (I, H), jnp.float32) * 0.02
        w_up = jax.random.normal(k3, (I, H), jnp.float32) * 0.02
        w_down = jax.random.normal(k4, (H, I), jnp.float32) * 0.02
        return {'x': x, 'w_gate': w_gate, 'w_up': w_up, 'w_down': w_down}
    _L1_ffn_all = _L1_ffn_setup()
    _L1_ffn_in = {k: v for k, v in _L1_ffn_all.items() if k in ('w_gate', 'w_up', 'w_down')}
    del _L1_ffn_all
    return {'x': x, 'ctx_1024': ctx_1024, 'mask_BxS2_bk1': mask_BxS2_bk1, 'L0_xattn_Wq': _L0_xattn_in['Wq'], 'L0_xattn_Wk': _L0_xattn_in['Wk'], 'L0_xattn_Wv': _L0_xattn_in['Wv'], 'L0_xattn_Wo': _L0_xattn_in['Wo'], 'L0_attn_W_qkv': _L0_attn_in['W_qkv'], 'L0_attn_u_qkv': _L0_attn_in['u_qkv'], 'L0_attn_sigma_qkv': _L0_attn_in['sigma_qkv'], 'L0_attn_W_proj': _L0_attn_in['W_proj'], 'L0_attn_u_proj': _L0_attn_in['u_proj'], 'L0_attn_sigma_proj': _L0_attn_in['sigma_proj'], 'L0_ffn_P_w': _L0_ffn_in['P_w'], 'L0_ffn_U1': _L0_ffn_in['U1'], 'L0_ffn_U2': _L0_ffn_in['U2'], 'L0_ffn_U3': _L0_ffn_in['U3'], 'L0_ffn_W1': _L0_ffn_in['W1'], 'L0_ffn_W2': _L0_ffn_in['W2'], 'L0_ffn_b2': _L0_ffn_in['b2'], 'L1_xattn_Wq': _L1_xattn_in['Wq'], 'L1_xattn_bq': _L1_xattn_in['bq'], 'L1_xattn_Wk': _L1_xattn_in['Wk'], 'L1_xattn_bk': _L1_xattn_in['bk'], 'L1_xattn_Wv': _L1_xattn_in['Wv'], 'L1_xattn_bv': _L1_xattn_in['bv'], 'L1_xattn_Wo': _L1_xattn_in['Wo'], 'L1_xattn_bo': _L1_xattn_in['bo'], 'L1_xattn_ln_gamma': _L1_xattn_in['ln_gamma'], 'L1_xattn_ln_beta': _L1_xattn_in['ln_beta'], 'L1_attn_Wq': _L1_attn_in['Wq'], 'L1_attn_Wk': _L1_attn_in['Wk'], 'L1_attn_Wv': _L1_attn_in['Wv'], 'L1_attn_Wo': _L1_attn_in['Wo'], 'L1_ffn_w_gate': _L1_ffn_in['w_gate'], 'L1_ffn_w_up': _L1_ffn_in['w_up'], 'L1_ffn_w_down': _L1_ffn_in['w_down']}

def reference(x, ctx_1024, mask_BxS2_bk1, L0_xattn_Wq, L0_xattn_Wk, L0_xattn_Wv, L0_xattn_Wo, L0_attn_W_qkv, L0_attn_u_qkv, L0_attn_sigma_qkv, L0_attn_W_proj, L0_attn_u_proj, L0_attn_sigma_proj, L0_ffn_P_w, L0_ffn_U1, L0_ffn_U2, L0_ffn_U3, L0_ffn_W1, L0_ffn_W2, L0_ffn_b2, L1_xattn_Wq, L1_xattn_bq, L1_xattn_Wk, L1_xattn_bk, L1_xattn_Wv, L1_xattn_bv, L1_xattn_Wo, L1_xattn_bo, L1_xattn_ln_gamma, L1_xattn_ln_beta, L1_attn_Wq, L1_attn_Wk, L1_attn_Wv, L1_attn_Wo, L1_ffn_w_gate, L1_ffn_w_up, L1_ffn_w_down):
    import jax
    import jax.numpy as jnp

    def _L0_xattn_ref(src, tgt, attention_mask, Wq, Wk, Wv, Wo):
        import jax, jax.numpy as jnp
        import numpy as np
        B, S, T, D, H = (4, 512, 512, 256, 16)
        HD = D // H
        b, s, d = src.shape
        t = tgt.shape[1]
        q = (tgt @ Wq.T).reshape(b, t, H, HD).transpose(0, 2, 1, 3)
        k = (src @ Wk.T).reshape(b, s, H, HD).transpose(0, 2, 1, 3)
        v = (src @ Wv.T).reshape(b, s, H, HD).transpose(0, 2, 1, 3)
        scores = jnp.einsum('bhtd,bhsd->bhts', q, k) / np.sqrt(HD)
        mask = attention_mask[:, None, None, :]
        scores = jnp.where(mask, scores, -jnp.inf)
        attn = jax.nn.softmax(scores, axis=-1)
        out = jnp.einsum('bhts,bhsd->bhtd', attn, v)
        out = out.transpose(0, 2, 1, 3).reshape(b, t, d)
        return out @ Wo.T

    def _L0_attn_ref(batch, W_qkv, u_qkv, sigma_qkv, W_proj, u_proj, sigma_proj):
        import jax, jax.numpy as jnp
        from jax import lax
        import numpy as np
        DIM = 256
        HEADS = 16
        B, N = (2, 512)

        def sn_dense(x, W, u, sigma_param):
            v = lax.stop_gradient(W @ u)
            v = lax.stop_gradient(v / jnp.linalg.norm(v, ord=2))
            u2 = lax.stop_gradient(W.T @ v)
            u2 = lax.stop_gradient(u2 / jnp.linalg.norm(u2, ord=2))
            sigma = jnp.einsum('c,cd,d->', v, W, u2)
            return x @ (sigma_param[0] / sigma * W)
        b, n, d = batch.shape
        h = HEADS
        hd = d // h
        qkv = sn_dense(batch, W_qkv, u_qkv, sigma_qkv)
        q, k, v = jnp.split(qkv, 3, axis=-1)
        split_heads = lambda t: t.reshape(b, n, h, hd).transpose(0, 2, 1, 3)
        q, k, v = (split_heads(q), split_heads(k), split_heads(v))
        scale = hd ** (-0.5)
        att = jnp.einsum('bhqd,bhkd->bhqk', q, k) * scale
        causal = jnp.tril(jnp.ones((n, n), dtype=jnp.float32))
        big_neg = jnp.finfo(att.dtype).min
        att = jnp.where(causal[None, None] == 0, big_neg, att)
        att = jax.nn.softmax(att, axis=-1)
        x = jnp.einsum('bhqk,bhkd->bhqd', att, v)
        x = x.transpose(0, 2, 1, 3).reshape(b, n, d)
        x = sn_dense(x, W_proj, u_proj, sigma_proj)
        return x

    def _L0_ffn_ref(x, P_w, U1, U2, U3, W1, W2, b2):
        import jax, jax.numpy as jnp
        import numpy as np
        TAU = 1.0
        K_ROUTE = 3
        EPS = 1e-08

        def _route_combine_weights(x_addr, U, k, tau):
            z = x_addr @ U.T
            topv, topi = jax.lax.top_k(z, k)
            w = jax.nn.softmax(topv / (tau + EPS), axis=1)
            N, L = z.shape
            rows = jnp.arange(N)[:, None]
            return jnp.zeros((N, L), z.dtype).at[rows, topi].add(w)

        def _mixture(inp, C, W):
            L = W.shape[0]
            y = jnp.zeros((inp.shape[0], W.shape[1]), inp.dtype)
            for e in range(L):
                y = y + C[:, e:e + 1] * (inp @ W[e].T)
            return y
        B, T, D = x.shape
        xf = x.reshape(B * T, D)
        xa = xf @ P_w.T
        C1 = _route_combine_weights(xa, U1, K_ROUTE, TAU)
        C2 = _route_combine_weights(xa, U2, K_ROUTE, TAU)
        C3 = _route_combine_weights(xa, U3, K_ROUTE, TAU)
        h = jax.nn.gelu(_mixture(xf, C1, W1), approximate=False)
        y = _mixture(h, C2, W2) + C3 @ b2
        return y.reshape(B, T, -1)

    def _L1_xattn_ref(query, key, value, Wq, bq, Wk, bk, Wv, bv, Wo, bo, ln_gamma, ln_beta):
        import jax, jax.numpy as jnp
        import numpy as np
        N_HEAD, MODEL_DIM, KEY_DIM, VALUE_DIM = (16, 256, 64, 64)
        B, S = (4, 512)
        EPS = 1e-05
        TEMP = float(np.sqrt(KEY_DIM))
        b, sq, _ = query.shape
        residual = query
        q = (query @ Wq + bq).reshape(b, sq, N_HEAD, KEY_DIM)
        k = (key @ Wk + bk).reshape(b, key.shape[1], N_HEAD, KEY_DIM)
        v = (value @ Wv + bv).reshape(b, value.shape[1], N_HEAD, VALUE_DIM)
        scores = jnp.einsum('bqhd,bkhd->bhqk', q, k) / TEMP
        attn = jax.nn.softmax(scores, axis=-1)
        out = jnp.einsum('bhqk,bkhd->bqhd', attn, v).reshape(b, sq, N_HEAD * VALUE_DIM)
        out = out @ Wo + bo + residual
        mu = jnp.mean(out, axis=-1, keepdims=True)
        var = jnp.var(out, axis=-1, keepdims=True)
        return (out - mu) * jax.lax.rsqrt(var + EPS) * ln_gamma + ln_beta

    def _L1_attn_ref(x, Wq, Wk, Wv, Wo):
        import jax, jax.numpy as jnp
        import numpy as np
        B, S, E = (4, 256, 256)
        H = 16
        D = E // H
        b, s, e = x.shape

        def split_heads(t):
            return t.reshape(b, s, H, D).transpose(0, 2, 1, 3)
        q = split_heads(x @ Wq)
        k = split_heads(x @ Wk)
        v = split_heads(x @ Wv)
        qc = q - q.mean(axis=-1, keepdims=True)
        kc = k - k.mean(axis=-1, keepdims=True)
        cov = jnp.einsum('bhsd,bhtd->bhst', qc, kc) / D
        q_var = jnp.var(q, axis=-1, ddof=1)
        k_var = jnp.var(k, axis=-1, ddof=1)
        var_comp = q_var[..., :, None] * k_var[..., None, :] / D
        scores = cov + var_comp
        attn = jax.nn.softmax(scores, axis=-1)
        out = jnp.einsum('bhst,bhtd->bhsd', attn, v)
        out = out.transpose(0, 2, 1, 3).reshape(b, s, e)
        return out @ Wo

    def _L1_ffn_ref(x, w_gate, w_up, w_down):
        import jax, jax.numpy as jnp
        import numpy as np
        BLOCK = 32
        W_BITS = 4
        ACT_BITS = 16

        def act_qdq(x):
            qmax = 2.0 ** (ACT_BITS - 1) - 1.0
            scale = jnp.maximum(jnp.max(jnp.abs(x)) / qmax, 1e-12)
            return jnp.clip(jnp.round(x / scale), -qmax - 1.0, qmax) * scale

        def fixed_qdq_u16(x):
            scale = 1.0 / 65536.0
            return jnp.clip(jnp.round(x / scale), 0.0, 65535.0) * scale

        def lpbq_dequant(w):
            O, I = w.shape
            qmax = 2.0 ** (W_BITS - 1) - 1.0
            wb = w.reshape(O, I // BLOCK, BLOCK)
            s = jnp.maximum(jnp.max(jnp.abs(wb), axis=-1, keepdims=True) / qmax, 1e-12)
            wq = jnp.clip(jnp.round(wb / s), -qmax - 1.0, qmax) * s
            return wq.reshape(O, I)
        x = act_qdq(x)
        up = act_qdq(x @ lpbq_dequant(w_up).T)
        gate = act_qdq(x @ lpbq_dequant(w_gate).T)
        sig = fixed_qdq_u16(jax.nn.sigmoid(gate))
        gate = act_qdq(gate * sig)
        o = act_qdq(gate * up)
        return o @ lpbq_dequant(w_down).T
    x = x + _L0_xattn_ref(ctx_1024, _layernorm(x, axis=-1), mask_BxS2_bk1, L0_xattn_Wq, L0_xattn_Wk, L0_xattn_Wv, L0_xattn_Wo)
    x = x + _L0_attn_ref(_layernorm(x, axis=-1), L0_attn_W_qkv, L0_attn_u_qkv, L0_attn_sigma_qkv, L0_attn_W_proj, L0_attn_u_proj, L0_attn_sigma_proj)
    x = x + _L0_ffn_ref(_layernorm(x, axis=-1), L0_ffn_P_w, L0_ffn_U1, L0_ffn_U2, L0_ffn_U3, L0_ffn_W1, L0_ffn_W2, L0_ffn_b2)
    x = x + _L1_xattn_ref(_layernorm(x, axis=-1), ctx_1024, ctx_1024, L1_xattn_Wq, L1_xattn_bq, L1_xattn_Wk, L1_xattn_bk, L1_xattn_Wv, L1_xattn_bv, L1_xattn_Wo, L1_xattn_bo, L1_xattn_ln_gamma, L1_xattn_ln_beta)
    x = x + _L1_attn_ref(_layernorm(x, axis=-1), L1_attn_Wq, L1_attn_Wk, L1_attn_Wv, L1_attn_Wo)
    x = x + _L1_ffn_ref(_layernorm(x, axis=-1), L1_ffn_w_gate, L1_ffn_w_up, L1_ffn_w_down)
    return x

_drawn_inputs = setup_inputs


def setup_inputs(seed=0):
    import zlib

    import numpy as np

    out = dict(_drawn_inputs(seed))
    spreads = {'L1_xattn_bq': (0.0, 0.4),
     'L1_xattn_bk': (0.0, 0.8),
     'L1_xattn_bv': (0.0, 0.1),
     'L1_xattn_bo': (0.0, 0.1),
     'L1_xattn_ln_gamma': (1.0, 0.2),
     'L1_xattn_ln_beta': (0.0, 0.1)}
    factors = {'L0_attn_u_qkv': 8.0,
     'L0_attn_u_proj': 8.0,
     'L0_ffn_U1': 8.0,
     'L0_ffn_U2': 8.0,
     'L0_ffn_W1': 8.0,
     'L0_ffn_W2': 8.0,
     'L1_attn_Wq': 8.0,
     'L1_attn_Wk': 8.0,
     'L1_ffn_w_gate': 3.399,
     'L1_ffn_w_up': 3.029,
     'L1_ffn_w_down': 3.014}
    for name, (base, spread) in spreads.items():
        noise = np.random.default_rng([zlib.crc32(name.encode()), seed]).standard_normal(out[name].shape)
        drawn = base * np.exp(spread * noise) if base else spread * noise
        out[name] = jnp.asarray(drawn.astype(out[name].dtype))
    for name, factor in factors.items():
        out[name] = (out[name] * factor).astype(out[name].dtype)
    return out
```

```python
import concourse.bass as bass
from concourse import mybir
from contextlib import ExitStack

F32 = mybir.dt.float32
F16 = mybir.dt.float16
BF16 = mybir.dt.bfloat16
U8 = mybir.dt.uint8
ALU = mybir.AluOpType
ACT = mybir.ActivationFunctionType
AX = mybir.AxisListType

P = 128
B = 2
SQ = 256
NT = B * SQ // P
TOK = B * SQ
D = 256
KT = D // P
SK = 4096
NH = 16
CH = 512
NCH = B * SK // CH
LAST = 6


def hold(eng, sem, value, passed):
    eng.wait_ge(sem, value)
    eng.sem_inc(passed, 1)


class Chip:

    def __init__(self, nc, ctx):
        self.nc, self.ctx, self.sems = nc, ctx, []
        self.sem_scope = ctx.enter_context(ExitStack())
        self.s_all = self.psum("s_all", 2048)
        self.s_ps = [self.s_all[:, 0:1024], self.s_all[:, 1024:2048]]
        self.s_banks = [self.s_all[:, i * 512:(i + 1) * 512] for i in range(4)]
        self.a_ps = [self.psum("a0", 512), self.psum("a1", 512)]
        self.o_ps = [self.psum("o0", 512), self.psum("o1", 512)]
        self.banks = [self.a_ps[0][:, :], self.a_ps[1][:, :], self.o_ps[0][:, :], self.o_ps[1][:, :],
                      *self.s_banks]
        self.x = self.sb("x", [P, NT, D], F32)
        self.xn = self.sb("xn", [P, NT, D], F32)
        self.xnT = self.sb("xnT", [P, KT, TOK], F32)
        self.ident = self.sb("ident", [P, P], F32)
        self.ones = self.sb("ones", [P, P], F32)
        self.half = self.sb("half", [P, 8], F32)

    def psum(self, name, cols):
        return self.ctx.enter_context(self.nc.psum_tensor(name, [P, cols], F32))

    def sb(self, name, shape, dt, scope=None):
        return (scope or self.ctx).enter_context(self.nc.sbuf_tensor(name, shape, dt))

    def sem(self, name):
        self.sems.append(self.sem_scope.enter_context(self.nc.semaphore(name)))
        return self.sems[-1]

    def recycle_semaphores(self):
        sems, self.sems = self.sems, []
        with self.nc.Block() as block:
            @block.gpsimd
            def _(pool):
                for s in sems:
                    pool.sem_clear(s)
        self.sem_scope.close()


def load_constants(chip, x_dram):
    nc = chip.nc
    loaded, made = chip.sem("x_loaded"), chip.sem("const_made")
    with nc.Block() as block:
        @block.sync
        def _(sp):
            sp.dma_start(chip.x[:], x_dram.rearrange("(t p) d -> p t d", p=P)).then_inc(loaded, 16)
            sp.wait_ge(loaded, 16)

        @block.gpsimd
        def _(pool):
            pool.memset(chip.ones[:], 1.0).then_inc(made, 1)
            pool.memset(chip.half[:], -0.5).then_inc(made, 1)
            pool.memset(chip.ident[:], 0.0).then_inc(made, 1)
            pool.wait_ge(made, 3)
            pool.affine_select(out=chip.ident[:], in_=chip.ident[:], compare_op=ALU.not_equal, fill=1.0,
                               base=0, pattern=[[-1, P]], channel_multiplier=1).then_inc(made, 1)


def layer_norm(chip, tag, rows_only=False):
    nc = chip.nc
    with ExitStack() as scope:
        st = chip.sb(f"{tag}_st", [P, NT, 6], F32, scope)
        mv = chip.sb(f"{tag}_mv", [P, NT, 2], F32, scope)
        ve = chip.sb(f"{tag}_ve", [P, NT], F32, scope)
        rs = chip.sb(f"{tag}_rs", [P, NT], F32, scope)
        stats, var, rstd, xn_done, tr, tr_out = (
            chip.sem(f"{tag}_{n}") for n in ("stats", "var", "rstd", "xn", "tr", "trout"))
        with nc.Block() as block:
            @block.vector
            def _(dve):
                for t in range(NT):
                    dve.bn_stats(st[:, t, :], chip.x[:, t, :]).then_inc(stats, 1)
                dve.wait_ge(stats, NT)
                for t in range(NT):
                    dve.bn_aggr(mv[:, t, :], st[:, t, :]).then_inc(stats, 1)
                dve.wait_ge(stats, 2 * NT)
                dve.tensor_scalar(ve[:], mv[:, :, 1], 1e-5, None, ALU.add).then_inc(var, 1)
                dve.wait_ge(rstd, 1)
                for t in range(NT):
                    dve.tensor_scalar(chip.xn[:, t, :], chip.x[:, t, :], mv[:, t, 0:1], rs[:, t:t + 1],
                                      ALU.subtract, ALU.mult).then_inc(xn_done, 1)
                if not rows_only:
                    dve.wait_ge(tr, 1)
                    dve.tensor_copy(chip.xnT[:, 0, :], chip.a_ps[0][:]).then_inc(var, 1)

            @block.gpsimd
            def _(pool):
                pool.wait_ge(var, 1)
                pool.tensor_tensor(rs[:], ve[:], chip.half[:, 0:NT], ALU.pow).then_inc(rstd, 1)

            @block.tensor
            def _(pe):
                if not rows_only:
                    pe.wait_ge(xn_done, NT)
                    for k in range(KT):
                        for t in range(NT):
                            last = pe.transpose(chip.a_ps[k][:, t * P:(t + 1) * P],
                                                chip.xn[:, t, k * P:(k + 1) * P], chip.ident[:])
                        last.then_inc(tr, 1)

            @block.scalar
            def _(act):
                if not rows_only:
                    act.wait_ge(tr, 2)
                    act.activation(chip.xnT[:, 1, :], chip.a_ps[1][:], ACT.Copy).then_inc(tr_out, 1)


def project_context(chip, ctxT, weights, bias_k, scratch):
    nc = chip.nc
    hds = [16, 64]
    dims = [NH * hd for hd in hds]
    SUB = CH // P
    MT = [d // P for d in dims]
    VW = [min(512, d) for d in dims]
    tiles = []
    for l in range(2):
        tiles += [(l, "k", m, 0) for m in range(MT[l])]
        tiles += [(l, "v", m, s) for s in range(SUB) for m in range(dims[l] // VW[l])]
    NTILE = len(tiles)
    NB = 4
    assert 2 * NTILE % NB == 0
    OUTS = 6
    PAIRS = NCH // 2
    with ExitStack() as scope:
        wf = [chip.sb(f"wf{i}", [P, KT, dims[i // 2]], F32, scope) for i in range(4)]
        wh = [chip.sb(f"wh{i}", [P, KT, dims[i // 2]], F16, scope) for i in range(4)]
        wl = [chip.sb(f"wl{i}", [P, KT, dims[i // 2]], F16, scope) for i in range(4)]
        bk = chip.sb("bk", [P, MT[1]], F32, scope)
        cf = [chip.sb(f"cf{j}", [P, KT, CH], F32, scope) for j in range(2)]
        chi = [chip.sb(f"chi{j}", [P, KT, CH], F16, scope) for j in range(2)]
        clo = [chip.sb(f"clo{j}", [P, KT, CH], F16, scope) for j in range(2)]
        kst = [[[chip.sb(f"kst{l}{h}{j}", [P, MT[l], CH], F16, scope) for j in range(2)]
                for h in range(2)] for l in range(2)]
        vst = [[chip.sb(f"vst{l}{j}", [P, NH, SUB, 1 + 2 * hds[l]], F16, scope) for j in range(2)]
               for l in range(2)]
        w_loaded, w_hi, w_lo = (chip.sem(n) for n in ("w_loaded", "w_hi", "w_lo"))
        c_loaded = [chip.sem(f"c_loaded{j}") for j in range(2)]
        c_hi, c_lo, passed = chip.sem("c_hi"), chip.sem("c_lo"), chip.sem("c_passed")
        tile_ready, hi_done, lo_done = chip.sem("tile_ready"), chip.sem("hi_done"), chip.sem("lo_done")
        stage_free = [chip.sem(f"stage_free{j}") for j in range(2)]

        def tile_no(it, j, n):
            return it * (2 * NTILE) + (j * NTILE + n)

        def halves(j, n):
            l, kind, m, s = tiles[n]
            bank = chip.banks[(j * NTILE + n) % NB]
            if kind == "k":
                return bank, kst[l][0][j][:, m, :], kst[l][1][j][:, m, :]
            hd, nh = hds[l], VW[l] // hds[l]
            out = vst[l][j][:, m * nh:(m + 1) * nh, s, :]
            return (bank[:, 0:VW[l]].rearrange("p (h e) -> p h e", e=hd),
                    out[:, :, 1:1 + hd], out[:, :, 1 + hd:1 + 2 * hd])

        with nc.Block() as block:
            @block.sync
            def _(sp):
                for i in range(4):
                    sp.dma_start(wf[i][:], weights[i // 2][i % 2].rearrange("(k p) n -> p k n", p=P)).then_inc(w_loaded, 16)
                sp.dma_start(bk[:], bias_k).then_inc(w_loaded, 16)
                ctx_v = ctxT.rearrange("(k p) t -> p k t", p=P)
                for j in range(2):
                    sp.dma_start(cf[j][:], ctx_v[:, :, j * CH:(j + 1) * CH]).then_inc(c_loaded[j], 16)

                def step(it, j, last):
                    if not last:
                        hold(sp, c_lo, it * 2 + (j + 1), passed)
                        sp.dma_start(cf[j][:], ctx_v[:, :, bass.ds(it * (2 * CH) + (2 + j) * CH, CH)]).then_inc(c_loaded[j], 16)
                    hold(sp, lo_done, tile_no(it, j, NTILE) + NB, passed)
                    for l in range(2):
                        kd = scratch[l][0].rearrange("h (m p) t -> h p m t", p=P)
                        for h in range(2):
                            sp.dma_start(kd[h, :, :, bass.ds(it * (2 * CH) + j * CH, CH)], kst[l][h][j][:]).then_inc(stage_free[j], 16)
                        vd = scratch[l][1].rearrange("h p c e -> p h c e")
                        sp.dma_start(vd[:, :, bass.ds(it * (2 * SUB) + j * SUB, SUB), :], vst[l][j][:]).then_inc(stage_free[j], 16)

                with sp.Fori(0, PAIRS - 1) as it:
                    for j in range(2):
                        step(it, j, False)
                for j in range(2):
                    step(PAIRS - 1, j, True)
                for j in range(2):
                    sp.wait_ge(stage_free[j], PAIRS * OUTS * 16 + 16)

            @block.gpsimd
            def _(pool):
                for l in range(2):
                    for j in range(2):
                        pool.memset(vst[l][j][:, :, :, 0:1], 1.0).then_inc(stage_free[j], 8)

            @block.tensor
            def _(pe):
                pe.wait_ge(w_lo, 4)
                with pe.Fori(0, PAIRS) as it:
                    for j in range(2):
                        pe.wait_ge(c_lo, it * 2 + (j + 1))
                        for n, (l, kind, m, s) in enumerate(tiles):
                            pe.wait_ge(lo_done, tile_no(it, j, n + 1))
                            bank = chip.banks[(j * NTILE + n) % NB]
                            q = 0
                            for k in range(KT):
                                if kind == "k":
                                    ws = slice(m * P, (m + 1) * P)
                                    out, wi = bank, 2 * l
                                    products = [(wh[wi][:, k, ws], chi[j][:, k, :]), (wh[wi][:, k, ws], clo[j][:, k, :]),
                                                (wl[wi][:, k, ws], chi[j][:, k, :])]
                                else:
                                    cs, ws = slice(s * P, (s + 1) * P), slice(m * VW[l], (m + 1) * VW[l])
                                    out, wi = bank[:, 0:VW[l]], 2 * l + 1
                                    products = [(chi[j][:, k, cs], wh[wi][:, k, ws]), (chi[j][:, k, cs], wl[wi][:, k, ws]),
                                                (clo[j][:, k, cs], wh[wi][:, k, ws])]
                                for a, b in products:
                                    last = pe.matmul(out, a, b, start=(q == 0), stop=(q == 3 * KT - 1))
                                    q += 1
                            last.then_inc(tile_ready, 1)

            @block.scalar
            def _(act):
                act.wait_ge(w_loaded, 80)
                for i in range(4):
                    act.activation(wh[i][:], wf[i][:], ACT.Copy).then_inc(w_hi, 1)
                act.wait_ge(c_loaded[0], 16)
                act.activation(chi[0][:], cf[0][:], ACT.Copy).then_inc(c_hi, 1)

                def step(it, j, last):
                    act.wait_ge(stage_free[j], it * (OUTS * 16) + 16)
                    for n, (l, kind, m, s) in enumerate(tiles):
                        if n == NTILE // 2 and not last:
                            act.wait_ge(c_loaded[1 - j], it * 16 + 16 * (1 + j))
                            act.activation(chi[1 - j][:], cf[1 - j][:], ACT.Copy).then_inc(c_hi, 1)
                        act.wait_ge(tile_ready, tile_no(it, j, n + 1))
                        src, hi, _lo = halves(j, n)
                        if l == 1 and kind == "k":
                            act.activation(hi, src, ACT.Identity, bias=bk[:, m:m + 1]).then_inc(hi_done, 1)
                        else:
                            act.activation(hi, src, ACT.Copy).then_inc(hi_done, 1)

                with act.Fori(0, PAIRS - 1) as it:
                    for j in range(2):
                        step(it, j, False)
                step(PAIRS - 1, 0, False)
                step(PAIRS - 1, 1, True)

            @block.vector
            def _(dve):
                dve.memset(chip.half[:, 7:8], -0.5).then_inc(lo_done, NB)
                for i in range(4):
                    dve.wait_ge(w_hi, i + 1)
                    dve.tensor_tensor(wl[i][:], wf[i][:], wh[i][:], ALU.subtract).then_inc(w_lo, 1)
                dve.wait_ge(c_hi, 1)
                dve.tensor_tensor(clo[0][:], cf[0][:], chi[0][:], ALU.subtract).then_inc(c_lo, 1)

                def step(it, j, last):
                    for n, (l, kind, m, s) in enumerate(tiles):
                        if n == NTILE // 2 and not last:
                            dve.wait_ge(c_hi, it * 2 + (j + 2))
                            dve.tensor_tensor(clo[1 - j][:], cf[1 - j][:], chi[1 - j][:], ALU.subtract).then_inc(c_lo, 1)
                        dve.wait_ge(hi_done, tile_no(it, j, n + 1))
                        src, hi, lo = halves(j, n)
                        if l == 1 and kind == "k":
                            dve.scalar_tensor_tensor(out=lo, in0=src, scalar=bk[:, m:m + 1], in1=hi,
                                                     op0=ALU.add, op1=ALU.subtract).then_inc(lo_done, 1)
                        else:
                            dve.tensor_tensor(lo, src, hi, ALU.subtract).then_inc(lo_done, 1)

                with dve.Fori(0, PAIRS - 1) as it:
                    for j in range(2):
                        step(it, j, False)
                step(PAIRS - 1, 0, False)
                step(PAIRS - 1, 1, True)


def project_queries(chip, tag, wq, bias_q, hd, q_dram):
    nc = chip.nc
    MT = NH * hd // P
    with ExitStack() as scope:
        w = chip.sb(f"{tag}_w", [P, KT, NH * hd], F32, scope)
        bq = chip.sb(f"{tag}_bq", [P, MT], F32, scope)
        qh = chip.sb(f"{tag}_qh", [P, MT, TOK], F16, scope)
        ql = chip.sb(f"{tag}_ql", [P, MT, TOK], F16, scope)
        loaded, ready, hi, lo, out = (chip.sem(f"{tag}_{n}") for n in ("ld", "rdy", "hi", "lo", "out"))
        with nc.Block() as block:
            @block.sync
            def _(sp):
                sp.dma_start(w[:], wq.rearrange("(k p) n -> p k n", p=P)).then_inc(loaded, 16)
                if bias_q is not None:
                    sp.dma_start(bq[:], bias_q).then_inc(loaded, 16)
                qd = q_dram.rearrange("h (m p) t -> h p m t", p=P)
                sp.wait_ge(hi, MT)
                sp.dma_start(qd[0], qh[:]).then_inc(out, 16)
                sp.wait_ge(lo, MT)
                sp.dma_start(qd[1], ql[:]).then_inc(out, 16)
                sp.wait_ge(out, 32)

            @block.tensor
            def _(pe):
                pe.wait_ge(loaded, 16 if bias_q is None else 32)
                for m in range(MT):
                    if m >= 4:
                        pe.wait_ge(lo, m - 3)
                    for k in range(KT):
                        last = pe.matmul(chip.banks[m % 4], w[:, k, m * P:(m + 1) * P], chip.xnT[:, k, :],
                                         start=(k == 0), stop=(k == KT - 1))
                    last.then_inc(ready, 1)

            @block.scalar
            def _(act):
                for m in range(MT):
                    act.wait_ge(ready, m + 1)
                    if bias_q is None:
                        act.activation(qh[:, m, :], chip.banks[m % 4], ACT.Copy).then_inc(hi, 1)
                    else:
                        if m == 0:
                            act.wait_ge(loaded, 32)
                        act.activation(qh[:, m, :], chip.banks[m % 4], ACT.Identity, bias=bq[:, m:m + 1]).then_inc(hi, 1)

            @block.vector
            def _(dve):
                for m in range(MT):
                    dve.wait_ge(hi, m + 1)
                    if bias_q is None:
                        dve.tensor_tensor(ql[:, m, :], chip.banks[m % 4], qh[:, m, :], ALU.subtract).then_inc(lo, 1)
                    else:
                        dve.scalar_tensor_tensor(out=ql[:, m, :], in0=chip.banks[m % 4], scalar=bq[:, m:m + 1],
                                                 in1=qh[:, m, :], op0=ALU.add, op1=ALU.subtract).then_inc(lo, 1)


def cross_attention(chip, tag, hd, q_dram, k_dram, v_dram, att, mask_rows=None, key_rows=None, q_rows=None):
    nc = chip.nc
    small = hd == 16
    GR = 8
    GK = SK // P // GR
    NA = 2 * SK // 512
    AI = NA + 1
    VC = 1 + 2 * hd
    NP = 4
    W = 4
    PAIRS = NH // 2
    KR = 64 if small else 66
    MC = 49 if small else 64
    POOL_GROUPS = (1, 2, 4, 5, 7) if small else (1, 3, 5, 7)
    with ExitStack() as scope:
        if small:
            kbuf = [chip.sb(f"{tag}_k{w}", [P, SK], F16, scope) for w in range(W)]
            qa = [chip.sb(f"{tag}_qa{w}", [P, SQ], F16, scope) for w in range(W)]
            qb = [chip.sb(f"{tag}_qb{w}", [P, SQ], F16, scope) for w in range(W)]
        else:
            k1 = [chip.sb(f"{tag}_k1{w}", [P, SK], F16, scope) for w in range(W)]
            k2 = [chip.sb(f"{tag}_k2{w}", [KR, SK], F16, scope) for w in range(W)]
            q1 = [chip.sb(f"{tag}_q1{w}", [P, SQ], F16, scope) for w in range(W)]
            qa = [chip.sb(f"{tag}_qa{w}", [KR, SQ], F16, scope) for w in range(W)]
            qb = [chip.sb(f"{tag}_qb{w}", [KR, SQ], F16, scope) for w in range(W)]
        v = [chip.sb(f"{tag}_v{w}", [P, SK // P, VC], F16, scope) for w in range(W)]
        prob = [chip.sb(f"{tag}_p{i}", [P, GK, SQ], F32, scope) for i in range(NP)]
        rest = [chip.sb(f"{tag}_r{i}", [P, GK, SQ], F16, scope) for i in range(NP)]
        mx = [chip.sb(f"{tag}_mx{i}", [P, 2, NA // 2], F32, scope) for i in range(2)]
        nm = [chip.sb(f"{tag}_nm{i}", [P, 2], F32, scope) for i in range(2)]
        nmh = [chip.sb(f"{tag}_nmh{i}", [P, 2], F16, scope) for i in range(2)]
        mcol = [chip.sb(f"{tag}_mcol{i}", [P, 2, P], F32, scope) for i in range(2)]
        rd = [chip.sb(f"{tag}_rd{i}", [P, 2], F32, scope) for i in range(2)]
        ov = [chip.sb(f"{tag}_ov{i}", [P, 2, hd], F32, scope) for i in range(2)]
        if small:
            m8 = chip.sb(f"{tag}_m8", [B, SK], U8, scope)
            m16 = chip.sb(f"{tag}_m16", [B, SK], F16, scope)
        preset, rows_in, mask_in, mask_made = (chip.sem(f"{tag}_{n}") for n in ("preset", "rows", "maskin", "mask"))
        loaded = [chip.sem(f"{tag}_ld{w}") for w in range(W)]
        s_ready, p_ready = chip.sem(f"{tag}_s"), chip.sem(f"{tag}_p")
        a_ready, a_done = chip.sem(f"{tag}_a"), chip.sem(f"{tag}_ad")
        rest_dve, rest_pool = chip.sem(f"{tag}_rv"), chip.sem(f"{tag}_rp")
        pv_done, o_step, m_step = chip.sem(f"{tag}_pv"), chip.sem(f"{tag}_o"), chip.sem(f"{tag}_m")
        NLOAD = 7
        PRESETS = 3 * W if small else 2 * W
        cleared, passed = chip.sem(f"{tag}_cleared"), chip.sem(f"{tag}_passed")
        SP_, PP_, AP_, OP_ = 2, NP, 2, 8
        NPOOL = len(POOL_GROUPS)

        def k_pass2(w, c):
            ks = slice(c * P, (c + 1) * P)
            if small:
                return [(kbuf[w][:, ks], qb[w][:, :])]
            return [(k1[w][:, ks], q1[w][:, :]), (k2[w][:, ks], qb[w][:, :])]

        def k_pass1(w, qt, c):
            qs, ks = slice(qt * P, (qt + 1) * P), slice(c * 512, (c + 1) * 512)
            if small:
                return qa[w][:, qs], kbuf[w][:, ks]
            return q1[w][:, qs], k1[w][:, ks]

        def group_no(it, w, g):
            return it * (W * GR) + (w * GR + g)

        def a_no(it, w, n):
            return it * (W * AI) + (w * AI + n)

        def ahead(it, w, n):
            w += n
            if w >= W:
                w, it = w - W, it + 1
                if isinstance(it, int) and it >= PAIRS:
                    return None
            return it, w

        def a_work(it, w, g):
            if g < 4:
                u = ahead(it, w, 1)
                return [(u, NA // 2 + 2 * g + i) for i in range(2)] if u else []
            u = ahead(it, w, 2)
            uses = [(u, 2 * (g - 4) + i) for i in range(2)] if u else []
            n = ahead(it, w, 1)
            return [(n, "t")] + uses if g == 5 and n else uses

        order = {}
        seq = ([(0, n) for n in range(NA)] + [(1, 0), (1, 1), (0, "t")] + [(1, n) for n in range(2, NA // 2)])
        for u in range(3 * W):
            for g in range(GR):
                for (uu, n) in a_work(0, 0, g):
                    seq.append((u + uu[1], n))
        for i, key in enumerate(seq):
            order[key] = i
        assert order[(1 + W, 0)] - order[(1, 0)] == W * AI and W * AI % 2 == 0

        def a_base(it, w, n):
            if isinstance(it, int) and it == 0 and (w, n) in ((0, 0), (0, 1)):
                return n
            if isinstance(it, int) and it == PAIRS - 1 and (w, n) == (W - 1, "t"):
                return order[(w + W, n)] - W * AI - 2
            return order[(w + W, n)] - W * AI

        def a_use(it, w, n):
            return it * (W * AI) + a_base(it, w, n)

        def a_bank(it, w, n):
            return chip.a_ps[a_base(it, w, n) % 2]

        LEAD = ([((0, 0), n) for n in range(NA)] + [((0, 1), 0), ((0, 1), 1), ((0, 0), "t")]
                + [((0, 1), n) for n in range(2, NA // 2)])

        def all_units(eng, body, first):
            first()
            body(0, 0)
            with eng.Fori(0, PAIRS - 1) as it:
                for w in range(1, W):
                    body(it, w)
                body(it + 1, 0)
            for w in range(1, W):
                body(PAIRS - 1, w)

        with nc.Block() as block:
            @block.sync
            def _(sp):
                if small:
                    sp.dma_start(m8[:], mask_rows).then_inc(mask_in, 16)
                    sp.wait_ge(preset, PRESETS)
                    for w in range(W):
                        sp.dma_start(qa[w][48:64, :], q_rows).then_inc(rows_in, 16)
                        sp.dma_start(kbuf[w][49:51, :], key_rows).then_inc(rows_in, 16)
                    sp.wait_ge(mask_made, 1)
                    for w in range(W):
                        sp.dma_start(kbuf[w][48:49, :], m16[w // 2:w // 2 + 1, :]).then_inc(rows_in, 16)

                def load(it, w):
                    b, j = w // 2, w % 2
                    keys, toks = slice(b * SK, (b + 1) * SK), slice(b * SQ, (b + 1) * SQ)
                    head = bass.ds(it * (2 * hd) + j * hd, hd)
                    if small:
                        for at, half in ((0, 0), (16, 1), (32, 0)):
                            sp.dma_start(kbuf[w][at:at + 16, :], k_dram[half, head, keys]).then_inc(loaded[w], 16)
                        for at, half in ((0, 0), (16, 0), (32, 1)):
                            sp.dma_start(qa[w][at:at + 16, :], q_dram[half, head, toks]).then_inc(loaded[w], 16)
                        n = 6
                    else:
                        sp.dma_start(k1[w][0:64, :], k_dram[0, head, keys]).then_inc(loaded[w], 16)
                        sp.dma_start(k1[w][64:128, :], k_dram[1, head, keys]).then_inc(loaded[w], 16)
                        sp.dma_start(k2[w][0:64, :], k_dram[0, head, keys]).then_inc(loaded[w], 16)
                        sp.dma_start(q1[w][0:64, :], q_dram[0, head, toks]).then_inc(loaded[w], 16)
                        sp.dma_start(q1[w][64:128, :], q_dram[0, head, toks]).then_inc(loaded[w], 16)
                        sp.dma_start(qa[w][0:64, :], q_dram[1, head, toks]).then_inc(loaded[w], 16)
                        n = 6
                    vd = v_dram[bass.ds(it * 2 + j, 1), :, b * (SK // P):(b + 1) * (SK // P), :]
                    sp.dma_start(v[w][:], vd.rearrange("h p c e -> p (h c) e")).then_inc(loaded[w], 16)
                    return n + 1

                for w in range(W):
                    assert load(0, w) == NLOAD
                with sp.Fori(0, PAIRS - 1) as it:
                    for w in range(W):
                        hold(sp, pv_done, group_no(it, w, GR) + PP_, passed)
                        load(it + 1, w)
                sp.wait_ge(pv_done, group_no(PAIRS - 1, W - 1, GR) + PP_)
                sp.wait_ge(rows_in, 192) if small else None

            @block.tensor
            def _(pe):
                def scores(it, w, g):
                    if g == 0:
                        pe.wait_ge(a_done, a_use(it, w, "t") + 1 + AP_)
                    pe.wait_ge(p_ready, group_no(it, w, g) + 1)
                    out = chip.s_ps[g % 2]
                    for c in range(GK):
                        products = k_pass2(w, g * GK + c)
                        for i, (a, b) in enumerate(products):
                            last = pe.matmul(out[:, c * SQ:(c + 1) * SQ], a, b, start=(i == 0), stop=(i == len(products) - 1))
                    last.then_inc(s_ready, 1)

                def maxima(u, n):
                    it, w = u
                    pe.wait_ge(a_done, a_use(it, w, n) + 1)
                    if n == "t":
                        pe.wait_ge(m_step, it * (W * 4) + (w * 4 + 4))
                        for qt in range(2):
                            last = pe.transpose(a_bank(it, w, n)[:, qt * P:(qt + 1) * P], mcol[w % 2][:, qt, :], chip.ident[:])
                    else:
                        if n == 0:
                            pe.wait_ge(loaded[w], it * (16 * NLOAD) + 16 * NLOAD)
                        a, b = k_pass1(w, n // (NA // 2), n % (NA // 2))
                        last = pe.matmul(a_bank(it, w, n)[:], a, b, start=True, stop=True)
                    last.then_inc(a_ready, 1)

                def values(it, w, g):
                    if g == 0:
                        pe.wait_ge(o_step, it * (W * 4) + (w * 4 + 3))
                    pe.wait_ge(p_ready, group_no(it, w, g) + 1 + SP_)
                    if g in POOL_GROUPS:
                        pe.wait_ge(rest_pool, it * (W * NPOOL) + (w * NPOOL + POOL_GROUPS.index(g) + 1))
                    else:
                        done = [x for x in range(GR) if x not in POOL_GROUPS]
                        pe.wait_ge(rest_dve, it * (W * len(done)) + (w * len(done) + done.index(g) + 1))
                    o = chip.o_ps[w % 2]
                    for c in range(GK):
                        for qt in range(2):
                            qs = slice(qt * P, (qt + 1) * P)
                            hi = prob[g % NP][:, c, qs].bitcast(BF16).rearrange("p (q t) -> p q t", t=2)[:, :, 1]
                            first, end = g == 0 and c == 0, g == GR - 1 and c == GK - 1
                            pe.matmul(o[:, qt * VC:(qt + 1) * VC], hi, v[w][:, g * GK + c, :],
                                      start=first and qt == 0, stop=False, skip_group_check=True)
                            last = pe.matmul(o[:, qt * VC:qt * VC + 1 + hd], rest[g % NP][:, c, qs],
                                             v[w][:, g * GK + c, 0:1 + hd], start=False, stop=end, skip_group_check=True)
                    last.then_inc(pv_done, 1)

                def first():
                    if small:
                        pe.wait_ge(rows_in, 192)
                    pe.wait_ge(preset, PRESETS)
                    for a in LEAD:
                        maxima(*a)
                    for g in range(2):
                        scores(0, 0, g)

                def unit(it, w):
                    for g in range(GR):
                        u = (it, w) if g + 2 < GR else ahead(it, w, 1)
                        if u:
                            scores(u[0], u[1], (g + 2) % GR)
                        for a in a_work(it, w, g):
                            maxima(*a)
                        values(it, w, g)

                all_units(pe, unit, first)

            @block.scalar
            def _(act):
                act.wait_ge(preset, PRESETS)

                def unit(it, w):
                    for g in range(GR):
                        act.wait_ge(s_ready, group_no(it, w, g) + 1)
                        act.wait_ge(pv_done, group_no(it, w, g) + 1)
                        act.activation(prob[g % NP][:], chip.s_ps[g % 2][:].rearrange("p (c q) -> p c q", q=SQ),
                                       ACT.Exp, scale=hd ** -0.5).then_inc(p_ready, 1)

                all_units(act, unit, lambda: None)

            def remainder(eng, sem, it, w, g):
                eng.wait_ge(p_ready, group_no(it, w, g) + 1 + SP_)
                hi = prob[g % NP][:].bitcast(BF16).rearrange("p c (q t) -> p c q t", t=2)[:, :, :, 1]
                eng.tensor_tensor(rest[g % NP][:], prob[g % NP][:], hi, ALU.subtract).then_inc(sem, 1)

            @block.gpsimd
            def _(pool):
                for i in range(2):
                    pool.memset(mcol[i][:], 0.0).then_inc(cleared, 1)

                def unit(it, w):
                    for g in POOL_GROUPS:
                        remainder(pool, rest_pool, it, w, g)

                all_units(pool, unit, lambda: None)

            @block.vector
            def _(dve):
                def maxima(u, n):
                    it, w = u
                    dve.wait_ge(a_ready, a_use(it, w, n) + 1)
                    if n == "t":
                        dve.tensor_tensor(qb[w][0:KR, :], a_bank(it, w, n)[0:KR, 0:SQ], qa[w][0:KR, :], ALU.add).then_inc(a_done, 1)
                        return
                    dve.tensor_reduce(mx[w % 2][:, n // (NA // 2), n % (NA // 2):n % (NA // 2) + 1], a_bank(it, w, n)[:],
                                      AX.X, ALU.max).then_inc(a_done, 1)
                    if n == NA - 1:
                        steps = it * (W * 4) + w * 4
                        i = w % 2
                        dve.wait_ge(a_done, a_use(it, w, n) + 1 + AP_)
                        dve.tensor_reduce(nm[i][:], mx[i][:], AX.X, ALU.max, negate=True).then_inc(m_step, 1)
                        dve.wait_ge(m_step, steps + 1)
                        dve.tensor_copy(nmh[i][:], nm[i][:]).then_inc(m_step, 1)
                        dve.wait_ge(m_step, steps + 2)
                        dve.tensor_copy(mcol[i][:, :, MC], nmh[i][:]).then_inc(m_step, 1)
                        dve.tensor_tensor(mcol[i][:, :, MC + 1], nm[i][:], nmh[i][:], ALU.subtract).then_inc(m_step, 1)

                def output(it, w):
                    i, steps = w % 2, it * (W * 4) + w * 4 + OP_
                    o = chip.o_ps[i][:, 0:2 * VC].rearrange("p (t e) -> p t e", e=VC)
                    dve.wait_ge(pv_done, group_no(it, w, GR) + PP_)
                    dve.reciprocal(rd[i][:], o[:, :, 0]).then_inc(o_step, 1)
                    dve.tensor_copy(ov[i][:], o[:, :, 1 + hd:VC]).then_inc(o_step, 1)
                    dve.wait_ge(o_step, steps + 2)
                    dve.tensor_tensor(ov[i][:], o[:, :, 1:1 + hd], ov[i][:], ALU.add).then_inc(o_step, 1)
                    dve.wait_ge(o_step, steps + 3)
                    b, j = w // 2, w % 2
                    out = att[:, 2 * b:2 * b + 2, bass.ds(it * (2 * hd) + j * hd, hd)]
                    dve.tensor_tensor(out, ov[i][:], rd[i][:].unsqueeze(2).to_broadcast([P, 2, hd]), ALU.mult).then_inc(o_step, 1)

                def first():
                    if small:
                        for w in range(W):
                            for t in (kbuf[w], qa[w], qb[w]):
                                dve.memset(t[:], 0.0).then_inc(preset, 1)
                    if small:
                        dve.wait_ge(mask_in, 16)
                        dve.tensor_scalar(m16[:], m8[:], 60000.0, -60000.0, ALU.mult, ALU.add).then_inc(mask_made, 1)
                    else:
                        for w in range(W):
                            dve.memset(k2[w][64:66, :], 1.0).then_inc(preset, 1)
                            dve.memset(qa[w][64:66, :], 0.0).then_inc(preset, 1)
                    dve.memset(nmh[0][:], 0.0).then_inc(p_ready, SP_)
                    dve.memset(nm[0][:], 0.0).then_inc(pv_done, PP_)
                    dve.memset(nm[1][:], 0.0).then_inc(a_done, AP_)
                    dve.memset(nmh[1][:], 0.0).then_inc(o_step, OP_)
                    dve.wait_ge(preset, PRESETS)
                    dve.wait_ge(o_step, OP_)
                    dve.wait_ge(a_done, AP_)
                    dve.wait_ge(cleared, 2)
                    for a in LEAD:
                        maxima(*a)
                    remainder(dve, rest_dve, 0, 0, 0)

                def unit(it, w):
                    for g in range(GR):
                        u = (it, w) if g + 1 < GR else ahead(it, w, 1)
                        if u and (g + 1) % GR not in POOL_GROUPS:
                            remainder(dve, rest_dve, u[0], u[1], (g + 1) % GR)
                        for a in a_work(it, w, g):
                            maxima(*a)
                        if g == 1 and not (isinstance(it, int) and it == 0 and w == 0):
                            output(it - (w == 0), (w - 1) % W)

                all_units(dve, unit, first)
                output(PAIRS - 1, W - 1)


def rows_project(chip, tag, src, dims, w_dram, finish, bias_in=None):
    nc = chip.nc
    K = dims // P
    with ExitStack() as scope:
        w = chip.sb(f"{tag}_w", [P, K, D], F32, scope)
        srcT = chip.sb(f"{tag}_srcT", [P, K, TOK], F32, scope)
        bi = chip.sb(f"{tag}_bi", [P, K], F32, scope)
        loaded, tr, tr_out, ready, done = (chip.sem(f"{tag}_{n}") for n in ("ld", "tr", "trout", "rdy", "done"))
        NLD = 16 if bias_in is None else 32
        tbank = chip.s_banks
        with nc.Block() as block:
            @block.sync
            def _(sp):
                sp.dma_start(w[:], w_dram.rearrange("(k p) n -> p k n", p=P)).then_inc(loaded, 16)
                if bias_in is not None:
                    sp.dma_start(bi[:], bias_in).then_inc(loaded, 16)
                sp.wait_ge(loaded, NLD)

            @block.tensor
            def _(pe):
                for k in range(K):
                    if k >= 2:
                        pe.wait_ge(tr_out, k - 1)
                    for t in range(NT):
                        last = pe.transpose(tbank[k % 2][:, t * P:(t + 1) * P], src[:, t, k * P:(k + 1) * P], chip.ident[:])
                    last.then_inc(tr, 1)
                pe.wait_ge(loaded, NLD)
                pe.wait_ge(tr_out, K)
                for t in range(NT):
                    for k in range(K):
                        last = pe.matmul(chip.banks[t][:, 0:D], srcT[:, k, t * P:(t + 1) * P], w[:, k, :],
                                         start=(k == 0), stop=(k == K - 1))
                    last.then_inc(ready, 1)

            @block.scalar
            def _(act):
                for k in range(K):
                    act.wait_ge(tr, k + 1)
                    if bias_in is None:
                        act.activation(srcT[:, k, :], tbank[k % 2][:], ACT.Copy).then_inc(tr_out, 1)
                    else:
                        if k == 0:
                            act.wait_ge(loaded, NLD)
                        act.activation(srcT[:, k, :], tbank[k % 2][:], ACT.Identity, bias=bi[:, k:k + 1]).then_inc(tr_out, 1)

            @block.vector
            def _(dve):
                for t in range(NT):
                    dve.wait_ge(ready, t + 1)
                    finish(dve, t, done)
                dve.wait_ge(done, NT)


def add_to_x(chip):
    def finish(dve, t, done):
        dve.tensor_tensor(chip.x[:, t, :], chip.banks[t][:, 0:D], chip.x[:, t, :], ALU.add).then_inc(done, 1)
    return finish


def normed_output(chip, tag, acc, bo, gamma, beta):
    nc = chip.nc
    with ExitStack() as scope:
        rows = [chip.sb(f"{tag}_row{i}", [P, D], F32, scope) for i in range(3)]
        st = chip.sb(f"{tag}_st", [P, NT, 6], F32, scope)
        mv = chip.sb(f"{tag}_mv", [P, NT, 2], F32, scope)
        ve = chip.sb(f"{tag}_ve", [P, NT], F32, scope)
        rs = chip.sb(f"{tag}_rs", [P, NT], F32, scope)
        loaded, step, var, rstd = (chip.sem(f"{tag}_{n}") for n in ("ld", "step", "var", "rstd"))
        with nc.Block() as block:
            @block.sync
            def _(sp):
                for r, d in zip(rows, (bo, gamma, beta)):
                    sp.dma_start(r[:], d.partition_broadcast(P)).then_inc(loaded, 16)
                sp.wait_ge(loaded, 48)

            @block.gpsimd
            def _(pool):
                pool.wait_ge(var, 1)
                pool.tensor_tensor(rs[:], ve[:], chip.half[:, 0:NT], ALU.pow).then_inc(rstd, 1)

            @block.vector
            def _(dve):
                n = 0

                def wide(row):
                    return row[:].unsqueeze(1).to_broadcast([P, NT, D])

                dve.wait_ge(loaded, 48)
                dve.tensor_tensor(acc[:], acc[:], wide(rows[0]), ALU.add).then_inc(step, 1)
                dve.wait_ge(step, 1)
                dve.tensor_tensor(acc[:], acc[:], chip.xn[:], ALU.add).then_inc(step, 1)
                dve.wait_ge(step, 2)
                for t in range(NT):
                    dve.bn_stats(st[:, t, :], acc[:, t, :]).then_inc(step, 1)
                dve.wait_ge(step, 2 + NT)
                for t in range(NT):
                    dve.bn_aggr(mv[:, t, :], st[:, t, :]).then_inc(step, 1)
                dve.wait_ge(step, 2 + 2 * NT)
                dve.tensor_scalar(ve[:], mv[:, :, 1], 1e-5, None, ALU.add).then_inc(var, 1)
                dve.wait_ge(rstd, 1)
                for t in range(NT):
                    dve.tensor_scalar(acc[:, t, :], acc[:, t, :], mv[:, t, 0:1], rs[:, t:t + 1],
                                      ALU.subtract, ALU.mult).then_inc(step, 1)
                dve.wait_ge(step, 2 + 3 * NT)
                dve.tensor_tensor(acc[:], acc[:], wide(rows[1]), ALU.mult).then_inc(step, 1)
                dve.wait_ge(step, 3 + 3 * NT)
                dve.tensor_tensor(acc[:], acc[:], wide(rows[2]), ALU.add).then_inc(step, 1)
                dve.wait_ge(step, 4 + 3 * NT)
                dve.tensor_tensor(chip.x[:], chip.x[:], acc[:], ALU.add).then_inc(step, 1)
                dve.wait_ge(step, 5 + 3 * NT)


def spectral_scale(chip, tag, w_dram, n, u_bc, sp_bc, out):
    nc = chip.nc
    H = n // 2 if n > 512 else n
    NH2 = n // H
    with ExitStack() as scope:
        w = chip.sb(f"{tag}_w", [P, KT, n], F32, scope)
        u = chip.sb(f"{tag}_u", [P, n], F32, scope)
        prm = chip.sb(f"{tag}_prm", [P, 1], F32, scope)
        wu = chip.sb(f"{tag}_wu", [P, KT, n], F32, scope)
        a = chip.sb(f"{tag}_a", [P, KT], F32, scope)
        a2 = chip.sb(f"{tag}_a2", [P, KT], F32, scope)
        abc = chip.sb(f"{tag}_abc", [P, KT, P], F32, scope)
        b2 = chip.sb(f"{tag}_b2", [P, NH2, H], F32, scope)
        q = chip.sb(f"{tag}_q", [P, 6], F32, scope)
        loaded, step, summed, prod, rooted, sq = (chip.sem(f"{tag}_{x}") for x in ("ld", "step", "sum", "prod", "root", "sq"))
        with nc.Block() as block:
            @block.sync
            def _(sp):
                sp.dma_start(w[:], w_dram.rearrange("(k p) n -> p k n", p=P)).then_inc(loaded, 16)
                sp.dma_start(u[:], u_bc.partition_broadcast(P)).then_inc(loaded, 16)
                sp.dma_start(prm[:], sp_bc.partition_broadcast(P)).then_inc(loaded, 16)
                sp.wait_ge(loaded, 48)

            @block.vector
            def _(dve):
                dve.wait_ge(loaded, 48)
                dve.tensor_tensor(wu[:], w[:], u[:].unsqueeze(1).to_broadcast([P, KT, n]), ALU.mult).then_inc(step, 1)
                dve.wait_ge(step, 1)
                dve.tensor_reduce(a[:], wu[:], AX.X, ALU.add).then_inc(step, 1)
                dve.wait_ge(step, 2)
                dve.tensor_tensor(a2[:], a[:], a[:], ALU.mult).then_inc(step, 1)
                dve.tensor_copy(abc[:], a[:].unsqueeze(2).to_broadcast([P, KT, P])).then_inc(step, 1)
                dve.wait_ge(summed, 1)
                dve.tensor_reduce(q[:, 0:1], chip.banks[0][:, 0:KT], AX.X, ALU.add).then_inc(step, 1)
                dve.wait_ge(sq, 1)
                dve.tensor_reduce(q[:, 1:2], b2[:], AX.XY, ALU.add).then_inc(step, 1)
                dve.wait_ge(step, 6)
                dve.reciprocal(q[:, 2:3], q[:, 1:2]).then_inc(step, 1)
                dve.wait_ge(step, 7)
                dve.tensor_tensor(q[:, 3:4], q[:, 0:1], q[:, 2:3], ALU.mult).then_inc(step, 1)
                dve.memset(q[:, 5:6], 0.5).then_inc(step, 1)
                dve.wait_ge(rooted, 1)
                dve.tensor_tensor(out, q[:, 4:5], prm[:], ALU.mult).then_inc(step, 1)
                dve.wait_ge(step, 10)

            @block.gpsimd
            def _(pool):
                pool.wait_ge(step, 9)
                pool.tensor_tensor(q[:, 4:5], q[:, 3:4], q[:, 5:6], ALU.pow).then_inc(rooted, 1)

            @block.tensor
            def _(pe):
                pe.wait_ge(step, 4)
                pe.matmul(chip.banks[0][:, 0:KT], chip.ones[:], a2[:], start=True, stop=True).then_inc(summed, 1)
                for h in range(NH2):
                    for k in range(KT):
                        last = pe.matmul(chip.banks[1 + h][:, 0:H], abc[:, k, :], w[:, k, h * H:(h + 1) * H],
                                         start=(k == 0), stop=(k == KT - 1))
                last.then_inc(prod, 1)

            @block.scalar
            def _(act):
                act.wait_ge(prod, 1)
                for h in range(NH2):
                    last = act.activation(b2[:, h, :], chip.banks[1 + h][:, 0:H], ACT.Square)
                last.then_inc(sq, 1)


def self_attention(chip, tag, wq, wk, wv, att, scale=None, mask=None, centre=None):
    nc = chip.nc
    NG = NH // 4
    with ExitStack() as scope:
        w = [chip.sb(f"{tag}_w{i}", [P, KT, 512 if i < 2 else D], F32, scope) for i in range(3)]
        qk = [chip.sb(f"{tag}_qk{i}", [P, NG, TOK], F32, scope) for i in range(2)]
        v = chip.sb(f"{tag}_v", [P, NT, D], F32, scope)
        raw = [chip.sb(f"{tag}_raw{i}", [P, TOK], F32, scope) for i in range(2)]
        sqr = [chip.sb(f"{tag}_sqr{i}", [P, TOK], F32, scope) for i in range(2)]
        cm = chip.sb(f"{tag}_cm", [P, 2, P], F32, scope)
        mk = chip.sb(f"{tag}_mk", [P, 2, SQ], F32, scope)
        s4 = chip.sb(f"{tag}_s4", [P, 1], F32, scope)
        sc = [chip.sb(f"{tag}_sc{i}", [P, 4, SQ], F32, scope) for i in range(2)]
        pr = [chip.sb(f"{tag}_pr{i}", [P, 4, SQ], F32, scope) for i in range(2)]
        pT = [chip.sb(f"{tag}_pT{i}", [P, 8, P], F32, scope) for i in range(2)]
        nm = [chip.sb(f"{tag}_nm{i}", [P, 4], F32, scope) for i in range(2)]
        sm = [chip.sb(f"{tag}_sm{i}", [P, 4], F32, scope) for i in range(2)]
        rc = [chip.sb(f"{tag}_rc{i}", [P, 4], F32, scope) for i in range(2)]
        names = ("ld", "pj", "pjo", "rawo", "cen", "sqd", "s4d", "sr", "srd", "nmd", "ex", "tr", "tro", "pv", "od", "rcd")
        ld, pj, pjo, rawo, cen, sqd, s4d, sr, srd, nmd, ex, tr, tro, pv, od, rcd = (chip.sem(f"{tag}_{x}") for x in names)
        NLD = 48 + (16 if mask is not None else 0) + (16 if centre is not None else 0)
        steps = [(t, g) for t in range(NT) for g in range(NG)]
        with nc.Block() as block:
            @block.sync
            def _(sp):
                for i, src in enumerate((wq, wk, wv)):
                    sp.dma_start(w[i][:], src.rearrange("(k p) n -> p k n", p=P)).then_inc(ld, 16)
                if mask is not None:
                    sp.dma_start(mk[:], mask.rearrange("(t p) k -> p t k", p=P)).then_inc(ld, 16)
                if centre is not None:
                    sp.dma_start(cm[:], centre.rearrange("c p m -> p c m")).then_inc(ld, 16)
                sp.wait_ge(ld, NLD)

            NQK = 2 * NG

            @block.tensor
            def _(pe):
                pe.wait_ge(ld, NLD)
                for n in range(NQK + NT):
                    if n >= 2:
                        pe.wait_ge(pjo, n - 1)
                    for k in range(KT):
                        if n < NQK:
                            i, g = n // NG, n % NG
                            last = pe.matmul(chip.banks[n % 2], w[i][:, k, g * P:(g + 1) * P], chip.xnT[:, k, :],
                                             start=(k == 0), stop=(k == KT - 1))
                        else:
                            t = n - NQK
                            last = pe.matmul(chip.banks[n % 2][:, 0:D], chip.xnT[:, k, t * P:(t + 1) * P], w[2][:, k, :],
                                             start=(k == 0), stop=(k == KT - 1))
                    last.then_inc(pj, 1)
                    if centre is not None and n < NQK:
                        pe.wait_ge(rawo, n + 1)
                        pe.matmul(chip.banks[2 + n % 2], cm[:, 0, :], raw[n % 2][:], start=True, stop=False,
                                  skip_group_check=True).then_inc(cen, 1)
                        pe.wait_ge(sqd, n + 1)
                        pe.matmul(chip.banks[2 + n % 2], cm[:, 1, :], sqr[n % 2][:], start=False, stop=True,
                                  skip_group_check=True).then_inc(cen, 1)
                pe.wait_ge(pjo, NQK + NT)

                def scores(i):
                    t, g = steps[i]
                    b = t // 2
                    if i >= 1:
                        pe.wait_ge(srd, i)
                    for j in range(4):
                        r = slice(32 * j, 32 * j + 32)
                        last = pe.matmul(chip.s_all[:, j * 512:j * 512 + SQ], qk[0][r, g, t * P:(t + 1) * P],
                                         qk[1][r, g, b * SQ:(b + 1) * SQ], start=True, stop=True)
                    last.then_inc(sr, 1)

                scores(0)
                for i, (t, g) in enumerate(steps):
                    if i + 1 < len(steps):
                        scores(i + 1)
                    pe.wait_ge(ex, i + 1)
                    for h in range(2):
                        if i >= 1:
                            pe.wait_ge(tro, 2 * i - 1 + h)
                        for jk in range(4 * h, 4 * h + 4):
                            last = pe.transpose(chip.banks[h][:, (jk % 4) * P:(jk % 4 + 1) * P],
                                                pr[i % 2][:, jk // 2, (jk % 2) * P:(jk % 2 + 1) * P], chip.ident[:])
                        last.then_inc(tr, 1)
                    pe.wait_ge(tro, 2 * i + 2)
                    if i >= 2:
                        pe.wait_ge(od, i - 1)
                    for j in range(4):
                        for kt in range(2):
                            last = pe.matmul(chip.banks[2 + i % 2][:, 16 * j:16 * j + 16], pT[i % 2][:, 2 * j + kt, :],
                                             v[:, 2 * (t // 2) + kt, (4 * g + j) * 16:(4 * g + j + 1) * 16],
                                             start=(kt == 0), stop=(kt == 1))
                    last.then_inc(pv, 1)

            @block.scalar
            def _(act):
                if scale is not None:
                    act.activation(s4[:], scale, ACT.Copy, scale=0.25).then_inc(s4d, 1)
                    act.wait_ge(s4d, 1)
                for n in range(NQK + NT):
                    act.wait_ge(pj, n + 1)
                    if n < NQK and centre is not None:
                        act.activation(raw[n % 2][:], chip.banks[n % 2], ACT.Copy).then_inc(rawo, 1)
                        act.wait_ge(cen, 2 * n + 1)
                        act.activation(sqr[n % 2][:], chip.banks[2 + n % 2], ACT.Square).then_inc(sqd, 1)
                        act.wait_ge(cen, 2 * n + 2)
                        act.activation(qk[n // NG][:, n % NG, :], chip.banks[2 + n % 2], ACT.Copy,
                                       scale=(1 / 16 if n < NG else 1.0)).then_inc(pjo, 1)
                    elif n < NQK:
                        act.activation(qk[n // NG][:, n % NG, :], chip.banks[n % 2], ACT.Copy,
                                       scale=(s4[:] if n < NG else scale)).then_inc(pjo, 1)
                    else:
                        act.activation(v[:, n - NQK, :], chip.banks[n % 2][:, 0:D], ACT.Copy,
                                       scale=(scale if scale is not None else 1.0)).then_inc(pjo, 1)
                for i in range(len(steps)):
                    act.wait_ge(nmd, i + 1)
                    if i >= 2:
                        act.wait_ge(tr, 2 * (i - 1))
                        act.wait_ge(rcd, i - 1)
                    for j in range(4):
                        last = act.activation(pr[i % 2][:, j, :], sc[i % 2][:, j, :], ACT.Exp, bias=nm[i % 2][:, j:j + 1],
                                              accum_out=sm[i % 2][:, j:j + 1])
                    last.then_inc(ex, 1)
                    if i >= 2:
                        act.wait_ge(pv, i - 1)
                    act.wait_ge(tr, 2 * i + 1)
                    act.activation(pT[i % 2][:, 0:4, :], chip.banks[0].rearrange("p (a q) -> p a q", q=P), ACT.Copy).then_inc(tro, 1)
                    act.wait_ge(tr, 2 * i + 2)
                    act.activation(pT[i % 2][:, 4:8, :], chip.banks[1].rearrange("p (a q) -> p a q", q=P), ACT.Copy).then_inc(tro, 1)

            @block.vector
            def _(dve):
                if mask is not None:
                    dve.wait_ge(ld, NLD)

                def front(i):
                    t, g = steps[i]
                    dve.wait_ge(sr, i + 1)
                    if i >= 2:
                        dve.wait_ge(ex, i - 1)
                    s_in = chip.s_all[:].rearrange("p (j c) -> p j c", j=4)[:, :, 0:SQ]
                    if mask is not None:
                        dve.tensor_tensor(sc[i % 2][:], s_in, mk[:, t % 2, :].unsqueeze(1).to_broadcast([P, 4, SQ]),
                                          ALU.add).then_inc(srd, 1)
                    else:
                        dve.tensor_copy(sc[i % 2][:], s_in).then_inc(srd, 1)
                    dve.wait_ge(srd, i + 1)
                    dve.tensor_reduce(nm[i % 2][:], sc[i % 2][:], AX.X, ALU.max, negate=True).then_inc(nmd, 1)

                front(0)
                for i, (t, g) in enumerate(steps):
                    if i + 1 < len(steps):
                        front(i + 1)
                    dve.wait_ge(ex, i + 1)
                    if i >= 2:
                        dve.wait_ge(od, i - 1)
                    dve.reciprocal(rc[i % 2][:], sm[i % 2][:]).then_inc(rcd, 1)
                    dve.wait_ge(rcd, i + 1)
                    dve.wait_ge(pv, i + 1)
                    dve.tensor_tensor(att[:, t, g * 64:(g + 1) * 64].rearrange("p (j e) -> p j e", e=16),
                                      chip.banks[2 + i % 2][:, 0:64].rearrange("p (j e) -> p j e", e=16),
                                      rc[i % 2][:].unsqueeze(2).to_broadcast([P, 4, 16]), ALU.mult).then_inc(od, 1)
                dve.wait_ge(od, len(steps))


def experts(chip, tag, pT, uT, w1T, w2T, b2, tri):
    nc = chip.nc
    L, DA = 12, 64
    NC3 = NT * 3
    with ExitStack() as scope:
        pw = chip.sb(f"{tag}_pw", [P, KT, DA], F32, scope)
        uw = chip.sb(f"{tag}_uw", [DA, 3 * L], F32, scope)
        ws = [chip.sb(f"{tag}_ws{i}", [P, KT, L * D], F32, scope) for i in range(2)]
        bb = chip.sb(f"{tag}_bb", [L, D], F32, scope)
        tr_ = chip.sb(f"{tag}_tri", [P, L, L], F32, scope)
        xa = chip.sb(f"{tag}_xa", [DA, TOK], F32, scope)
        z = chip.sb(f"{tag}_z", [P, NC3, L], F32, scope)
        gt = chip.sb(f"{tag}_gt", [P, NC3, L, L], F32, scope)
        eq = chip.sb(f"{tag}_eq", [P, NC3, L, L], F32, scope)
        rk = chip.sb(f"{tag}_rk", [P, NC3, L], F32, scope)
        mz = chip.sb(f"{tag}_mz", [P, NC3], F32, scope)
        ez = chip.sb(f"{tag}_ez", [P, NC3, L], F32, scope)
        cz = chip.sb(f"{tag}_cz", [P, NC3, L], F32, scope)
        c3T = chip.sb(f"{tag}_c3T", [L, TOK], F32, scope)
        y = [chip.sb(f"{tag}_y{i}", [P, NT, D], F32, scope) for i in range(2)]
        hid = chip.sb(f"{tag}_hid", [P, NT, D], F32, scope)
        hT = chip.sb(f"{tag}_hT", [P, KT, TOK], F32, scope)
        names = ("ld", "ldw", "xap", "xao", "zp", "zc", "rt", "exd", "c3p", "c3o", "ep", "acc", "gl", "ht", "hto", "bp")
        ld, ldw, xap, xao, zp, zc, rt, exd, c3p, c3o, ep, acc, gl, ht, hto, bp = (chip.sem(f"{tag}_{x}") for x in names)
        PAIRS = L // 2
        tiles = [(e, t) for e in range(PAIRS) for t in range(NT)]
        NTL = len(tiles)
        with nc.Block() as block:
            @block.sync
            def _(sp):
                sp.dma_start(pw[:], pT.rearrange("(k p) n -> p k n", p=P)).then_inc(ld, 16)
                sp.dma_start(uw[:], uT).then_inc(ld, 16)
                sp.dma_start(bb[:], b2).then_inc(ld, 16)
                sp.dma_start(tr_[:], tri.rearrange("a b -> (a b)").partition_broadcast(P)).then_inc(ld, 16)
                for i, src in enumerate((w1T, w2T)):
                    sp.dma_start(ws[i][:], src.rearrange("(k p) n -> p k n", p=P)).then_inc(ldw, 16)
                    sp.wait_ge(ldw, 16 * (i + 1))

            @block.tensor
            def _(pe):
                pe.wait_ge(ld, 64)
                for k in range(KT):
                    last = pe.matmul(chip.banks[0][0:DA, :], pw[:, k, :], chip.xnT[:, k, :], start=(k == 0), stop=(k == KT - 1))
                last.then_inc(xap, 1)
                pe.wait_ge(xao, 1)
                for t in range(NT):
                    last = pe.matmul(chip.banks[1][:, t * 3 * L:(t + 1) * 3 * L], xa[:, t * P:(t + 1) * P], uw[:],
                                     start=True, stop=True)
                last.then_inc(zp, 1)

                def mixture(i, srcT):
                    pe.wait_ge(ldw, 16 * (i + 1))
                    for n, (e, t) in enumerate(tiles):
                        m = i * NTL + n
                        if m >= 4:
                            pe.wait_ge(acc, 2 * (m - 3))
                        for k in range(KT):
                            last = pe.matmul(chip.banks[4 + n % 4], srcT[:, k, t * P:(t + 1) * P],
                                             ws[i][:, k, e * 2 * D:(e + 1) * 2 * D], start=(k == 0), stop=(k == KT - 1))
                        last.then_inc(ep, 1)

                mixture(0, chip.xnT)
                pe.wait_ge(rt, 10)
                for t in range(NT):
                    last = pe.transpose(chip.banks[2][0:L, t * P:(t + 1) * P], cz[:, t * 3 + 2, :], chip.ident[:])
                last.then_inc(c3p, 1)
                for k in range(KT):
                    for t in range(NT):
                        pe.wait_ge(gl, t + 1)
                        last = pe.transpose(chip.banks[k][:, t * P:(t + 1) * P], hid[:, t, k * P:(k + 1) * P], chip.ident[:])
                    last.then_inc(ht, 1)
                pe.wait_ge(hto, KT)
                mixture(1, hT)
                pe.wait_ge(c3o, 1)
                for t in range(NT):
                    last = pe.matmul(chip.banks[t // 2][:, (t % 2) * D:(t % 2 + 1) * D], c3T[:, t * P:(t + 1) * P], bb[:],
                                     start=True, stop=True)
                last.then_inc(bp, 1)

            @block.scalar
            def _(act):
                act.wait_ge(xap, 1)
                act.activation(xa[:], chip.banks[0][0:DA, :], ACT.Copy).then_inc(xao, 1)
                act.wait_ge(rt, 7)
                act.activation(ez[:], ez[:], ACT.Exp).then_inc(exd, 1)
                act.wait_ge(acc, 2 * NTL)
                for t in range(NT):
                    act.activation(hid[:, t, :], y[0][:, t, :], ACT.Gelu).then_inc(gl, 1)
                act.wait_ge(c3p, 1)
                act.activation(c3T[:], chip.banks[2][0:L, :], ACT.Copy).then_inc(c3o, 1)
                for k in range(KT):
                    act.wait_ge(ht, k + 1)
                    act.activation(hT[:, k, :], chip.banks[k], ACT.Copy).then_inc(hto, 1)

            @block.vector
            def _(dve):
                dve.wait_ge(zp, 1)
                dve.wait_ge(ld, 64)
                dve.tensor_copy(z[:], chip.banks[1][:, 0:NC3 * L].rearrange("p (c l) -> p c l", l=L)).then_inc(zc, 1)
                dve.wait_ge(zc, 1)
                for c in range(NC3):
                    zj = z[:, c, :].unsqueeze(1).to_broadcast([P, L, L])
                    zi = z[:, c, :].unsqueeze(2).to_broadcast([P, L, L])
                    dve.tensor_tensor(gt[:, c], zj, zi, ALU.is_gt)
                    last = dve.tensor_tensor(eq[:, c], zj, zi, ALU.is_equal)
                last.then_inc(rt, 1)
                dve.tensor_reduce(mz[:], z[:], AX.X, ALU.max).then_inc(rt, 1)
                dve.wait_ge(rt, 2)
                dve.tensor_tensor(eq[:].rearrange("p c i j -> p c (i j)"), eq[:].rearrange("p c i j -> p c (i j)"),
                                  tr_[:].rearrange("p i j -> p (i j)").unsqueeze(1).to_broadcast([P, NC3, L * L]), ALU.mult).then_inc(rt, 1)
                dve.wait_ge(rt, 3)
                dve.tensor_tensor(gt[:], gt[:], eq[:], ALU.add).then_inc(rt, 1)
                dve.wait_ge(rt, 4)
                dve.tensor_reduce(rk[:], gt[:], AX.X, ALU.add).then_inc(rt, 1)
                dve.wait_ge(rt, 5)
                dve.tensor_scalar(rk[:], rk[:], 2.5, None, ALU.is_lt).then_inc(rt, 1)
                dve.tensor_tensor(ez[:], z[:], mz[:].unsqueeze(2).to_broadcast([P, NC3, L]), ALU.subtract).then_inc(rt, 1)
                dve.wait_ge(exd, 1)
                dve.wait_ge(rt, 7)
                dve.tensor_tensor(ez[:], ez[:], rk[:], ALU.mult).then_inc(rt, 1)
                dve.wait_ge(rt, 8)
                dve.tensor_reduce(mz[:], ez[:], AX.X, ALU.add).then_inc(rt, 1)
                dve.wait_ge(rt, 9)
                dve.reciprocal(mz[:], mz[:]).then_inc(zc, 1)
                dve.wait_ge(zc, 2)
                dve.tensor_tensor(cz[:], ez[:], mz[:].unsqueeze(2).to_broadcast([P, NC3, L]), ALU.mult).then_inc(rt, 1)
                dve.wait_ge(rt, 10)
                for i in range(2):
                    for n, (e, t) in enumerate(tiles):
                        m = i * NTL + n
                        dve.wait_ge(ep, m + 1)
                        for h in range(2):
                            src = chip.banks[4 + n % 4][:, h * D:(h + 1) * D]
                            c = cz[:, t * 3 + i, 2 * e + h:2 * e + h + 1]
                            if e == 0 and h == 0:
                                dve.tensor_scalar(y[i][:, t, :], src, c, None, ALU.mult).then_inc(acc, 1)
                            else:
                                dve.wait_ge(acc, 2 * m + h if h else 2 * (m - NT) + 2)
                                dve.scalar_tensor_tensor(out=y[i][:, t, :], in0=src, scalar=c, in1=y[i][:, t, :],
                                                         op0=ALU.mult, op1=ALU.add).then_inc(acc, 1)
                dve.wait_ge(acc, 4 * NTL)
                dve.tensor_tensor(chip.x[:], chip.x[:], y[1][:], ALU.add).then_inc(zc, 1)
                dve.wait_ge(bp, 1)
                dve.wait_ge(zc, 3)
                for t in range(NT):
                    dve.tensor_tensor(chip.x[:, t, :], chip.banks[t // 2][:, (t % 2) * D:(t % 2 + 1) * D], chip.x[:, t, :],
                                      ALU.add).then_inc(zc, 1)
                dve.wait_ge(zc, 3 + NT)


MAGIC = 12582912.0


def dequantised_weights(chip, tag, mats, outs):
    nc = chip.nc
    F = 1536
    NBK = F // 32
    with ExitStack() as scope:
        w = [chip.sb(f"{tag}_w{i}", [P, NBK, 32], F32, scope) for i in range(3)]
        s = [chip.sb(f"{tag}_s{i}", [P, NBK], F32, scope) for i in range(3)]
        r = [chip.sb(f"{tag}_r{i}", [P, NBK], F32, scope) for i in range(3)]
        ld, st, tr, tro = (chip.sem(f"{tag}_{x}") for x in ("ld", "st", "tr", "tro"))
        jobs = []
        for i in range(3):
            rows, cols = mats[i].shape
            o = rows // P
            wv = w[i][:].rearrange("p b e -> p (b e)").rearrange("p (o c) -> p o c", o=o)
            for k in range(cols // P):
                for o0 in range(0, o, 4):
                    on = min(4, o - o0)
                    jobs.append((i, outs[i][:, k, o0 * P:(o0 + on) * P], [wv[:, o0 + a, k * P:(k + 1) * P] for a in range(on)]))
        with nc.Block() as block:
            @block.sync
            def _(sp):
                for i in range(3):
                    rows, cols = mats[i].shape
                    sp.dma_start(w[i][:].rearrange("p b e -> p (b e)").rearrange("p (o c) -> p o c", o=rows // P),
                                 mats[i].rearrange("(o p) c -> p o c", p=P)).then_inc(ld, 16)
                sp.wait_ge(ld, 48)

            @block.vector
            def _(dve):
                n = 0

                def link(ins):
                    nonlocal n
                    n += 1
                    ins.then_inc(st, 1)
                    dve.wait_ge(st, n)

                dve.wait_ge(ld, 48)
                for i in range(3):
                    wide = lambda a: a[:].unsqueeze(2).to_broadcast([P, NBK, 32])
                    link(dve.tensor_reduce(s[i][:], w[i][:], AX.X, ALU.max, apply_absolute_value=True))
                    link(dve.tensor_scalar(s[i][:], s[i][:], 1.0 / 7.0, 1e-12, ALU.mult, ALU.max))
                    link(dve.reciprocal(r[i][:], s[i][:]))
                    link(dve.tensor_tensor(w[i][:], w[i][:], wide(r[i]), ALU.mult))
                    link(dve.tensor_scalar(w[i][:], w[i][:], MAGIC, MAGIC, ALU.add, ALU.subtract))
                    link(dve.tensor_scalar(w[i][:], w[i][:], 7.0, -8.0, ALU.min, ALU.max))
                    link(dve.tensor_tensor(w[i][:], w[i][:], wide(s[i]), ALU.mult))

            @block.tensor
            def _(pe):
                for n, (i, _dst, srcs) in enumerate(jobs):
                    pe.wait_ge(st, 7 * (i + 1))
                    if n >= 4:
                        pe.wait_ge(tro, n - 3)
                    for a, src in enumerate(srcs):
                        last = pe.transpose(chip.banks[n % 4][:, a * P:(a + 1) * P], src, chip.ident[:])
                    last.then_inc(tr, 1)

            @block.scalar
            def _(act):
                for n, (_i, dst, srcs) in enumerate(jobs):
                    act.wait_ge(tr, n + 1)
                    act.activation(dst, chip.banks[n % 4][:, 0:len(srcs) * P], ACT.Copy).then_inc(tro, 1)


def quantised_ffn(chip, tag, upT, gateT, downT, out_dram):
    nc = chip.nc
    I6 = 6
    QM = 32767.0
    with ExitStack() as scope:
        xq = chip.sb(f"{tag}_xq", [P, KT, TOK], F32, scope)
        up = chip.sb(f"{tag}_up", [P, I6, TOK], F32, scope)
        gate = chip.sb(f"{tag}_gate", [P, I6, TOK], F32, scope)
        sg = chip.sb(f"{tag}_sg", [P, I6, TOK], F32, scope)
        am = chip.sb(f"{tag}_am", [P, 5], F32, scope)
        ar = chip.sb(f"{tag}_ar", [P, 5], F32, scope)
        sc = chip.sb(f"{tag}_sc", [P, 5], F32, scope)
        rc = chip.sb(f"{tag}_rc", [P, 5], F32, scope)
        st, amd, ard, mm, ev, sgd, dn, out, qd = (chip.sem(f"{tag}_{x}") for x in ("st", "amd", "ard", "mm", "ev", "sgd", "dn", "out", "qd"))
        stored = chip.sem(f"{tag}_stored")
        with nc.Block() as block:
            @block.vector
            def _(dve):
                n = 0

                def link(ins):
                    nonlocal n
                    n += 1
                    ins.then_inc(st, 1)
                    dve.wait_ge(st, n)

                def qdq(i, t):
                    dve.tensor_reduce(am[:, i:i + 1], t, AX.XY, ALU.max, apply_absolute_value=True).then_inc(amd, 1)
                    dve.wait_ge(ard, i + 1)
                    link(dve.tensor_scalar(sc[:, i:i + 1], ar[:, i:i + 1], 1.0 / QM, 1e-12, ALU.mult, ALU.max))
                    link(dve.reciprocal(rc[:, i:i + 1], sc[:, i:i + 1]))
                    link(dve.tensor_scalar(t, t, rc[:, i:i + 1], MAGIC, ALU.mult, ALU.add))
                    link(dve.tensor_scalar(t, t, MAGIC, QM, ALU.subtract, ALU.min))
                    dve.tensor_scalar(t, t, -QM - 1.0, sc[:, i:i + 1], ALU.max, ALU.mult).then_inc(qd, 1)
                    dve.wait_ge(qd, i + 1)

                link(dve.tensor_copy(xq[:], chip.xnT[:]))
                qdq(0, xq[:])
                dve.wait_ge(ev, I6)
                qdq(1, gate[:])
                dve.wait_ge(ev, 2 * I6)
                qdq(2, up[:])
                dve.wait_ge(sgd, 1)
                link(dve.tensor_scalar(sg[:], sg[:], 65536.0, MAGIC, ALU.mult, ALU.add))
                link(dve.tensor_scalar(sg[:], sg[:], MAGIC, 65535.0, ALU.subtract, ALU.min))
                link(dve.tensor_scalar(sg[:], sg[:], 0.0, 1.0 / 65536.0, ALU.max, ALU.mult))
                link(dve.tensor_tensor(gate[:], gate[:], sg[:], ALU.mult))
                qdq(3, gate[:])
                link(dve.tensor_tensor(gate[:], gate[:], up[:], ALU.mult))
                qdq(4, gate[:])
                for t in range(NT):
                    dve.wait_ge(dn, t + 1)
                    dve.tensor_tensor(chip.x[:, t, :], chip.banks[t][:, 0:D], chip.x[:, t, :], ALU.add).then_inc(out, 1)

            @block.gpsimd
            def _(pool):
                for i in range(5):
                    pool.wait_ge(amd, i + 1)
                    pool.partition_all_reduce(ar[:, i:i + 1], am[:, i:i + 1], P, bass.bass_isa.ReduceOp.absmax).then_inc(ard, 1)

            @block.tensor
            def _(pe):
                pe.wait_ge(qd, 1)
                for n in range(2 * I6):
                    w = gateT if n < I6 else upT
                    m = n % I6
                    if n >= 4:
                        pe.wait_ge(ev, n - 3)
                    for k in range(KT):
                        last = pe.matmul(chip.banks[n % 4], w[:, k, m * P:(m + 1) * P], xq[:, k, :],
                                         start=(k == 0), stop=(k == KT - 1))
                    last.then_inc(mm, 1)
                pe.wait_ge(ev, 2 * I6)
                pe.wait_ge(qd, 5)
                for t in range(NT):
                    for k in range(I6):
                        last = pe.matmul(chip.banks[t][:, 0:D], gate[:, k, t * P:(t + 1) * P], downT[:, k, :],
                                         start=(k == 0), stop=(k == I6 - 1))
                    last.then_inc(dn, 1)

            @block.scalar
            def _(act):
                for n in range(2 * I6):
                    act.wait_ge(mm, n + 1)
                    act.activation((gate if n < I6 else up)[:, n % I6, :], chip.banks[n % 4], ACT.Copy).then_inc(ev, 1)
                act.wait_ge(qd, 2)
                act.activation(sg[:], gate[:], ACT.Sigmoid).then_inc(sgd, 1)

            @block.sync
            def _(sp):
                ov = out_dram.rearrange("(t p) d -> p t d", p=P)
                for t in range(NT):
                    sp.wait_ge(out, t + 1)
                    sp.dma_start(ov[:, t, :], chip.x[:, t, :]).then_inc(stored, 16)
                sp.wait_ge(stored, 16 * NT)


def perceiver(nc, t, out):
    with ExitStack() as ctx:
        chip = Chip(nc, ctx)
        load_constants(chip, t["x"])
        scratch = [(nc.dram_tensor(f"keys{l}", [2, NH * hd, B * SK], F16).ap(),
                    nc.dram_tensor(f"values{l}", [NH, P, B * SK // P, 1 + 2 * hd], F16).ap())
                   for l, hd in enumerate((16, 64))]
        queries = [nc.dram_tensor(f"queries{l}", [2, NH * hd, TOK], F16).ap() for l, hd in enumerate((16, 64))]
        project_context(chip, t["ctxT"], [(t["a0k"], t["a0v"]), (t["a1k"], t["a1v"])], t["a1bk"], scratch)

        layer_norm(chip, "ln0")
        project_queries(chip, "q0", t["a0q"], None, 16, queries[0])
        with ExitStack() as scope:
            att = chip.sb("att0", [P, NT, D], F32, scope)
            cross_attention(chip, "x0", 16, queries[0], *scratch[0], att, t["mask"], t["ones2"], t["qrows"])
            rows_project(chip, "o0", att, D, t["a0o"], add_to_x(chip))
        if LAST >= 2:
            layer_norm(chip, "ln1")
            with ExitStack() as scope:
                sc = chip.sb("sn", [P, 2], F32, scope)
                spectral_scale(chip, "sq", t["s0w"], 3 * D, t["s0u"], t["s0s"], sc[:, 0:1])
                spectral_scale(chip, "sp", t["s0p"], D, t["s0pu"], t["s0ps"], sc[:, 1:2])
                att = chip.sb("att1", [P, NT, D], F32, scope)
                self_attention(chip, "s0", t["s0q"], t["s0k"], t["s0v"], att, scale=sc[:, 0:1], mask=t["causal"])

                def finish(dve, n, done):
                    dve.scalar_tensor_tensor(out=chip.x[:, n, :], in0=chip.banks[n][:, 0:D], scalar=sc[:, 1:2],
                                             in1=chip.x[:, n, :], op0=ALU.mult, op1=ALU.add).then_inc(done, 1)
                rows_project(chip, "o1", att, D, t["s0p"], finish)
        if LAST >= 3:
            layer_norm(chip, "ln2")
            experts(chip, "moe", t["f0p"], t["f0u"], t["f0w1"], t["f0w2"], t["f0b"], t["tri"])
        if LAST >= 4:
            chip.recycle_semaphores()
            layer_norm(chip, "ln3")
            project_queries(chip, "q1", t["a1q"], t["a1bq"], 64, queries[1])
            with ExitStack() as scope:
                acc = chip.sb("acc1", [P, NT, D], F32, scope)
                att = chip.sb("att2", [P, NT, NH * 64], F32, scope)
                cross_attention(chip, "x1", 64, queries[1], *scratch[1], att)

                def finish(dve, n, done):
                    dve.tensor_copy(acc[:, n, :], chip.banks[n][:, 0:D]).then_inc(done, 1)
                rows_project(chip, "o2", att, NH * 64, t["a1o"], finish, bias_in=t["a1bv"])
                normed_output(chip, "no", acc, t["a1bo"], t["a1g"], t["a1b"])
        if LAST >= 5:
            layer_norm(chip, "ln4")
            with ExitStack() as scope:
                att = chip.sb("att3", [P, NT, D], F32, scope)
                self_attention(chip, "s1", t["s1q"], t["s1k"], t["s1v"], att, centre=t["centre"])
                rows_project(chip, "o3", att, D, t["s1o"], add_to_x(chip))
        if LAST >= 6:
            layer_norm(chip, "ln5")
            with ExitStack() as scope:
                upT = chip.sb("upT", [P, KT, 768], F32, scope)
                gateT = chip.sb("gateT", [P, KT, 768], F32, scope)
                downT = chip.sb("downT", [P, 6, D], F32, scope)
                dequantised_weights(chip, "dq", [t["f1u"], t["f1g"], t["f1d"]], [upT, gateT, downT])
                quantised_ffn(chip, "f1", upT, gateT, downT, out)
        else:
            stored = chip.sem("stored")
            with nc.Block() as block:
                @block.sync
                def _(sp):
                    sp.dma_start(out.rearrange("(t p) d -> p t d", p=P), chip.x[:]).then_inc(stored, 16)
                    sp.wait_ge(stored, 16)


def kernel(**inputs):
    import numpy as np
    import concourse.bacc as bacc
    from concourse.bass_utils import run_bass_kernel_spmd

    def a(name):
        return np.asarray(inputs[name])

    def columns(name):
        return a(name).reshape(-1, P).T

    def pad_heads(w):
        out = np.zeros((w.shape[0], NH, 32), w.dtype)
        out[:, :, :16] = w.reshape(w.shape[0], NH, 16)
        return out.reshape(w.shape[0], NH * 32)

    centre = np.zeros((2, P, P), np.float32)
    for h in range(4):
        s = slice(32 * h, 32 * h + 16)
        centre[0, s, s] = np.eye(16) - 1 / 16
        centre[1, s, 32 * h + 16] = 1 / 15
    qrows = np.zeros((16, SQ), np.float16)
    qrows[0] = 32768.0
    qkv = a("L0_attn_W_qkv")
    host = {
        "x": a("x").reshape(TOK, D), "ctxT": a("ctx_1024").reshape(B * SK, D).T,
        "mask": a("mask_BxS2_bk1"),
        "ones2": np.ones((2, SK), np.float16), "qrows": qrows,
        "a0q": a("L0_xattn_Wq").T, "a0k": a("L0_xattn_Wk").T, "a0v": a("L0_xattn_Wv").T, "a0o": a("L0_xattn_Wo").T,
        "s0w": qkv, "s0q": pad_heads(qkv[:, 0:D]), "s0k": pad_heads(qkv[:, D:2 * D]), "s0v": qkv[:, 2 * D:],
        "s0u": a("L0_attn_u_qkv"), "s0s": a("L0_attn_sigma_qkv"), "s0p": a("L0_attn_W_proj"),
        "s0pu": a("L0_attn_u_proj"), "s0ps": a("L0_attn_sigma_proj"),
        "causal": np.triu(np.full((SQ, SQ), -1e30, np.float32), 1),
        "f0p": a("L0_ffn_P_w").T, "f0u": np.concatenate([a("L0_ffn_U1"), a("L0_ffn_U2"), a("L0_ffn_U3")]).T,
        "f0w1": a("L0_ffn_W1").transpose(2, 0, 1).reshape(D, 12 * D),
        "f0w2": a("L0_ffn_W2").transpose(2, 0, 1).reshape(D, 12 * D), "f0b": a("L0_ffn_b2"),
        "tri": np.tril(np.ones((12, 12), np.float32), -1),
        "a1q": a("L1_xattn_Wq"), "a1bq": columns("L1_xattn_bq"), "a1k": a("L1_xattn_Wk"), "a1bk": columns("L1_xattn_bk"),
        "a1v": a("L1_xattn_Wv"), "a1bv": columns("L1_xattn_bv"), "a1o": a("L1_xattn_Wo"), "a1bo": a("L1_xattn_bo"),
        "a1g": a("L1_xattn_ln_gamma"), "a1b": a("L1_xattn_ln_beta"),
        "s1q": pad_heads(a("L1_attn_Wq")), "s1k": pad_heads(a("L1_attn_Wk")), "s1v": a("L1_attn_Wv"),
        "s1o": a("L1_attn_Wo"), "centre": centre,
        "f1g": a("L1_ffn_w_gate"), "f1u": a("L1_ffn_w_up"), "f1d": a("L1_ffn_w_down"),
    }
    nc = bacc.Bacc("TRN2", target_bir_lowering=False, num_devices=1)
    arrays, t = {}, {}
    for name, value in host.items():
        value = np.ascontiguousarray(value)
        arrays[f"in_{name}"] = value
        t[name] = nc.dram_tensor(f"in_{name}", value.shape, mybir.dt.from_np(value.dtype), kind="ExternalInput").ap()
    out = nc.dram_tensor("out_0", (TOK, D), F32, kind="ExternalOutput").ap()
    perceiver(nc, t, out)
    r = run_bass_kernel_spmd(nc, [arrays], core_ids=[0])
    return r.results[0]["out_0"].reshape(B, SQ, D)
```

```python
import concourse.bass as bass
from concourse import mybir
from contextlib import ExitStack

F32 = mybir.dt.float32
F16 = mybir.dt.float16
BF16 = mybir.dt.bfloat16
U8 = mybir.dt.uint8
ALU = mybir.AluOpType
ACT = mybir.ActivationFunctionType
AX = mybir.AxisListType

P = 128
B = 2
SQ = 256
NT = B * SQ // P
TOK = B * SQ
D = 256
KT = D // P
SK = 4096
NH = 16
CH = 512
NCH = B * SK // CH


def hold(eng, sem, value, passed):
    eng.wait_ge(sem, value)
    eng.sem_inc(passed, 1)


class Chip:

    def __init__(self, nc, ctx):
        self.nc, self.ctx, self.sems = nc, ctx, []
        self.sem_scope = ctx.enter_context(ExitStack())
        self.s_all = self.psum("s_all", 2048)
        self.s_ps = [self.s_all[:, 0:1024], self.s_all[:, 1024:2048]]
        self.s_banks = [self.s_all[:, i * 512:(i + 1) * 512] for i in range(4)]
        self.a_ps = [self.psum("a0", 512), self.psum("a1", 512)]
        self.o_ps = [self.psum("o0", 512), self.psum("o1", 512)]
        self.banks = [self.a_ps[0][:, :], self.a_ps[1][:, :], self.o_ps[0][:, :], self.o_ps[1][:, :],
                      *self.s_banks]
        self.x = self.sb("x", [P, NT, D], F32)
        self.xn = self.sb("xn", [P, NT, D], F32)
        self.xnT = self.sb("xnT", [P, KT, TOK], F32)
        self.ident = self.sb("ident", [P, P], F32)
        self.ones = self.sb("ones", [P, P], F32)
        self.half = self.sb("half", [P, 8], F32)

    def psum(self, name, cols):
        return self.ctx.enter_context(self.nc.psum_tensor(name, [P, cols], F32))

    def sb(self, name, shape, dt, scope=None):
        return (scope or self.ctx).enter_context(self.nc.sbuf_tensor(name, shape, dt))

    def sem(self, name):
        self.sems.append(self.sem_scope.enter_context(self.nc.semaphore(name)))
        return self.sems[-1]

    def recycle_semaphores(self):
        sems, self.sems = self.sems, []
        with self.nc.Block() as block:
            @block.gpsimd
            def _(pool):
                for s in sems[0::4]:
                    pool.sem_clear(s)

            @block.vector
            def _(dve):
                for s in sems[1::4]:
                    dve.sem_clear(s)

            @block.scalar
            def _(act):
                for s in sems[2::4]:
                    act.sem_clear(s)

            @block.tensor
            def _(pe):
                for s in sems[3::4]:
                    pe.sem_clear(s)
        self.sem_scope.close()


def load_constants(chip, x_dram, query_weight, context):
    nc = chip.nc
    loaded, made = chip.sem("x_loaded"), chip.sem("const_made")
    with nc.Block() as block:
        @block.sync
        def _(sp):
            sp.dma_start(chip.x[:], x_dram.rearrange("(t p) d -> p t d", p=P)).then_inc(loaded, 16)
            query_weight.loads(sp)
            context.first_loads(sp)
            sp.wait_ge(loaded, 16)

        @block.gpsimd
        def _(pool):
            pool.memset(chip.ones[:], 1.0).then_inc(made, 1)
            pool.memset(chip.half[:], -0.5).then_inc(made, 1)
            pool.memset(chip.ident[:], 0.0).then_inc(made, 1)
            pool.wait_ge(made, 3)
            pool.affine_select(out=chip.ident[:], in_=chip.ident[:], compare_op=ALU.not_equal, fill=1.0,
                               base=0, pattern=[[-1, P]], channel_multiplier=1).then_inc(made, 1)


def layer_norm(chip, tag, after=()):
    nc = chip.nc
    with ExitStack() as scope:
        st = chip.sb(f"{tag}_st", [P, NT, 6], F32, scope)
        mv = chip.sb(f"{tag}_mv", [P, NT, 2], F32, scope)
        ve = chip.sb(f"{tag}_ve", [P, NT], F32, scope)
        rs = chip.sb(f"{tag}_rs", [P, NT], F32, scope)
        stats, var, rstd, xn_done, tr, tr_out = (
            chip.sem(f"{tag}_{n}") for n in ("stats", "var", "rstd", "xn", "tr", "trout"))
        with nc.Block() as block:
            @block.sync
            def _(sp):
                for p in after:
                    p.loads(sp)

            @block.vector
            def _(dve):
                for t in range(NT):
                    dve.bn_stats(st[:, t, :], chip.x[:, t, :]).then_inc(stats, 1)
                dve.wait_ge(stats, NT)
                for t in range(NT):
                    dve.bn_aggr(mv[:, t, :], st[:, t, :]).then_inc(stats, 1)
                dve.wait_ge(stats, 2 * NT)
                dve.tensor_scalar(ve[:], mv[:, :, 1], 1e-5, None, ALU.add).then_inc(var, 1)
                dve.wait_ge(rstd, 1)
                for t in range(NT):
                    dve.tensor_scalar(chip.xn[:, t, :], chip.x[:, t, :], mv[:, t, 0:1], rs[:, t:t + 1],
                                      ALU.subtract, ALU.mult).then_inc(xn_done, 1)
                dve.wait_ge(tr, 1)
                dve.tensor_copy(chip.xnT[:, 0, :], chip.a_ps[0][:]).then_inc(var, 1)

            @block.gpsimd
            def _(pool):
                pool.wait_ge(var, 1)
                pool.tensor_tensor(rs[:], ve[:], chip.half[:, 0:NT], ALU.pow).then_inc(rstd, 1)

            @block.tensor
            def _(pe):
                pe.wait_ge(xn_done, NT)
                for k in range(KT):
                    for t in range(NT):
                        last = pe.transpose(chip.a_ps[k][:, t * P:(t + 1) * P],
                                            chip.xn[:, t, k * P:(k + 1) * P], chip.ident[:])
                    last.then_inc(tr, 1)

            @block.scalar
            def _(act):
                act.wait_ge(tr, 2)
                act.activation(chip.xnT[:, 1, :], chip.a_ps[1][:], ACT.Copy).then_inc(tr_out, 1)


class Prefetch:

    def __init__(self, chip, tag, scope, dram):
        self.src = dram.rearrange("(k p) n -> p k n", p=P)
        self.w = chip.sb(f"{tag}_pw", list(self.src.shape), F32, scope)
        self.loaded = chip.sem(f"{tag}_pld")

    def loads(self, sp):
        sp.dma_start(self.w[:], self.src).then_inc(self.loaded, 16)

    def work(self, pool):
        pass


class Context:

    def __init__(self, chip, scope, ctxT, weights, bias_k):
        self.weights, self.bias_k = weights, bias_k
        self.wf = [chip.sb(f"wf{i}", [P, KT, NH * hd], F32, scope) for i, hd in enumerate((16, 16, 64, 64))]
        self.bk = chip.sb("bk", [P, NH * 64 // P], F32, scope)
        self.cf = [chip.sb(f"cf{j}", [P, KT, CH], F32, scope) for j in range(2)]
        self.ctx_v = ctxT.rearrange("(k p) t -> p k t", p=P)
        self.bk_loaded = chip.sem("bk_loaded")
        self.w_loaded, self.c_loaded = [chip.sem(f"w_loaded{i}") for i in range(4)], [chip.sem(f"c_loaded{j}") for j in range(2)]

    def first_loads(self, sp):
        for i in range(4):
            sp.dma_start(self.wf[i][:], self.weights[i // 2][i % 2].rearrange("(k p) n -> p k n", p=P)).then_inc(self.w_loaded[i], 16)
            if i == 1:
                sp.dma_start(self.cf[0][:], self.ctx_v[:, :, 0:CH]).then_inc(self.c_loaded[0], 16)
        sp.dma_start(self.bk[:], self.bias_k).then_inc(self.bk_loaded, 16)
        sp.dma_start(self.cf[1][:], self.ctx_v[:, :, CH:2 * CH]).then_inc(self.c_loaded[1], 16)


def project_context(chip, context, mask, mask_out, scratch, beside):
    nc = chip.nc
    hds = [16, 64]
    dims = [NH * hd for hd in hds]
    SUB = CH // P
    MT = [d // P for d in dims]
    VW = [min(512, d) for d in dims]
    tiles = []
    for l in range(2):
        tiles += [(l, "k", m, 0) for m in range(MT[l])]
        tiles += [(l, "v", m, s) for s in range(SUB) for m in range(dims[l] // VW[l])]
    NTILE = len(tiles)
    NB = 4
    assert 2 * NTILE % NB == 0
    OUTS = 6
    PAIRS = NCH // 2
    with ExitStack() as scope:
        wf, bk, cf, ctx_v = context.wf, context.bk, context.cf, context.ctx_v
        c_loaded = context.c_loaded
        m8 = chip.sb("m8", [B, SK], U8, scope)
        m16 = chip.sb("m16", [B, SK], F16, scope)
        mask_in, mask_made, mask_gone = chip.sem("mask_in"), chip.sem("mask_made"), chip.sem("mask_gone")
        wh = [chip.sb(f"wh{i}", [P, KT, dims[i // 2]], F16, scope) for i in range(4)]
        wl = [chip.sb(f"wl{i}", [P, KT, dims[i // 2]], F16, scope) for i in range(4)]
        chi = [chip.sb(f"chi{j}", [P, KT, CH], F16, scope) for j in range(2)]
        clo = [chip.sb(f"clo{j}", [P, KT, CH], F16, scope) for j in range(2)]
        kst = [[[chip.sb(f"kst{l}{h}{j}", [P, MT[l], CH], F16, scope) for j in range(2)]
                for h in range(2)] for l in range(2)]
        vst = [[chip.sb(f"vst{l}{j}", [P, NH, SUB, 1 + 2 * hds[l]], F16, scope) for j in range(2)]
               for l in range(2)]
        w_hi, w_lo = chip.sem("w_hi"), chip.sem("w_lo")
        c_hi, c_lo, passed = chip.sem("c_hi"), chip.sem("c_lo"), chip.sem("c_passed")
        tile_ready, hi_done, lo_done = chip.sem("tile_ready"), chip.sem("hi_done"), chip.sem("lo_done")
        stage_free = [chip.sem(f"stage_free{j}") for j in range(2)]

        def tile_no(it, j, n):
            return it * (2 * NTILE) + (j * NTILE + n)

        def halves(j, n):
            l, kind, m, s = tiles[n]
            bank = chip.banks[(j * NTILE + n) % NB]
            if kind == "k":
                return bank, kst[l][0][j][:, m, :], kst[l][1][j][:, m, :]
            hd, nh = hds[l], VW[l] // hds[l]
            out = vst[l][j][:, m * nh:(m + 1) * nh, s, :]
            return (bank[:, 0:VW[l]].rearrange("p (h e) -> p h e", e=hd),
                    out[:, :, 1:1 + hd], out[:, :, 1 + hd:1 + 2 * hd])

        with nc.Block() as block:
            @block.sync
            def _(sp):
                sp.dma_start(m8[:], mask).then_inc(mask_in, 16)
                for side in beside:
                    side.loads(sp)

                def step(it, j, last):
                    if not last:
                        hold(sp, c_lo, it * 2 + (j + 1), passed)
                        sp.dma_start(cf[j][:], ctx_v[:, :, bass.ds(it * (2 * CH) + (2 + j) * CH, CH)]).then_inc(c_loaded[j], 16)
                    def split(l, kind):
                        n = max(n for n, tile in enumerate(tiles) if tile[:2] == (l, kind))
                        hold(sp, lo_done, tile_no(it, j, n + 1) + NB, passed)

                    for l in range(2):
                        kd = scratch[l][0].rearrange("h (m p) t -> h p m t", p=P)
                        split(l, "k")
                        for h in range(2):
                            sp.dma_start(kd[h, :, :, bass.ds(it * (2 * CH) + j * CH, CH)], kst[l][h][j][:]).then_inc(stage_free[j], 16)
                        vd = scratch[l][1].rearrange("h p c e -> p h c e")
                        split(l, "v")
                        sp.dma_start(vd[:, :, bass.ds(it * (2 * SUB) + j * SUB, SUB), :], vst[l][j][:]).then_inc(stage_free[j], 16)

                with sp.Fori(0, PAIRS - 1) as it:
                    for j in range(2):
                        step(it, j, False)
                for j in range(2):
                    step(PAIRS - 1, j, True)
                sp.wait_ge(mask_made, 1)
                sp.dma_start(mask_out, m16[:]).then_inc(mask_gone, 16)
                for j in range(2):
                    sp.wait_ge(stage_free[j], PAIRS * OUTS * 16 + 16)
                sp.wait_ge(mask_gone, 16)

            @block.gpsimd
            def _(pool):
                for l in range(2):
                    for j in range(2):
                        pool.memset(vst[l][j][:, :, :, 0:1], 1.0).then_inc(stage_free[j], 8)
                for side in beside:
                    side.work(pool)

            @block.tensor
            def _(pe):
                with pe.Fori(0, PAIRS) as it:
                    for j in range(2):
                        pe.wait_ge(c_lo, it * 2 + (j + 1))
                        for n, (l, kind, m, s) in enumerate(tiles):
                            if j == 0 and (n == 0 or tiles[n - 1][:2] != (l, kind)):
                                pe.wait_ge(w_lo, 2 * l + (2 if kind == "v" else 1))
                            pe.wait_ge(lo_done, tile_no(it, j, n + 1))
                            bank = chip.banks[(j * NTILE + n) % NB]
                            q = 0
                            for k in range(KT):
                                if kind == "k":
                                    ws = slice(m * P, (m + 1) * P)
                                    out, wi = bank, 2 * l
                                    products = [(wh[wi][:, k, ws], chi[j][:, k, :]), (wh[wi][:, k, ws], clo[j][:, k, :]),
                                                (wl[wi][:, k, ws], chi[j][:, k, :])]
                                else:
                                    cs, ws = slice(s * P, (s + 1) * P), slice(m * VW[l], (m + 1) * VW[l])
                                    out, wi = bank[:, 0:VW[l]], 2 * l + 1
                                    products = [(chi[j][:, k, cs], wh[wi][:, k, ws]), (chi[j][:, k, cs], wl[wi][:, k, ws]),
                                                (clo[j][:, k, cs], wh[wi][:, k, ws])]
                                for a, b in products:
                                    last = pe.matmul(out, a, b, start=(q == 0), stop=(q == 3 * KT - 1))
                                    q += 1
                            last.then_inc(tile_ready, 1)

            @block.scalar
            def _(act):
                for i in range(4):
                    act.wait_ge(context.w_loaded[i], 16)
                    act.activation(wh[i][:], wf[i][:], ACT.Copy).then_inc(w_hi, 1)
                    if i == 1:
                        act.wait_ge(c_loaded[0], 16)
                        act.activation(chi[0][:], cf[0][:], ACT.Copy).then_inc(c_hi, 1)
                act.wait_ge(context.bk_loaded, 16)

                def step(it, j, last):
                    act.wait_ge(stage_free[j], it * (OUTS * 16) + 16)
                    for n, (l, kind, m, s) in enumerate(tiles):
                        if n == NTILE // 2 and not last:
                            act.wait_ge(c_loaded[1 - j], it * 16 + 16 * (1 + j))
                            act.activation(chi[1 - j][:], cf[1 - j][:], ACT.Copy).then_inc(c_hi, 1)
                        act.wait_ge(tile_ready, tile_no(it, j, n + 1))
                        src, hi, _lo = halves(j, n)
                        if l == 1 and kind == "k":
                            act.activation(hi, src, ACT.Identity, bias=bk[:, m:m + 1]).then_inc(hi_done, 1)
                        else:
                            act.activation(hi, src, ACT.Copy).then_inc(hi_done, 1)

                with act.Fori(0, PAIRS - 1) as it:
                    for j in range(2):
                        step(it, j, False)
                step(PAIRS - 1, 0, False)
                step(PAIRS - 1, 1, True)

            @block.vector
            def _(dve):
                dve.memset(chip.half[:, 7:8], -0.5).then_inc(lo_done, NB)
                for i in range(4):
                    dve.wait_ge(w_hi, i + 1)
                    dve.tensor_tensor(wl[i][:], wf[i][:], wh[i][:], ALU.subtract).then_inc(w_lo, 1)
                    if i == 1:
                        dve.wait_ge(c_hi, 1)
                        dve.tensor_tensor(clo[0][:], cf[0][:], chi[0][:], ALU.subtract).then_inc(c_lo, 1)
                dve.wait_ge(mask_in, 16)
                dve.tensor_scalar(m16[:], m8[:], 60000.0, -60000.0, ALU.mult, ALU.add).then_inc(mask_made, 1)

                def step(it, j, last):
                    for n, (l, kind, m, s) in enumerate(tiles):
                        if n == NTILE // 2 and not last:
                            dve.wait_ge(c_hi, it * 2 + (j + 2))
                            dve.tensor_tensor(clo[1 - j][:], cf[1 - j][:], chi[1 - j][:], ALU.subtract).then_inc(c_lo, 1)
                        dve.wait_ge(hi_done, tile_no(it, j, n + 1))
                        src, hi, lo = halves(j, n)
                        if l == 1 and kind == "k":
                            dve.scalar_tensor_tensor(out=lo, in0=src, scalar=bk[:, m:m + 1], in1=hi,
                                                     op0=ALU.add, op1=ALU.subtract).then_inc(lo_done, 1)
                        else:
                            dve.tensor_tensor(lo, src, hi, ALU.subtract).then_inc(lo_done, 1)

                with dve.Fori(0, PAIRS - 1) as it:
                    for j in range(2):
                        step(it, j, False)
                step(PAIRS - 1, 0, False)
                step(PAIRS - 1, 1, True)


def project_queries(chip, tag, weight, bias_q, hd, q_dram, early=None):
    nc = chip.nc
    MT = NH * hd // P
    with ExitStack() as scope:
        w = weight.w
        bq = chip.sb(f"{tag}_bq", [P, MT], F32, scope)
        qh = chip.sb(f"{tag}_qh", [P, MT, TOK], F16, scope)
        ql = chip.sb(f"{tag}_ql", [P, MT, TOK], F16, scope)
        loaded, ready, hi, lo, out = (chip.sem(f"{tag}_{n}") for n in ("ld", "rdy", "hi", "lo", "out"))
        with nc.Block() as block:
            @block.sync
            def _(sp):
                if bias_q is not None:
                    sp.dma_start(bq[:], bias_q).then_inc(loaded, 16)
                if early is not None:
                    early(sp)
                qd = q_dram.rearrange("h (m p) t -> h p m t", p=P)
                sp.wait_ge(hi, MT)
                sp.dma_start(qd[0], qh[:]).then_inc(out, 16)
                sp.wait_ge(lo, MT)
                sp.dma_start(qd[1], ql[:]).then_inc(out, 16)
                sp.wait_ge(out, 32)

            @block.tensor
            def _(pe):
                pe.wait_ge(weight.loaded, 16)
                for m in range(MT):
                    if m >= 4:
                        pe.wait_ge(lo, m - 3)
                    for k in range(KT):
                        last = pe.matmul(chip.banks[m % 4], w[:, k, m * P:(m + 1) * P], chip.xnT[:, k, :],
                                         start=(k == 0), stop=(k == KT - 1))
                    last.then_inc(ready, 1)

            @block.scalar
            def _(act):
                for m in range(MT):
                    act.wait_ge(ready, m + 1)
                    if bias_q is None:
                        act.activation(qh[:, m, :], chip.banks[m % 4], ACT.Copy).then_inc(hi, 1)
                    else:
                        if m == 0:
                            act.wait_ge(loaded, 16)
                        act.activation(qh[:, m, :], chip.banks[m % 4], ACT.Identity, bias=bq[:, m:m + 1]).then_inc(hi, 1)

            @block.vector
            def _(dve):
                for m in range(MT):
                    dve.wait_ge(hi, m + 1)
                    if bias_q is None:
                        dve.tensor_tensor(ql[:, m, :], chip.banks[m % 4], qh[:, m, :], ALU.subtract).then_inc(lo, 1)
                    else:
                        dve.scalar_tensor_tensor(out=ql[:, m, :], in0=chip.banks[m % 4], scalar=bq[:, m:m + 1],
                                                 in1=qh[:, m, :], op0=ALU.add, op1=ALU.subtract).then_inc(lo, 1)


class CrossBuffers:

    def __init__(self, chip, tag, hd, scope, q_dram, k_dram, v_dram):
        self.hd, self.q_dram, self.k_dram, self.v_dram = hd, q_dram, k_dram, v_dram
        small = hd == 16
        KR = P if small else 66
        if small:
            self.k1 = [chip.sb(f"{tag}_k{w}", [P, SK], F16, scope) for w in range(4)]
        else:
            self.k1 = [chip.sb(f"{tag}_k1{w}", [P, SK], F16, scope) for w in range(4)]
            self.k2 = [chip.sb(f"{tag}_k2{w}", [KR, SK], F16, scope) for w in range(4)]
            self.q1 = [chip.sb(f"{tag}_q1{w}", [P, SQ], F16, scope) for w in range(4)]
        self.qa = [chip.sb(f"{tag}_qa{w}", [KR, SQ], F16, scope) for w in range(4)]
        self.qb = [chip.sb(f"{tag}_qb{w}", [KR, SQ], F16, scope) for w in range(4)]
        self.v = [chip.sb(f"{tag}_v{w}", [P, SK // P, 1 + 2 * hd], F16, scope) for w in range(4)]
        self.loaded = [chip.sem(f"{tag}_ld{w}") for w in range(4)]
        self.rows_in = [chip.sem(f"{tag}_rows{w}") for w in range(4)]

    def load_keys_values(self, eng, it, w):
        b, j, hd = w // 2, w % 2, self.hd
        keys, head = slice(b * SK, (b + 1) * SK), bass.ds(it * (2 * hd) + j * hd, hd)
        if hd == 16:
            places = ((self.k1[w], 0, 0), (self.k1[w], 16, 1), (self.k1[w], 32, 0))
        else:
            places = ((self.k1[w], 0, 0), (self.k1[w], 64, 1), (self.k2[w], 0, 0))
        for buf, at, half in places:
            eng.dma_start(buf[at:at + hd, :], self.k_dram[half, head, keys]).then_inc(self.loaded[w], 16)
        vd = self.v_dram[bass.ds(it * 2 + j, 1), :, b * (SK // P):(b + 1) * (SK // P), :]
        eng.dma_start(self.v[w][:], vd.rearrange("h p c e -> p (h c) e")).then_inc(self.loaded[w], 16)

    def load_queries(self, eng, it, w):
        b, j, hd = w // 2, w % 2, self.hd
        toks, head = slice(b * SQ, (b + 1) * SQ), bass.ds(it * (2 * hd) + j * hd, hd)
        if hd == 16:
            places = ((self.qa[w], 0, 0), (self.qa[w], 16, 0), (self.qa[w], 32, 1))
        else:
            places = ((self.q1[w], 0, 0), (self.q1[w], 64, 0), (self.qa[w], 0, 1))
        for buf, at, half in places:
            eng.dma_start(buf[at:at + hd, :], self.q_dram[half, head, toks]).then_inc(self.loaded[w], 16)


def cross_attention(chip, tag, buffers, att, mask_rows=None, key_rows=None, q_rows=None, after=()):
    nc = chip.nc
    hd = buffers.hd
    small = hd == 16
    GR = 8
    GK = SK // P // GR
    NA = 2 * SK // 512
    AI = NA + 1
    VC = 1 + 2 * hd
    NP = 8
    VL = 3
    W = 4
    PAIRS = NH // 2
    KR = 64 if small else 66
    MC = 49 if small else 64
    POOL_GROUPS = (1, 2, 4, 5, 6, 7) if small else (1, 2, 4, 5, 7)
    VECTOR_GROUPS = tuple(g for g in range(GR) if g not in POOL_GROUPS)
    with ExitStack() as scope:
        qa, qb, v, loaded, rows_in = buffers.qa, buffers.qb, buffers.v, buffers.loaded, buffers.rows_in
        if small:
            kbuf = buffers.k1
        else:
            k1, k2, q1 = buffers.k1, buffers.k2, buffers.q1
        prob = [chip.sb(f"{tag}_p{i}", [P, GK, SQ], F32, scope) for i in range(NP)]
        rest = [chip.sb(f"{tag}_r{i}", [P, GK, SQ], F16, scope) for i in range(NP)]
        mx = [chip.sb(f"{tag}_mx{i}", [P, 2, NA // 2], F32, scope) for i in range(2)]
        nm = [chip.sb(f"{tag}_nm{i}", [P, 2], F32, scope) for i in range(2)]
        nmh = [chip.sb(f"{tag}_nmh{i}", [P, 2], F16, scope) for i in range(2)]
        mcol = [chip.sb(f"{tag}_mcol{i}", [P, 2, P], F32, scope) for i in range(2)]
        rd = [chip.sb(f"{tag}_rd{i}", [P, 2], F32, scope) for i in range(2)]
        ov = [chip.sb(f"{tag}_ov{i}", [P, 2, hd], F32, scope) for i in range(2)]
        preset = [chip.sem(f"{tag}_preset{w}") for w in range(W)]
        s_ready, p_ready = chip.sem(f"{tag}_s"), chip.sem(f"{tag}_p")
        a_ready, a_done = chip.sem(f"{tag}_a"), chip.sem(f"{tag}_ad")
        rest_dve, rest_pool = chip.sem(f"{tag}_rv"), chip.sem(f"{tag}_rp")
        pv_done, o_step, m_step = chip.sem(f"{tag}_pv"), chip.sem(f"{tag}_o"), chip.sem(f"{tag}_m")
        NLOAD = 7
        PRESETS = 3 if small else 1
        ROWS = 48 if small else 16
        cleared, passed = chip.sem(f"{tag}_cleared"), chip.sem(f"{tag}_passed")
        SP_, PP_, AP_, OP_ = 2, NP, 2, 8
        NPOOL = len(POOL_GROUPS)

        def k_pass2(w, c):
            ks = slice(c * P, (c + 1) * P)
            if small:
                return [(kbuf[w][:, ks], qb[w][:, :])]
            return [(k1[w][:, ks], q1[w][:, :]), (k2[w][:, ks], qb[w][:, :])]

        def k_pass1(w, qt, c):
            qs, ks = slice(qt * P, (qt + 1) * P), slice(c * 512, (c + 1) * 512)
            if small:
                return qa[w][:, qs], kbuf[w][:, ks]
            return q1[w][:, qs], k1[w][:, ks]

        def group_no(it, w, g):
            return it * (W * GR) + (w * GR + g)

        def a_no(it, w, n):
            return it * (W * AI) + (w * AI + n)

        def ahead(it, w, n):
            w += n
            if w >= W:
                w, it = w - W, it + 1
                if isinstance(it, int) and it >= PAIRS:
                    return None
            return it, w

        def a_work(it, w, g):
            if g < 4:
                u = ahead(it, w, 1)
                return [(u, NA // 2 + 2 * g + i) for i in range(2)] if u else []
            u = ahead(it, w, 2)
            uses = [(u, 2 * (g - 4) + i) for i in range(2)] if u else []
            n = ahead(it, w, 1)
            return [(n, "t")] + uses if g == 5 and n else uses

        order = {}
        seq = ([(0, n) for n in range(NA)] + [(1, 0), (1, 1), (0, "t")] + [(1, n) for n in range(2, NA // 2)])
        for u in range(3 * W):
            for g in range(GR):
                for (uu, n) in a_work(0, 0, g):
                    seq.append((u + uu[1], n))
        for i, key in enumerate(seq):
            order[key] = i
        assert order[(1 + W, 0)] - order[(1, 0)] == W * AI and W * AI % 2 == 0

        def a_base(it, w, n):
            if isinstance(it, int) and it == 0 and (w, n) in ((0, 0), (0, 1)):
                return n
            if isinstance(it, int) and it == PAIRS - 1 and (w, n) == (W - 1, "t"):
                return order[(w + W, n)] - W * AI - 2
            return order[(w + W, n)] - W * AI

        def a_use(it, w, n):
            return it * (W * AI) + a_base(it, w, n)

        def a_bank(it, w, n):
            return chip.a_ps[a_base(it, w, n) % 2]

        LEAD = ([((0, 0), n) for n in range(NA)] + [((0, 1), 0), ((0, 1), 1), ((0, 0), "t")]
                + [((0, 1), n) for n in range(2, NA // 2)])

        def all_units(eng, body, first):
            first()
            body(0, 0)
            with eng.Fori(0, PAIRS - 1) as it:
                for w in range(1, W):
                    body(it, w)
                body(it + 1, 0)
            for w in range(1, W):
                body(PAIRS - 1, w)

        with nc.Block() as block:
            @block.sync
            def _(sp):
                for w in range(W):
                    sp.wait_ge(preset[w], PRESETS)
                    if small:
                        sp.dma_start(kbuf[w][48:49, :], mask_rows[w // 2:w // 2 + 1, :]).then_inc(rows_in[w], 16)
                        sp.dma_start(kbuf[w][49:51, :], key_rows).then_inc(rows_in[w], 16)
                        buffers.load_keys_values(sp, 0, w)
                for p in after:
                    p.loads(sp)
                with sp.Fori(0, PAIRS - 1) as it:
                    for w in range(W):
                        hold(sp, pv_done, group_no(it, w, GR) + PP_, passed)
                        buffers.load_keys_values(sp, it + 1, w)
                        buffers.load_queries(sp, it + 1, w)
                sp.wait_ge(pv_done, group_no(PAIRS - 1, W - 1, GR) + PP_)

            @block.tensor
            def _(pe):
                def scores(it, w, g, half):
                    if g == 0 and half == 0:
                        pe.wait_ge(a_done, a_use(it, w, "t") + 1 + AP_)
                    pe.wait_ge(p_ready, group_no(it, w, g) + 1)
                    out = chip.s_ps[g % 2]
                    for c in (2 * half, 2 * half + 1):
                        products = k_pass2(w, g * GK + c)
                        for i, (a, b) in enumerate(products):
                            last = pe.matmul(out[:, c * SQ:(c + 1) * SQ], a, b, start=(i == 0), stop=(i == len(products) - 1))
                    if half:
                        last.then_inc(s_ready, 1)

                def maxima(u, n):
                    it, w = u
                    pe.wait_ge(a_done, a_use(it, w, n) + 1)
                    if n == "t":
                        pe.wait_ge(m_step, it * (W * 4) + (w * 4 + 4))
                        for qt in range(2):
                            last = pe.transpose(a_bank(it, w, n)[:, qt * P:(qt + 1) * P], mcol[w % 2][:, qt, :], chip.ident[:])
                    else:
                        if n == 0:
                            pe.wait_ge(preset[w], PRESETS)
                            pe.wait_ge(rows_in[w], ROWS)
                            pe.wait_ge(loaded[w], it * (16 * NLOAD) + 16 * NLOAD)
                        a, b = k_pass1(w, n // (NA // 2), n % (NA // 2))
                        last = pe.matmul(a_bank(it, w, n)[:], a, b, start=True, stop=True)
                    last.then_inc(a_ready, 1)

                def values(it, w, g, half):
                    if g == 0 and half == 0:
                        pe.wait_ge(o_step, it * (W * 4) + (w * 4 + 3))
                    pe.wait_ge(p_ready, group_no(it, w, g) + 1 + SP_)
                    o = chip.o_ps[w % 2]
                    if g in POOL_GROUPS:
                        pe.wait_ge(rest_pool, it * (W * NPOOL) + (w * NPOOL + POOL_GROUPS.index(g) + 1))
                    else:
                        n = len(VECTOR_GROUPS)
                        pe.wait_ge(rest_dve, it * (2 * W * n) + 2 * (w * n + VECTOR_GROUPS.index(g) + 1))
                    for c in (2 * half, 2 * half + 1):
                        for qt in range(2):
                            qs = slice(qt * P, (qt + 1) * P)
                            hi = prob[g % NP][:, c, qs].bitcast(BF16).rearrange("p (q t) -> p q t", t=2)[:, :, 1]
                            first, end = g == 0 and c == 0, g == GR - 1 and c == GK - 1
                            pe.matmul(o[:, qt * VC:(qt + 1) * VC], hi, v[w][:, g * GK + c, :],
                                      start=first and qt == 0, stop=False, skip_group_check=True)
                            last = pe.matmul(o[:, qt * VC:qt * VC + 1 + hd], rest[g % NP][:, c, qs],
                                             v[w][:, g * GK + c, 0:1 + hd], start=False, stop=end, skip_group_check=True)
                    if half:
                        last.then_inc(pv_done, 1)

                def values_before(it, w, g, half):
                    if g >= VL:
                        values(it, w, g - VL, half)
                    elif not (isinstance(it, int) and it == 0 and w == 0):
                        values(it - (w == 0), (w - 1) % W, GR + g - VL, half)

                def first():
                    for a in LEAD:
                        maxima(*a)
                    for g in range(2):
                        for half in range(2):
                            scores(0, 0, g, half)

                def unit(it, w):
                    for g in range(GR):
                        u = (it, w) if g + 2 < GR else ahead(it, w, 1)
                        work = a_work(it, w, g)
                        if u:
                            scores(u[0], u[1], (g + 2) % GR, 0)
                        for a in work[:-1]:
                            maxima(*a)
                        if u:
                            scores(u[0], u[1], (g + 2) % GR, 1)
                        values_before(it, w, g, 0)
                        for a in work[-1:]:
                            maxima(*a)
                        values_before(it, w, g, 1)

                all_units(pe, unit, first)
                for g in range(GR - VL, GR):
                    for half in range(2):
                        values(PAIRS - 1, W - 1, g, half)

            @block.scalar
            def _(act):
                for w in range(W):
                    act.wait_ge(preset[w], PRESETS)
                    if small:
                        act.dma_start(qa[w][48:64, :], q_rows).then_inc(rows_in[w], 16)
                    buffers.load_queries(act, 0, w)

                def unit(it, w):
                    for g in range(GR):
                        act.wait_ge(s_ready, group_no(it, w, g) + 1)
                        act.wait_ge(pv_done, group_no(it, w, g) + 1)
                        act.activation(prob[g % NP][:], chip.s_ps[g % 2][:].rearrange("p (c q) -> p c q", q=SQ),
                                       ACT.Exp, scale=hd ** -0.5).then_inc(p_ready, 1)

                all_units(act, unit, lambda: None)

            def remainder(eng, sem, it, w, g, cs=slice(0, GK)):
                eng.wait_ge(p_ready, group_no(it, w, g) + 1 + SP_)
                hi = prob[g % NP][:, cs, :].bitcast(BF16).rearrange("p c (q t) -> p c q t", t=2)[:, :, :, 1]
                eng.tensor_tensor(rest[g % NP][:, cs, :], prob[g % NP][:, cs, :], hi, ALU.subtract).then_inc(sem, 1)

            @block.gpsimd
            def _(pool):
                for i in range(2):
                    pool.memset(mcol[i][:], 0.0).then_inc(cleared, 1)
                if small:
                    for w in (2, 3):
                        for t in (kbuf[w], qa[w], qb[w]):
                            pool.memset(t[:], 0.0).then_inc(preset[w], 1)

                def unit(it, w):
                    for g in POOL_GROUPS:
                        remainder(pool, rest_pool, it, w, g)

                all_units(pool, unit, lambda: None)

            @block.vector
            def _(dve):
                def maxima(u, n):
                    it, w = u
                    dve.wait_ge(a_ready, a_use(it, w, n) + 1)
                    if n == "t":
                        dve.tensor_tensor(qb[w][0:KR, :], a_bank(it, w, n)[0:KR, 0:SQ], qa[w][0:KR, :], ALU.add).then_inc(a_done, 1)
                        return
                    dve.tensor_reduce(mx[w % 2][:, n // (NA // 2), n % (NA // 2):n % (NA // 2) + 1], a_bank(it, w, n)[:],
                                      AX.X, ALU.max).then_inc(a_done, 1)
                    if n == NA - 1:
                        steps = it * (W * 4) + w * 4
                        i = w % 2
                        dve.wait_ge(a_done, a_use(it, w, n) + 1 + AP_)
                        dve.tensor_reduce(nm[i][:], mx[i][:], AX.X, ALU.max, negate=True).then_inc(m_step, 1)
                        dve.wait_ge(m_step, steps + 1)
                        dve.tensor_copy(nmh[i][:], nm[i][:]).then_inc(m_step, 1)
                        dve.wait_ge(m_step, steps + 2)
                        dve.tensor_copy(mcol[i][:, :, MC], nmh[i][:]).then_inc(m_step, 1)
                        dve.tensor_tensor(mcol[i][:, :, MC + 1], nm[i][:], nmh[i][:], ALU.subtract).then_inc(m_step, 1)

                def output(it, w):
                    i, steps = w % 2, it * (W * 4) + w * 4 + OP_
                    o = chip.o_ps[i][:, 0:2 * VC].rearrange("p (t e) -> p t e", e=VC)
                    dve.wait_ge(pv_done, group_no(it, w, GR) + PP_)
                    dve.reciprocal(rd[i][:], o[:, :, 0]).then_inc(o_step, 1)
                    dve.tensor_copy(ov[i][:], o[:, :, 1 + hd:VC]).then_inc(o_step, 1)
                    dve.wait_ge(o_step, steps + 2)
                    dve.tensor_tensor(ov[i][:], o[:, :, 1:1 + hd], ov[i][:], ALU.add).then_inc(o_step, 1)
                    dve.wait_ge(o_step, steps + 3)
                    b, j = w // 2, w % 2
                    out = att[:, 2 * b:2 * b + 2, bass.ds(it * (2 * hd) + j * hd, hd)]
                    dve.tensor_tensor(out, ov[i][:], rd[i][:].unsqueeze(2).to_broadcast([P, 2, hd]), ALU.mult).then_inc(o_step, 1)

                def first():
                    if small:
                        for w in (0, 1):
                            for t in (kbuf[w], qa[w], qb[w]):
                                dve.memset(t[:], 0.0).then_inc(preset[w], 1)
                    else:
                        for w in range(W):
                            dve.memset(qa[w][64:66, :], 0.0).then_inc(preset[w], 1)
                    dve.memset(nmh[0][:], 0.0).then_inc(p_ready, SP_)
                    dve.memset(nm[0][:], 0.0).then_inc(pv_done, PP_)
                    dve.memset(nm[1][:], 0.0).then_inc(a_done, AP_)
                    dve.memset(nmh[1][:], 0.0).then_inc(o_step, OP_)
                    dve.wait_ge(o_step, OP_)
                    dve.wait_ge(a_done, AP_)
                    dve.wait_ge(cleared, 2)
                    for a in LEAD:
                        maxima(*a)
                    for h in range(2):
                        remainder(dve, rest_dve, 0, 0, 0, slice(2 * h, 2 * h + 2))

                def unit(it, w):
                    for g in range(GR):
                        u = (it, w) if g + 1 < GR else ahead(it, w, 1)
                        work = a_work(it, w, g)
                        for a in work[:-1]:
                            maxima(*a)
                        for h in range(2):
                            if u and (g + 1) % GR in VECTOR_GROUPS:
                                remainder(dve, rest_dve, u[0], u[1], (g + 1) % GR, slice(2 * h, 2 * h + 2))
                            if h == 0:
                                for a in work[-1:]:
                                    maxima(*a)
                        if g == VL + 1 and not (isinstance(it, int) and it == 0 and w == 0):
                            output(it - (w == 0), (w - 1) % W)

                all_units(dve, unit, first)
                output(PAIRS - 1, W - 1)


def rows_project(chip, tag, src, dims, weight, finish, bias_in=None, after=()):
    nc = chip.nc
    K = dims // P
    with ExitStack() as scope:
        w = weight.w
        srcT = chip.sb(f"{tag}_srcT", [P, K, TOK], F32, scope)
        bi = chip.sb(f"{tag}_bi", [P, K], F32, scope)
        bias_ld, tr, tr_out, ready, done = (chip.sem(f"{tag}_{n}") for n in ("bld", "tr", "trout", "rdy", "done"))
        tbank = chip.s_banks
        with nc.Block() as block:
            @block.sync
            def _(sp):
                if bias_in is not None:
                    sp.dma_start(bi[:], bias_in).then_inc(bias_ld, 16)
                    weight.loads(sp)
                    sp.wait_ge(bias_ld, 16)
                for p in after:
                    p.loads(sp)

            @block.gpsimd
            def _(pool):
                for p in after:
                    p.work(pool)

            @block.tensor
            def _(pe):
                for k in range(K):
                    if k >= 2:
                        pe.wait_ge(tr_out, k - 1)
                    for t in range(NT):
                        last = pe.transpose(tbank[k % 2][:, t * P:(t + 1) * P], src[:, t, k * P:(k + 1) * P], chip.ident[:])
                    last.then_inc(tr, 1)
                pe.wait_ge(weight.loaded, 16)
                pe.wait_ge(tr_out, K)
                for t in range(NT):
                    for k in range(K):
                        last = pe.matmul(chip.banks[t][:, 0:D], srcT[:, k, t * P:(t + 1) * P], w[:, k, :],
                                         start=(k == 0), stop=(k == K - 1))
                    last.then_inc(ready, 1)

            @block.scalar
            def _(act):
                for k in range(K):
                    act.wait_ge(tr, k + 1)
                    if bias_in is None:
                        act.activation(srcT[:, k, :], tbank[k % 2][:], ACT.Copy).then_inc(tr_out, 1)
                    else:
                        if k == 0:
                            act.wait_ge(bias_ld, 16)
                        act.activation(srcT[:, k, :], tbank[k % 2][:], ACT.Identity, bias=bi[:, k:k + 1]).then_inc(tr_out, 1)

            @block.vector
            def _(dve):
                for t in range(NT):
                    dve.wait_ge(ready, t + 1)
                    finish(dve, t, done)
                dve.wait_ge(done, NT)


def add_to_x(chip):
    def finish(dve, t, done):
        dve.tensor_tensor(chip.x[:, t, :], chip.banks[t][:, 0:D], chip.x[:, t, :], ALU.add).then_inc(done, 1)
    return finish


class NormRows:

    def __init__(self, chip, scope, bo, gamma, beta):
        self.chip, self.src = chip, (bo, gamma, beta)
        self.rows = [chip.sb(f"nr_row{i}", [P, D], F32, scope) for i in range(3)]
        self.residual = chip.sb("nr_residual", [P, NT, D], F32, scope)
        self.shifted = chip.sb("nr_shifted", [P, NT, D], F32, scope)
        self.loaded, self.made = chip.sem("nr_ld"), chip.sem("nr_made")

    def wide(self, i):
        return self.rows[i][:].unsqueeze(1).to_broadcast([P, NT, D])

    def loads(self, sp):
        for r, d in zip(self.rows, self.src):
            sp.dma_start(r[:], d.partition_broadcast(P)).then_inc(self.loaded, 16)

    def work(self, pool):
        pool.wait_ge(self.loaded, 48)
        pool.tensor_tensor(self.residual[:], self.chip.xn[:], self.wide(0), ALU.add).then_inc(self.made, 1)
        pool.tensor_tensor(self.shifted[:], self.chip.x[:], self.wide(2), ALU.add).then_inc(self.made, 1)


def normed_output(chip, tag, acc, rows):
    nc = chip.nc
    with ExitStack() as scope:
        st = chip.sb(f"{tag}_st", [P, NT, 6], F32, scope)
        mv = chip.sb(f"{tag}_mv", [P, NT, 2], F32, scope)
        ve = chip.sb(f"{tag}_ve", [P, NT], F32, scope)
        rs = chip.sb(f"{tag}_rs", [P, NT], F32, scope)
        step, var, rstd = (chip.sem(f"{tag}_{n}") for n in ("step", "var", "rstd"))
        with nc.Block() as block:
            @block.gpsimd
            def _(pool):
                pool.wait_ge(var, 1)
                pool.tensor_tensor(rs[:], ve[:], chip.half[:, 0:NT], ALU.pow).then_inc(rstd, 1)

            @block.vector
            def _(dve):
                for t in range(NT):
                    dve.bn_stats(st[:, t, :], acc[:, t, :]).then_inc(step, 1)
                dve.wait_ge(step, NT)
                for t in range(NT):
                    dve.bn_aggr(mv[:, t, :], st[:, t, :]).then_inc(step, 1)
                dve.wait_ge(step, 2 * NT)
                dve.tensor_scalar(ve[:], mv[:, :, 1], 1e-5, None, ALU.add).then_inc(var, 1)
                dve.wait_ge(rstd, 1)
                for t in range(NT):
                    dve.tensor_scalar(acc[:, t, :], acc[:, t, :], mv[:, t, 0:1], rs[:, t:t + 1],
                                      ALU.subtract, ALU.mult).then_inc(step, 1)
                dve.wait_ge(step, 3 * NT)
                dve.tensor_tensor(acc[:], acc[:], rows.wide(1), ALU.mult).then_inc(step, 1)
                dve.wait_ge(step, 1 + 3 * NT)
                dve.tensor_tensor(chip.x[:], rows.shifted[:], acc[:], ALU.add).then_inc(step, 1)
                dve.wait_ge(step, 2 + 3 * NT)


class SpectralScale:

    def __init__(self, chip, tag, scope, w_dram, n, u_dram, sp_dram, out):
        self.chip, self.n, self.out = chip, n, out
        self.w_dram, self.u_dram, self.sp_dram = w_dram, u_dram, sp_dram
        self.w = chip.sb(f"{tag}_w", [P, KT, n], F32, scope)
        self.u = chip.sb(f"{tag}_u", [P, n], F32, scope)
        self.prm = chip.sb(f"{tag}_prm", [P, 1], F32, scope)
        self.wu = chip.sb(f"{tag}_wu", [P, KT, n], F32, scope)
        self.a = chip.sb(f"{tag}_a", [P, KT], F32, scope)
        self.q = chip.sb(f"{tag}_q", [P, 8], F32, scope)
        self.loaded, self.step = chip.sem(f"{tag}_ld"), chip.sem(f"{tag}_step")

    def loads(self, sp):
        sp.dma_start(self.w[:], self.w_dram.rearrange("(k p) n -> p k n", p=P)).then_inc(self.loaded, 16)
        sp.dma_start(self.u[:], self.u_dram.partition_broadcast(P)).then_inc(self.loaded, 16)
        sp.dma_start(self.prm[:], self.sp_dram.partition_broadcast(P)).then_inc(self.loaded, 16)

    def work(self, pool):
        w, u, wu, a, q, n = self.w, self.u, self.wu, self.a, self.q, self.n
        done = 0

        def link(ins):
            nonlocal done
            done += 1
            ins.then_inc(self.step, 1)
            pool.wait_ge(self.step, done)

        def folded(t, width):
            while width > 1:
                h = width // 2
                link(pool.tensor_tensor(t[:, 0:h], t[:, 0:h], t[:, h:2 * h], ALU.add))
                if width % 2:
                    link(pool.tensor_tensor(t[:, 0:1], t[:, 0:1], t[:, 2 * h:width], ALU.add))
                width = h

        pool.wait_ge(self.loaded, 48)
        link(pool.memset(q[:, 6:7], 0.5))
        link(pool.memset(q[:, 7:8], -0.5))
        for k in range(KT):
            link(pool.tensor_tensor(wu[:, k, :], w[:, k, :], u[:], ALU.mult))
            folded(wu[:, k, :], n)
            link(pool.tensor_copy(a[:, k:k + 1], wu[:, k, 0:1]))
            link(pool.tensor_tensor(q[:, k:k + 1], a[:, k:k + 1], a[:, k:k + 1], ALU.mult))
        link(pool.tensor_tensor(q[:, 0:1], q[:, 0:1], q[:, 1:2], ALU.add))
        link(pool.partition_all_reduce(q[:, 2:3], q[:, 0:1], P, bass.bass_isa.ReduceOp.add))
        for k in range(KT):
            link(pool.tensor_tensor(wu[:, k, :], w[:, k, :], a[:, k:k + 1].to_broadcast([P, n]), ALU.mult))
        link(pool.tensor_tensor(wu[:, 0, :], wu[:, 0, :], wu[:, 1, :], ALU.add))
        link(pool.partition_all_reduce(wu[:, 1, :], wu[:, 0, :], P, bass.bass_isa.ReduceOp.add))
        link(pool.tensor_tensor(wu[:, 0, :], wu[:, 1, :], wu[:, 1, :], ALU.mult))
        folded(wu[:, 0, :], n)
        link(pool.tensor_tensor(q[:, 3:4], q[:, 2:3], q[:, 6:7], ALU.pow))
        link(pool.tensor_tensor(q[:, 4:5], wu[:, 0, 0:1], q[:, 7:8], ALU.pow))
        link(pool.tensor_tensor(q[:, 5:6], q[:, 3:4], q[:, 4:5], ALU.mult))
        link(pool.tensor_tensor(self.out, q[:, 5:6], self.prm[:], ALU.mult))


def self_attention(chip, tag, weights, select, att, beside, scale=None, mask=None, centre=None, scales=None):
    nc = chip.nc
    NG = NH // 4
    NQK = 2 * NG
    with ExitStack() as scope:
        w = [p.w for p in weights]
        stack = [chip.sb(f"{tag}_stack{i}", [P, 2 * NG, TOK], F16, scope) for i in range(2)]
        v = chip.sb(f"{tag}_v", [P, NT, NH, 2, 16], F16, scope)
        sel = chip.sb(f"{tag}_sel", [P, 8, P], F16, scope)
        hi = [chip.sb(f"{tag}_hi{i}", [P, TOK], F16, scope) for i in range(2)]
        lo = [chip.sb(f"{tag}_lo{i}", [P, TOK], F16, scope) for i in range(2)]
        raw = [chip.sb(f"{tag}_raw{i}", [P, TOK], F32, scope) for i in range(2)]
        sqr = [chip.sb(f"{tag}_sqr{i}", [P, TOK], F32, scope) for i in range(2)]
        cm = chip.sb(f"{tag}_cm", [P, 2, P], F32, scope)
        mk = chip.sb(f"{tag}_mk", [P, P], F32, scope)
        mkb = chip.sb(f"{tag}_mkb", [P, 3, P], BF16, scope)
        s4 = chip.sb(f"{tag}_s4", [P, 1], F32, scope)
        pr = [chip.sb(f"{tag}_pr{i}", [P, 4, SQ], F32, scope) for i in range(2)]
        pT = [[chip.sb(f"{tag}_pT{i}{j}", [P, 8, P], F16, scope) for j in range(2)] for i in range(2)]
        pw = [chip.sb(f"{tag}_pw{i}", [P, 4, 16], F32, scope) for i in range(2)]
        nm = [chip.sb(f"{tag}_nm{i}", [P, 4], F32, scope) for i in range(4)]
        sm = [chip.sb(f"{tag}_sm{i}", [P, 4], F32, scope) for i in range(4)]
        rc = [chip.sb(f"{tag}_rc{i}", [P, 4], F32, scope) for i in range(2)]
        names = ("ld", "pj", "rawo", "cen", "sqd", "s4d", "hid", "lod", "sl", "eva", "evd", "mkd",
                 "sr", "nmd", "ex", "tra", "trb", "toh", "tol", "pv", "od", "rcd", "vhd", "vld", "pwd")
        (ld, pj, rawo, cen, sqd, s4d, hid, lod, sl, eva, evd, mkd,
         sr, nmd, ex, tra, trb, toh, tol, pv, od, rcd, vhd, vld, pwd) = (chip.sem(f"{tag}_{x}") for x in names)
        NLD = 16 + (16 if mask is not None else 0) + (16 if centre is not None else 0)
        steps = [(t, g) for t in range(NT) for g in range(NG)]
        NS = len(steps)
        LAG = 1 if centre is None else 3

        def scale_of(n):
            if scale is not None:
                return s4[:] if n < NG else scale
            return 1 / 16 if n < NG else 1.0

        def src(n):
            return chip.a_ps[n % 2][:] if centre is None else chip.o_ps[n % 2][:]

        def use(u):
            if u < NT:
                return chip.s_banks[u][:, 0:D].rearrange("p (h e) -> p h e", e=16), v[:, u, :, 0, :]
            n, s = (u - NT) // 2, (u - NT) % 2
            return chip.s_banks[u % 4], stack[n // NG][:, 2 * (n % NG) + s, :]

        def nkeys(i):
            return 1 if mask is not None and steps[i][0] % 2 == 0 else 2

        def slot(j):
            return (j % 2) * 2 + j // 2

        with nc.Block() as block:
            @block.sync
            def _(sp):
                sp.dma_start(sel[:], select.rearrange("c p m -> p c m")).then_inc(ld, 16)
                if mask is not None:
                    sp.dma_start(mk[:], mask).then_inc(ld, 16)
                if centre is not None:
                    sp.dma_start(cm[:], centre.rearrange("c p m -> p c m")).then_inc(ld, 16)
                for side in beside:
                    side.loads(sp)
                sp.wait_ge(ld, NLD)

            @block.gpsimd
            def _(pool):
                for side in beside:
                    side.work(pool)

            @block.tensor
            def _(pe):
                pe.wait_ge(weights[2].loaded, 16)
                for t in range(NT):
                    for k in range(KT):
                        last = pe.matmul(chip.s_banks[t][:, 0:D], chip.xnT[:, k, t * P:(t + 1) * P], w[2][:, k, :],
                                         start=(k == 0), stop=(k == KT - 1))
                    last.then_inc(sl, 1)
                pe.wait_ge(weights[0].loaded, 16)
                pe.wait_ge(weights[1].loaded, 16)
                pe.wait_ge(ld, NLD)
                for n in range(NQK + LAG):
                    if n < NQK:
                        if n >= 2:
                            pe.wait_ge(lod if centre is None else rawo, n - 1)
                        for k in range(KT):
                            last = pe.matmul(chip.a_ps[n % 2][:], w[n // NG][:, k, (n % NG) * P:(n % NG + 1) * P],
                                             chip.xnT[:, k, :], start=(k == 0), stop=(k == KT - 1))
                        last.then_inc(pj, 1)
                    if centre is not None and 0 <= n - 1 < NQK:
                        m = n - 1
                        pe.wait_ge(rawo, m + 1)
                        if m >= 2:
                            pe.wait_ge(lod, m - 1)
                        pe.matmul(chip.o_ps[m % 2][:], cm[:, 0, :], raw[m % 2][:], start=True, stop=False,
                                  skip_group_check=True).then_inc(cen, 1)
                    if centre is not None and 0 <= n - 2 < NQK:
                        m = n - 2
                        pe.wait_ge(sqd, m + 1)
                        pe.matmul(chip.o_ps[m % 2][:], cm[:, 1, :], sqr[m % 2][:], start=False, stop=True,
                                  skip_group_check=True).then_inc(mkd, 1)
                    m = n - LAG
                    if m >= 0:
                        pe.wait_ge(lod, m + 1)
                        for s in range(2):
                            u = NT + 2 * m + s
                            if m < 2:
                                pe.wait_ge(vld, u - 3)
                            else:
                                pe.wait_ge(evd if u % 2 else eva, m - 1)
                            i = 4 * (m // NG) + s
                            pe.matmul(chip.s_banks[u % 4], sel[:, i, :], hi[m % 2][:], start=True, stop=False)
                            last = pe.matmul(chip.s_banks[u % 4], sel[:, i + 2, :], lo[m % 2][:], start=False, stop=True)
                            last.then_inc(sl, 1)

                def scores(i):
                    t, g = steps[i]
                    b, nk = t // 2, nkeys(i)
                    if i >= 2:
                        pe.wait_ge(ex, i - 1)
                    for j in range(4):
                        r, at = slice(64 * (j % 2), 64 * (j % 2) + 64), slot(j) * SQ
                        last = pe.matmul(chip.s_ps[i % 2][:, at:at + nk * P],
                                         stack[0][r, 2 * g + j // 2, t * P:(t + 1) * P],
                                         stack[1][r, 2 * g + j // 2, b * SQ:b * SQ + nk * P], start=True, stop=mask is None)
                        if mask is not None:
                            last = pe.matmul(chip.s_ps[i % 2][:, at:at + nk * P], mkb[:, 0, :], mkb[:, 3 - nk:3, :],
                                             start=False, stop=True)
                    last.then_inc(sr, 1)

                def values(i):
                    t, g = steps[i]
                    nk = nkeys(i)
                    pe.wait_ge(tol, 2 * i + 2)
                    if i >= 2:
                        pe.wait_ge(od, i - 1)
                    for j in range(4):
                        o = chip.o_ps[i % 2][:, 32 * j:32 * j + 32]
                        for kt in range(nk):
                            vh = v[:, 2 * (t // 2) + kt, 4 * g + j, :, :]
                            pe.matmul(o, pT[i % 2][0][:, slot(j) * 2 + kt, :], vh.rearrange("p a e -> p (a e)"),
                                      start=(j == 0 and kt == 0), stop=False, skip_group_check=True)
                            last = pe.matmul(o[:, 0:16], pT[i % 2][1][:, slot(j) * 2 + kt, :], vh[:, 0, :],
                                             start=False, stop=(j == 3 and kt == nk - 1), skip_group_check=True)
                    last.then_inc(pv, 1)

                pe.wait_ge(eva, NQK)
                pe.wait_ge(evd, NQK)
                if mask is not None:
                    pe.wait_ge(mkd, 3)
                scores(0)
                scores(1)
                for i in range(NS):
                    pe.wait_ge(ex, i + 1)
                    if i + 2 < NS:
                        scores(i + 2)
                    for h, tr in enumerate((tra, trb)):
                        if i >= 1:
                            pe.wait_ge(tol, 2 * i - 1 + h)
                        for a in (0, 1):
                            for kt in range(nkeys(i)):
                                last = pe.transpose(chip.a_ps[h][:, (2 * a + kt) * P:(2 * a + kt + 1) * P],
                                                    pr[i % 2][:, 2 * h + a, kt * P:(kt + 1) * P], chip.ident[:])
                        last.then_inc(tr, 1)
                    if i >= 1:
                        values(i - 1)
                values(NS - 1)

            def transposed(h, i):
                def part(t):
                    return t.rearrange("p (a k) q -> p a k q", k=2)[:, :, 0:nkeys(i), :]
                at = slice(4 * h, 4 * h + 4)
                return part(chip.a_ps[h][:].rearrange("p (a q) -> p a q", q=P)), part(pT[i % 2][0][:, at, :]), part(pT[i % 2][1][:, at, :])

            @block.scalar
            def _(act):
                if scale is not None:
                    act.activation(s4[:], scale, ACT.Copy, scale=0.25).then_inc(s4d, 1)
                    act.wait_ge(s4d, 1)
                else:
                    act.activation(s4[:], chip.ones[:, 0:1], ACT.Copy).then_inc(s4d, 1)
                for u in range(NT):
                    act.wait_ge(sl, u + 1)
                    source, out = use(u)
                    act.activation(out, source, ACT.Copy, scale=(scale if scale is not None else 1.0)).then_inc(vhd, 1)
                for n in range(NQK + LAG):
                    if centre is not None and n < NQK:
                        act.wait_ge(pj, n + 1)
                        if n >= 2:
                            act.wait_ge(cen, n - 1)
                        act.activation(raw[n % 2][:], chip.a_ps[n % 2][:], ACT.Copy).then_inc(rawo, 1)
                    if centre is not None and 0 <= n - 1 < NQK:
                        m = n - 1
                        act.wait_ge(cen, m + 1)
                        if m >= 2:
                            act.wait_ge(mkd, m - 1)
                        act.activation(sqr[m % 2][:], chip.o_ps[m % 2][:], ACT.Square).then_inc(sqd, 1)
                    m = n if centre is None else n - 2
                    if 0 <= m < NQK:
                        act.wait_ge(pj if centre is None else mkd, m + 1)
                        if m >= 2:
                            act.wait_ge(sl, NT + 2 * (m - 1))
                        act.activation(hi[m % 2][:], src(m), ACT.Copy, scale=scale_of(m)).then_inc(hid, 1)
                    m = n - LAG
                    if m >= 0:
                        u = NT + 2 * m
                        act.wait_ge(sl, u + 1)
                        source, out = use(u)
                        act.activation(out, source, ACT.Copy).then_inc(eva, 1)

                def exps(i):
                    act.wait_ge(nmd, i + 1)
                    if i >= 2:
                        act.wait_ge(trb, i - 1)
                    if i >= 4:
                        act.wait_ge(rcd, i - 3)
                    n = nkeys(i) * P
                    for j in range(4):
                        last = act.activation(pr[i % 2][:, j, 0:n], chip.s_ps[i % 2][:, j * SQ:j * SQ + n], ACT.Exp,
                                              bias=nm[i % 4][:, j:j + 1], accum_out=sm[i % 4][:, j:j + 1])
                    last.then_inc(ex, 1)

                exps(0)
                for i in range(NS):
                    if i + 1 < NS:
                        exps(i + 1)
                    for h, tr in enumerate((tra, trb)):
                        act.wait_ge(tr, i + 1)
                        if i >= 2 and h == 0:
                            act.wait_ge(pv, i - 1)
                        source, up, _low = transposed(h, i)
                        act.activation(up, source, ACT.Copy).then_inc(toh, 1)

            @block.vector
            def _(dve):
                dve.wait_ge(s4d, 1)
                if mask is not None:
                    dve.wait_ge(ld, NLD)
                    dve.tensor_copy(mkb[:, 0, :], chip.ident[:]).then_inc(mkd, 1)
                    dve.memset(mkb[:, 1, :], 0.0).then_inc(mkd, 1)
                    dve.tensor_copy(mkb[:, 2, :], mk[:]).then_inc(mkd, 1)
                for u in range(NT):
                    dve.wait_ge(vhd, u + 1)
                    source, out = use(u)
                    low = v[:, u, :, 1, :]
                    dve.scalar_tensor_tensor(out=low, in0=source, scalar=(scale if scale is not None else 1.0), in1=out,
                                             op0=ALU.mult, op1=ALU.subtract).then_inc(vld, 1)
                for n in range(NQK + LAG):
                    m = n if centre is None else n - 2
                    if 0 <= m < NQK:
                        dve.wait_ge(hid, m + 1)
                        dve.scalar_tensor_tensor(out=lo[m % 2][:], in0=src(m), scalar=scale_of(m), in1=hi[m % 2][:],
                                                 op0=ALU.mult, op1=ALU.subtract).then_inc(lod, 1)
                    m = n - LAG
                    if m >= 0:
                        u = NT + 2 * m + 1
                        dve.wait_ge(sl, u + 1)
                        source, out = use(u)
                        dve.tensor_copy(out, source).then_inc(evd, 1)

                def maxima(i):
                    dve.wait_ge(sr, i + 1)
                    if i >= 4:
                        dve.wait_ge(ex, i - 3)
                    s_in = chip.s_ps[i % 2].rearrange("p (j c) -> p j c", j=4)[:, :, 0:nkeys(i) * P]
                    dve.tensor_reduce(nm[i % 4][:], s_in, AX.X, ALU.max, negate=True).then_inc(nmd, 1)

                def output(i):
                    t, g = steps[i]
                    dve.wait_ge(pv, i + 1)
                    dve.reciprocal(rc[i % 2][:], sm[i % 4][:]).then_inc(rcd, 1)
                    dve.wait_ge(rcd, i + 1)
                    inv = rc[i % 2][:].rearrange("p (a b) -> p b a", a=2).unsqueeze(3).to_broadcast([P, 2, 2, 16])
                    halves = chip.o_ps[i % 2][:, 0:128].rearrange("p (j a e) -> p j a e", a=2, e=16)
                    dve.tensor_copy(pw[i % 2][:], halves[:, :, 1, :]).then_inc(pwd, 1)
                    dve.wait_ge(pwd, 2 * i + 1)
                    dve.tensor_tensor(pw[i % 2][:], halves[:, :, 0, :], pw[i % 2][:], ALU.add).then_inc(pwd, 1)
                    dve.wait_ge(pwd, 2 * i + 2)
                    dve.tensor_tensor(att[:, t, g * 64:(g + 1) * 64].rearrange("p (b a e) -> p b a e", b=2, e=16),
                                      pw[i % 2][:].rearrange("p (b a) e -> p b a e", b=2), inv, ALU.mult).then_inc(od, 1)

                maxima(0)
                maxima(1)
                for i in range(NS):
                    if i + 2 < NS:
                        maxima(i + 2)
                    for h in range(2):
                        dve.wait_ge(toh, 2 * i + h + 1)
                        source, up, low = transposed(h, i)
                        dve.tensor_tensor(low, source, up, ALU.subtract).then_inc(tol, 1)
                    if i >= 1:
                        output(i - 1)
                    if scales is not None and i < 3:
                        scales(dve, i)
                output(NS - 1)
                dve.wait_ge(od, NS)


class ExpertWeights:

    def __init__(self, chip, scope, w1T, w2T, pT, uT, b2, tri):
        L, DA = 12, 64
        self.pw = chip.sb("ew_pw", [P, KT, DA], F32, scope)
        self.uw = chip.sb("ew_uw", [DA, 3 * L], F32, scope)
        self.bb = chip.sb("ew_bb", [L, D], F32, scope)
        self.tri = chip.sb("ew_tri", [P, L, L], F32, scope)
        self.router = ((self.pw[:], pT.rearrange("(k p) n -> p k n", p=P)), (self.uw[:], uT), (self.bb[:], b2),
                       (self.tri[:], tri.rearrange("a b -> (a b)").partition_broadcast(P)))
        self.router_loaded = chip.sem("ew_rld")
        self.src = (w1T, w2T)
        self.ws = [chip.sb(f"ew{i}", [P, KT, 12 * D], F32, scope) for i in range(2)]
        self.hi = [chip.sb(f"ewh{i}", [P, KT, 12 * D], F16, scope) for i in range(2)]
        self.lo = [chip.sb(f"ewl{i}", [P, KT, 12 * D], F16, scope) for i in range(2)]
        self.loaded, self.split = chip.sem("ew_ld"), chip.sem("ew_split")

    def loads(self, sp):
        for i in range(2):
            sp.dma_start(self.ws[i][:], self.src[i].rearrange("(k p) n -> p k n", p=P)).then_inc(self.loaded, 16)
        for place, source in self.router:
            sp.dma_start(place, source).then_inc(self.router_loaded, 16)

    def halve(self, pool, i):
        pool.tensor_copy(self.hi[i][:], self.ws[i][:]).then_inc(self.split, 1)
        pool.wait_ge(self.split, 2 * i + 1)
        pool.tensor_tensor(self.lo[i][:], self.ws[i][:], self.hi[i][:], ALU.subtract).then_inc(self.split, 1)

    def work(self, pool):
        pool.wait_ge(self.loaded, 32)
        self.halve(pool, 0)


def experts(chip, tag, weights):
    nc = chip.nc
    L, DA = 12, 64
    NC3 = NT * 3
    with ExitStack() as scope:
        pw, uw, bb, tr_, ld = weights.pw, weights.uw, weights.bb, weights.tri, weights.router_loaded
        xh = [chip.sb(f"{tag}_xh{i}", [P, KT, TOK], F16, scope) for i in range(2)]
        xl = [chip.sb(f"{tag}_xl{i}", [P, KT, TOK], F16, scope) for i in range(2)]
        xa = chip.sb(f"{tag}_xa", [DA, TOK], F32, scope)
        z = chip.sb(f"{tag}_z", [P, NC3, L], F32, scope)
        gt = chip.sb(f"{tag}_gt", [P, NC3, L, L], F32, scope)
        eq = chip.sb(f"{tag}_eq", [P, NC3, L, L], F32, scope)
        rk = chip.sb(f"{tag}_rk", [P, NC3, L], F32, scope)
        mz = chip.sb(f"{tag}_mz", [P, NC3], F32, scope)
        ez = chip.sb(f"{tag}_ez", [P, NC3, L], F32, scope)
        cz = chip.sb(f"{tag}_cz", [P, NC3, L], F32, scope)
        c3T = chip.sb(f"{tag}_c3T", [L, TOK], F32, scope)
        y = [chip.sb(f"{tag}_y{i}", [P, NT, D], F32, scope) for i in range(2)]
        hid = chip.sb(f"{tag}_hid", [P, NT, D], F32, scope)
        names = ("xlo", "xap", "xao", "zp", "zc", "rt", "exd", "c3p", "c3o", "ep", "acc", "gl", "ht", "hto", "bp")
        xlo, xap, xao, zp, zc, rt, exd, c3p, c3o, ep, acc, gl, ht, hto, bp = (chip.sem(f"{tag}_{x}") for x in names)
        PAIRS = L // 2
        tiles = [(e, t) for e in range(PAIRS) for t in range(NT)]
        NTL = len(tiles)
        with nc.Block() as block:
            @block.gpsimd
            def _(pool):
                weights.halve(pool, 1)

            @block.tensor
            def _(pe):
                pe.wait_ge(ld, 64)
                for k in range(KT):
                    last = pe.matmul(chip.banks[0][0:DA, :], pw[:, k, :], chip.xnT[:, k, :], start=(k == 0), stop=(k == KT - 1))
                last.then_inc(xap, 1)
                pe.wait_ge(xao, 1)
                for t in range(NT):
                    last = pe.matmul(chip.banks[1][:, t * 3 * L:(t + 1) * 3 * L], xa[:, t * P:(t + 1) * P], uw[:],
                                     start=True, stop=True)
                last.then_inc(zp, 1)

                def mixture(i):
                    pe.wait_ge(xlo, i * KT + KT)
                    pe.wait_ge(weights.split, 2 * i + 2)
                    for n, (e, t) in enumerate(tiles):
                        m = i * NTL + n
                        if m >= 4:
                            pe.wait_ge(acc, 2 * (m - 3))
                        for k in range(KT):
                            ts, es = slice(t * P, (t + 1) * P), slice(e * 2 * D, (e + 1) * 2 * D)
                            products = ((xh[i], weights.hi[i]), (xh[i], weights.lo[i]), (xl[i], weights.hi[i]))
                            for q, (a, b) in enumerate(products):
                                last = pe.matmul(chip.banks[4 + n % 4], a[:, k, ts], b[:, k, es],
                                                 start=(k == 0 and q == 0), stop=(k == KT - 1 and q == 2))
                        last.then_inc(ep, 1)

                mixture(0)
                pe.wait_ge(rt, 10)
                for t in range(NT):
                    last = pe.transpose(chip.banks[2][0:L, t * P:(t + 1) * P], cz[:, t * 3 + 2, :], chip.ident[:])
                last.then_inc(c3p, 1)
                for k in range(KT):
                    for t in range(NT):
                        pe.wait_ge(gl, t + 1)
                        last = pe.transpose(chip.banks[k][:, t * P:(t + 1) * P], hid[:, t, k * P:(k + 1) * P], chip.ident[:])
                    last.then_inc(ht, 1)
                mixture(1)
                pe.wait_ge(c3o, 1)
                for t in range(NT):
                    last = pe.matmul(chip.banks[t // 2][:, (t % 2) * D:(t % 2 + 1) * D], c3T[:, t * P:(t + 1) * P], bb[:],
                                     start=True, stop=True)
                last.then_inc(bp, 1)

            @block.scalar
            def _(act):
                act.wait_ge(xap, 1)
                act.activation(xa[:], chip.banks[0][0:DA, :], ACT.Copy).then_inc(xao, 1)
                for k in range(KT):
                    act.activation(xh[0][:, k, :], chip.xnT[:, k, :], ACT.Copy).then_inc(hto, 1)
                act.wait_ge(rt, 7)
                act.activation(ez[:], ez[:], ACT.Exp).then_inc(exd, 1)
                act.wait_ge(acc, 2 * NTL)
                for t in range(NT):
                    act.activation(hid[:, t, :], y[0][:, t, :], ACT.Gelu).then_inc(gl, 1)
                act.wait_ge(c3p, 1)
                act.activation(c3T[:], chip.banks[2][0:L, :], ACT.Copy).then_inc(c3o, 1)
                for k in range(KT):
                    act.wait_ge(ht, k + 1)
                    act.activation(xh[1][:, k, :], chip.banks[k], ACT.Copy).then_inc(hto, 1)

            @block.vector
            def _(dve):
                for k in range(KT):
                    dve.wait_ge(hto, k + 1)
                    dve.tensor_tensor(xl[0][:, k, :], chip.xnT[:, k, :], xh[0][:, k, :], ALU.subtract).then_inc(xlo, 1)
                dve.wait_ge(zp, 1)
                dve.wait_ge(ld, 64)
                dve.tensor_copy(z[:], chip.banks[1][:, 0:NC3 * L].rearrange("p (c l) -> p c l", l=L)).then_inc(zc, 1)
                dve.wait_ge(zc, 1)
                for c in range(NC3):
                    zj = z[:, c, :].unsqueeze(1).to_broadcast([P, L, L])
                    zi = z[:, c, :].unsqueeze(2).to_broadcast([P, L, L])
                    dve.tensor_tensor(gt[:, c], zj, zi, ALU.is_gt)
                    last = dve.tensor_tensor(eq[:, c], zj, zi, ALU.is_equal)
                last.then_inc(rt, 1)
                dve.tensor_reduce(mz[:], z[:], AX.X, ALU.max).then_inc(rt, 1)
                dve.wait_ge(rt, 2)
                dve.tensor_tensor(eq[:].rearrange("p c i j -> p c (i j)"), eq[:].rearrange("p c i j -> p c (i j)"),
                                  tr_[:].rearrange("p i j -> p (i j)").unsqueeze(1).to_broadcast([P, NC3, L * L]), ALU.mult).then_inc(rt, 1)
                dve.wait_ge(rt, 3)
                dve.tensor_tensor(gt[:], gt[:], eq[:], ALU.add).then_inc(rt, 1)
                dve.wait_ge(rt, 4)
                dve.tensor_reduce(rk[:], gt[:], AX.X, ALU.add).then_inc(rt, 1)
                dve.wait_ge(rt, 5)
                dve.tensor_scalar(rk[:], rk[:], 2.5, None, ALU.is_lt).then_inc(rt, 1)
                dve.tensor_tensor(ez[:], z[:], mz[:].unsqueeze(2).to_broadcast([P, NC3, L]), ALU.subtract).then_inc(rt, 1)
                dve.wait_ge(exd, 1)
                dve.wait_ge(rt, 7)
                dve.tensor_tensor(ez[:], ez[:], rk[:], ALU.mult).then_inc(rt, 1)
                dve.wait_ge(rt, 8)
                dve.tensor_reduce(mz[:], ez[:], AX.X, ALU.add).then_inc(rt, 1)
                dve.wait_ge(rt, 9)
                dve.reciprocal(mz[:], mz[:]).then_inc(zc, 1)
                dve.wait_ge(zc, 2)
                dve.tensor_tensor(cz[:], ez[:], mz[:].unsqueeze(2).to_broadcast([P, NC3, L]), ALU.mult).then_inc(rt, 1)
                dve.wait_ge(rt, 10)
                for i in range(2):
                    if i == 1:
                        for k in range(KT):
                            dve.wait_ge(hto, KT + k + 1)
                            dve.tensor_tensor(xl[1][:, k, :], chip.banks[k], xh[1][:, k, :], ALU.subtract).then_inc(xlo, 1)
                    for n, (e, t) in enumerate(tiles):
                        m = i * NTL + n
                        dve.wait_ge(ep, m + 1)
                        for h in range(2):
                            src = chip.banks[4 + n % 4][:, h * D:(h + 1) * D]
                            c = cz[:, t * 3 + i, 2 * e + h:2 * e + h + 1]
                            if e == 0 and h == 0:
                                dve.tensor_scalar(y[i][:, t, :], src, c, None, ALU.mult).then_inc(acc, 1)
                            else:
                                dve.wait_ge(acc, 2 * m + h if h else 2 * (m - NT) + 2)
                                dve.scalar_tensor_tensor(out=y[i][:, t, :], in0=src, scalar=c, in1=y[i][:, t, :],
                                                         op0=ALU.mult, op1=ALU.add).then_inc(acc, 1)
                dve.wait_ge(acc, 4 * NTL)
                dve.tensor_tensor(chip.x[:], chip.x[:], y[1][:], ALU.add).then_inc(zc, 1)
                dve.wait_ge(bp, 1)
                dve.wait_ge(zc, 3)
                for t in range(NT):
                    dve.tensor_tensor(chip.x[:, t, :], chip.banks[t // 2][:, (t % 2) * D:(t % 2 + 1) * D], chip.x[:, t, :],
                                      ALU.add).then_inc(zc, 1)
                dve.wait_ge(zc, 3 + NT)


MAGIC = 12582912.0


class DequantisedWeights:

    def __init__(self, chip, tag, scope, mats, outs):
        self.mats = mats
        F = 1536
        self.NBK = F // 32
        self.w = [chip.sb(f"{tag}_w{i}", [P, self.NBK, 32], F32, scope) for i in range(3)]
        self.s = [chip.sb(f"{tag}_s{i}", [P, self.NBK], F32, scope) for i in range(3)]
        self.r = [chip.sb(f"{tag}_r{i}", [P, self.NBK], F32, scope) for i in range(3)]
        self.loaded, self.step, self.scaled = (chip.sem(f"{tag}_{n}") for n in ("ld", "step", "scaled"))
        self.jobs = []
        for i in range(3):
            rows, cols = mats[i].shape
            o = rows // P
            wv = self.flat(i)
            for k in range(cols // P):
                for o0 in range(0, o, 4):
                    on = min(4, o - o0)
                    self.jobs.append((i, outs[i][:, k, o0 * P:(o0 + on) * P],
                                      [wv[:, o0 + a, k * P:(k + 1) * P] for a in range(on)]))

    def flat(self, i):
        return self.w[i][:].rearrange("p b e -> p (b e)").rearrange("p (o c) -> p o c", o=self.mats[i].shape[0] // P)

    def loads(self, sp):
        for i in range(3):
            sp.dma_start(self.flat(i), self.mats[i].rearrange("(o p) c -> p o c", p=P)).then_inc(self.loaded, 16)

    def scales(self, dve, i):
        w, s, r = self.w[i], self.s[i], self.r[i]
        dve.wait_ge(self.loaded, 48)
        dve.tensor_reduce(s[:], w[:], AX.X, ALU.max, apply_absolute_value=True).then_inc(self.scaled, 1)
        dve.wait_ge(self.scaled, 3 * i + 1)
        dve.tensor_scalar(s[:], s[:], 1.0 / 7.0, 1e-12, ALU.mult, ALU.max).then_inc(self.scaled, 1)
        dve.wait_ge(self.scaled, 3 * i + 2)
        dve.reciprocal(r[:], s[:]).then_inc(self.scaled, 1)

    def work(self, pool):
        done = 0

        def link(ins):
            nonlocal done
            done += 1
            ins.then_inc(self.step, 1)
            pool.wait_ge(self.step, done)

        NBK = self.NBK
        for i in range(3):
            w, s, r = self.w[i], self.s[i], self.r[i]
            wide = lambda a: a[:].unsqueeze(2).to_broadcast([P, NBK, 32])
            pool.wait_ge(self.scaled, 3 * (i + 1))
            link(pool.tensor_tensor(w[:], w[:], wide(r), ALU.mult))
            link(pool.tensor_scalar(w[:], w[:], MAGIC, MAGIC, ALU.add, ALU.subtract))
            link(pool.tensor_scalar(w[:], w[:], 7.0, -8.0, ALU.min, ALU.max))
            link(pool.tensor_tensor(w[:], w[:], wide(s), ALU.mult))


def quantised_ffn(chip, tag, dequantised, upT, gateT, downT, out_dram):
    nc = chip.nc
    I6 = 6
    QM = 32767.0
    with ExitStack() as scope:
        xq = chip.sb(f"{tag}_xq", [P, KT, TOK], F32, scope)
        up = chip.sb(f"{tag}_up", [P, I6, TOK], F32, scope)
        gate = chip.sb(f"{tag}_gate", [P, I6, TOK], F32, scope)
        sg = chip.sb(f"{tag}_sg", [P, I6, TOK], F32, scope)
        am = chip.sb(f"{tag}_am", [P, 5], F32, scope)
        cm = chip.sb(f"{tag}_cm", [P, 2 * I6], F32, scope)
        magic = chip.sb(f"{tag}_magic", [P, 1], F32, scope)
        cmd, magic_set = chip.sem(f"{tag}_cmd"), chip.sem(f"{tag}_magic")
        ar = chip.sb(f"{tag}_ar", [P, 5], F32, scope)
        sc = chip.sb(f"{tag}_sc", [P, 5], F32, scope)
        rc = chip.sb(f"{tag}_rc", [P, 5], F32, scope)
        st, amd, ard, mm, ev, sgd, dn, out, qd = (chip.sem(f"{tag}_{x}") for x in ("st", "amd", "ard", "mm", "ev", "sgd", "dn", "out", "qd"))
        stored, tr, tro = chip.sem(f"{tag}_stored"), chip.sem(f"{tag}_tr"), chip.sem(f"{tag}_tro")
        with nc.Block() as block:
            @block.vector
            def _(dve):
                n = 0

                def link(ins):
                    nonlocal n
                    n += 1
                    ins.then_inc(st, 1)
                    dve.wait_ge(st, n)

                def scale(i, factor=1.0 / QM):
                    dve.wait_ge(ard, i + 1)
                    link(dve.tensor_scalar(sc[:, i:i + 1], ar[:, i:i + 1], factor, 1e-12, ALU.mult, ALU.max))
                    link(dve.reciprocal(rc[:, i:i + 1], sc[:, i:i + 1]))

                def rounded(t, src, factor):
                    link(dve.tensor_scalar(t, src, factor, MAGIC, ALU.mult, ALU.add))
                    link(dve.tensor_scalar(t, t, MAGIC + QM, MAGIC - QM - 1.0, ALU.min, ALU.max))

                def qdq(i, t, src):
                    scale(i)
                    rounded(t, src, rc[:, i:i + 1])
                    dve.tensor_scalar(t, t, MAGIC, sc[:, i:i + 1], ALU.subtract, ALU.mult).then_inc(qd, 1)

                def chunk_maxima(first):
                    for n in range(first, first + I6):
                        dve.wait_ge(ev, n + 1)
                        dve.tensor_reduce(cm[:, n:n + 1], (gate if n < I6 else up)[:, n % I6, :], AX.X, ALU.max, apply_absolute_value=True).then_inc(cmd, 1)
                    dve.wait_ge(cmd, first + I6)
                    i = 1 + first // I6
                    dve.tensor_reduce(am[:, i:i + 1], cm[:, first:first + I6], AX.X, ALU.max).then_inc(amd, 1)

                dve.memset(magic[:], MAGIC).then_inc(magic_set, 1)
                dve.tensor_reduce(am[:, 0:1], chip.xnT[:], AX.XY, ALU.max, apply_absolute_value=True).then_inc(amd, 1)
                qdq(0, xq[:], chip.xnT[:])
                chunk_maxima(0)
                qdq(1, gate[:], gate[:])
                chunk_maxima(I6)
                qdq(2, up[:], up[:])
                dve.wait_ge(qd, 3)
                dve.wait_ge(sgd, 2)
                link(dve.tensor_scalar(sg[:], sg[:], MAGIC + 65535.0, MAGIC, ALU.min, ALU.max))
                link(dve.scalar_tensor_tensor(out=gate[:], in0=sg[:], scalar=MAGIC, in1=gate[:], op0=ALU.subtract, op1=ALU.mult))
                dve.tensor_reduce(am[:, 3:4], gate[:], AX.XY, ALU.max, apply_absolute_value=True).then_inc(amd, 1)
                scale(3, 2.0 ** -16 / QM)
                link(dve.tensor_scalar(rc[:, 3:4], rc[:, 3:4], 2.0 ** -16, None, ALU.mult))
                rounded(gate[:], gate[:], rc[:, 3:4])
                link(dve.scalar_tensor_tensor(out=gate[:], in0=gate[:], scalar=MAGIC, in1=up[:], op0=ALU.subtract, op1=ALU.mult))
                dve.tensor_reduce(am[:, 4:5], gate[:], AX.XY, ALU.max, apply_absolute_value=True).then_inc(amd, 1)
                dve.wait_ge(ard, 5)
                link(dve.tensor_scalar(ar[:, 4:5], ar[:, 4:5], sc[:, 3:4], None, ALU.mult))
                scale(4)
                link(dve.tensor_tensor(rc[:, 4:5], rc[:, 4:5], sc[:, 3:4], ALU.mult))
                rounded(gate[:], gate[:], rc[:, 4:5])
                dve.tensor_scalar(gate[:], gate[:], MAGIC, sc[:, 4:5], ALU.subtract, ALU.mult).then_inc(qd, 1)
                for t in range(NT):
                    dve.wait_ge(dn, t + 1)
                    dve.tensor_tensor(chip.x[:, t, :], chip.banks[t][:, 0:D], chip.x[:, t, :], ALU.add).then_inc(out, 1)

            @block.gpsimd
            def _(pool):
                for i in range(5):
                    pool.wait_ge(amd, i + 1)
                    pool.partition_all_reduce(ar[:, i:i + 1], am[:, i:i + 1], P, bass.bass_isa.ReduceOp.absmax).then_inc(ard, 1)

            jobs = dequantised.jobs

            @block.tensor
            def _(pe):
                for n, (_i, _dst, srcs) in enumerate(jobs):
                    if n >= 4:
                        pe.wait_ge(tro, n - 3)
                    for a, src in enumerate(srcs):
                        last = pe.transpose(chip.banks[4 + n % 4][:, a * P:(a + 1) * P], src, chip.ident[:])
                    last.then_inc(tr, 1)
                pe.wait_ge(tro, len(jobs))
                pe.wait_ge(qd, 1)
                for n in range(2 * I6):
                    w = gateT if n < I6 else upT
                    m = n % I6
                    if n >= 4:
                        pe.wait_ge(ev, n - 3)
                    for k in range(KT):
                        last = pe.matmul(chip.banks[n % 4], w[:, k, m * P:(m + 1) * P], xq[:, k, :],
                                         start=(k == 0), stop=(k == KT - 1))
                    last.then_inc(mm, 1)
                pe.wait_ge(ev, 2 * I6)
                pe.wait_ge(qd, 4)
                for t in range(NT):
                    for k in range(I6):
                        last = pe.matmul(chip.banks[t][:, 0:D], gate[:, k, t * P:(t + 1) * P], downT[:, k, :],
                                         start=(k == 0), stop=(k == I6 - 1))
                    last.then_inc(dn, 1)

            @block.scalar
            def _(act):
                for n, (_i, dst, srcs) in enumerate(jobs):
                    act.wait_ge(tr, n + 1)
                    act.activation(dst, chip.banks[4 + n % 4][:, 0:len(srcs) * P], ACT.Copy).then_inc(tro, 1)
                for n in range(2 * I6):
                    act.wait_ge(mm, n + 1)
                    act.activation((gate if n < I6 else up)[:, n % I6, :], chip.banks[n % 4], ACT.Copy).then_inc(ev, 1)
                act.wait_ge(qd, 2)
                act.activation(sg[:], gate[:], ACT.Sigmoid).then_inc(sgd, 1)
                act.wait_ge(sgd, 1)
                act.wait_ge(magic_set, 1)
                act.activation(sg[:], sg[:], ACT.Identity, bias=magic[:], scale=65536.0).then_inc(sgd, 1)

            @block.sync
            def _(sp):
                ov = out_dram.rearrange("(t p) d -> p t d", p=P)
                for t in range(NT):
                    sp.wait_ge(out, t + 1)
                    sp.dma_start(ov[:, t, :], chip.x[:, t, :]).then_inc(stored, 16)
                sp.wait_ge(stored, 16 * NT)


def perceiver(nc, t, out):
    with ExitStack() as ctx:
        chip = Chip(nc, ctx)
        scratch = [(nc.dram_tensor(f"keys{l}", [2, NH * hd, B * SK], F16).ap(),
                    nc.dram_tensor(f"values{l}", [NH, P, B * SK // P, 1 + 2 * hd], F16).ap())
                   for l, hd in enumerate((16, 64))]
        queries = [nc.dram_tensor(f"queries{l}", [2, NH * hd, TOK], F16).ap() for l, hd in enumerate((16, 64))]
        mask_out = nc.dram_tensor("mask_rows", [B, SK], F16).ap()
        sc = chip.sb("sn", [P, 2], F32)

        with ExitStack() as scope:
            spectral = [SpectralScale(chip, "sq", scope, t["s0w"], 3 * D, t["s0u"], t["s0s"], sc[:, 0:1]),
                        SpectralScale(chip, "sp", scope, t["s0p"], D, t["s0pu"], t["s0ps"], sc[:, 1:2])]
            context = Context(chip, scope, t["ctxT"], [(t["a0k"], t["a0v"]), (t["a1k"], t["a1v"])], t["a1bk"])
            with ExitStack() as inner:
                wq = Prefetch(chip, "q0", inner, t["a0q"])
                load_constants(chip, t["x"], wq, context)
                layer_norm(chip, "ln0")
                project_queries(chip, "q0", wq, None, 16, queries[0])
            project_context(chip, context, t["mask"], mask_out, scratch, spectral)

        with ExitStack() as block0:
            wo = Prefetch(chip, "o0", block0, t["a0o"])
            weights = [Prefetch(chip, f"s0{n}", block0, t[f"s0{n}"]) for n in "qkv"]
            with ExitStack() as scope:
                att = chip.sb("att0", [P, NT, D], F32, scope)
                with ExitStack() as inner:
                    buffers = CrossBuffers(chip, "x0", 16, inner, queries[0], *scratch[0])
                    cross_attention(chip, "x0", buffers, att, mask_out, t["ones2"], t["qrows"], after=[wo, *weights])
                rows_project(chip, "o0", att, D, wo, add_to_x(chip))

            layer_norm(chip, "ln1")
            with ExitStack() as scope:
                expert_weights = ExpertWeights(chip, scope, t["f0w1"], t["f0w2"], t["f0p"], t["f0u"], t["f0b"], t["tri"])
                att = chip.sb("att1", [P, NT, D], F32, scope)
                wo = Prefetch(chip, "o1", scope, t["s0p"])
                self_attention(chip, "s0", weights, t["select"], att, [expert_weights, wo], scale=sc[:, 0:1], mask=t["causal"])

                def finish(dve, n, done):
                    dve.scalar_tensor_tensor(out=chip.x[:, n, :], in0=chip.banks[n][:, 0:D], scalar=sc[:, 1:2],
                                             in1=chip.x[:, n, :], op0=ALU.mult, op1=ALU.add).then_inc(done, 1)
                rows_project(chip, "o1", att, D, wo, finish)

                layer_norm(chip, "ln2")
                experts(chip, "moe", expert_weights)
        chip.recycle_semaphores()

        with ExitStack() as scope:
            acc = chip.sb("acc1", [P, NT, D], F32, scope)
            att = chip.sb("att2", [P, NT, NH * 64], F32, scope)
            with ExitStack() as inner:
                buffers = CrossBuffers(chip, "x1", 64, inner, queries[1], *scratch[1])

                def early(sp):
                    for w in range(4):
                        sp.dma_start(buffers.k2[w][64:66, :], t["ones2"]).then_inc(buffers.rows_in[w], 16)
                        buffers.load_keys_values(sp, 0, w)
                with ExitStack() as innermost:
                    wq = Prefetch(chip, "q1", innermost, t["a1q"])
                    layer_norm(chip, "ln3", after=[wq])
                    project_queries(chip, "q1", wq, t["a1bq"], 64, queries[1], early)
                cross_attention(chip, "x1", buffers, att)

            wo = Prefetch(chip, "o2", scope, t["a1o"])
            rows = NormRows(chip, scope, t["a1bo"], t["a1g"], t["a1b"])

            def finish(dve, n, done):
                if n == 0:
                    dve.wait_ge(rows.made, 2)
                dve.tensor_tensor(acc[:, n, :], chip.banks[n][:, 0:D], rows.residual[:, n, :], ALU.add).then_inc(done, 1)
            rows_project(chip, "o2", att, NH * 64, wo, finish, bias_in=t["a1bv"], after=[rows])
            normed_output(chip, "no", acc, rows)

        with ExitStack() as scope:
            weights = [Prefetch(chip, f"s1{n}", scope, t[f"s1{n}"]) for n in "qkv"]
            wo = Prefetch(chip, "o3", scope, t["s1o"])
            upT = chip.sb("upT", [P, KT, 768], F32, scope)
            gateT = chip.sb("gateT", [P, KT, 768], F32, scope)
            downT = chip.sb("downT", [P, 6, D], F32, scope)
            dequantised = DequantisedWeights(chip, "dq", scope, [t["f1u"], t["f1g"], t["f1d"]], [upT, gateT, downT])
            layer_norm(chip, "ln4", after=[*weights, wo])
            with ExitStack() as inner:
                att = chip.sb("att3", [P, NT, D], F32, inner)
                self_attention(chip, "s1", weights, t["select"], att, [dequantised], centre=t["centre"], scales=dequantised.scales)
                rows_project(chip, "o3", att, D, wo, add_to_x(chip))
            layer_norm(chip, "ln5")
            quantised_ffn(chip, "f1", dequantised, upT, gateT, downT, out)


def kernel(**inputs):
    import numpy as np
    import concourse.bacc as bacc
    from concourse.bass_utils import run_bass_kernel_spmd

    def a(name):
        return np.asarray(inputs[name])

    def columns(name):
        return a(name).reshape(-1, P).T

    def pad_heads(w):
        out = np.zeros((w.shape[0], NH, 32), w.dtype)
        out[:, :, :16] = w.reshape(w.shape[0], NH, 16)
        return out.reshape(w.shape[0], NH * 32)

    centre = np.zeros((2, P, P), np.float32)
    for h in range(4):
        s = slice(32 * h, 32 * h + 16)
        centre[0, s, s] = np.eye(16) - 1 / 16
        centre[1, s, 32 * h + 16] = 1 / 15
    select = np.zeros((2, 2, 2, P, P), np.float16)
    for kind, halves in enumerate(((0, 0, 1), (0, 1, 0))):
        for at, half in enumerate(halves):
            for pair in range(2):
                for h in range(2):
                    i = 32 * (2 * pair + h)
                    o = 64 * h + 17 * at
                    select[kind, half, pair, i:i + 17, o:o + 17] = np.eye(17)
    select = select.reshape(8, P, P)
    qrows = np.zeros((16, SQ), np.float16)
    qrows[0] = 32768.0
    qkv = a("L0_attn_W_qkv")
    host = {
        "x": a("x").reshape(TOK, D), "ctxT": a("ctx_1024").reshape(B * SK, D).T,
        "mask": a("mask_BxS2_bk1"),
        "ones2": np.ones((2, SK), np.float16), "qrows": qrows,
        "a0q": a("L0_xattn_Wq").T, "a0k": a("L0_xattn_Wk").T, "a0v": a("L0_xattn_Wv").T, "a0o": a("L0_xattn_Wo").T,
        "s0w": qkv, "s0q": pad_heads(qkv[:, 0:D]), "s0k": pad_heads(qkv[:, D:2 * D]), "s0v": qkv[:, 2 * D:],
        "s0u": a("L0_attn_u_qkv"), "s0s": a("L0_attn_sigma_qkv"), "s0p": a("L0_attn_W_proj"),
        "s0pu": a("L0_attn_u_proj"), "s0ps": a("L0_attn_sigma_proj"),
        "causal": np.triu(np.full((P, P), -1e30, np.float32), 1), "select": select,
        "f0p": a("L0_ffn_P_w").T, "f0u": np.concatenate([a("L0_ffn_U1"), a("L0_ffn_U2"), a("L0_ffn_U3")]).T,
        "f0w1": a("L0_ffn_W1").transpose(2, 0, 1).reshape(D, 12 * D),
        "f0w2": a("L0_ffn_W2").transpose(2, 0, 1).reshape(D, 12 * D), "f0b": a("L0_ffn_b2"),
        "tri": np.tril(np.ones((12, 12), np.float32), -1),
        "a1q": a("L1_xattn_Wq"), "a1bq": columns("L1_xattn_bq"), "a1k": a("L1_xattn_Wk"), "a1bk": columns("L1_xattn_bk"),
        "a1v": a("L1_xattn_Wv"), "a1bv": columns("L1_xattn_bv"), "a1o": a("L1_xattn_Wo"), "a1bo": a("L1_xattn_bo"),
        "a1g": a("L1_xattn_ln_gamma"), "a1b": a("L1_xattn_ln_beta"),
        "s1q": pad_heads(a("L1_attn_Wq")), "s1k": pad_heads(a("L1_attn_Wk")), "s1v": a("L1_attn_Wv"),
        "s1o": a("L1_attn_Wo"), "centre": centre,
        "f1g": a("L1_ffn_w_gate"), "f1u": a("L1_ffn_w_up"), "f1d": a("L1_ffn_w_down"),
    }
    nc = bacc.Bacc("TRN2", target_bir_lowering=False, num_devices=1)
    arrays, t = {}, {}
    for name, value in host.items():
        value = np.ascontiguousarray(value)
        arrays[f"in_{name}"] = value
        t[name] = nc.dram_tensor(f"in_{name}", value.shape, mybir.dt.from_np(value.dtype), kind="ExternalInput").ap()
    out = nc.dram_tensor("out_0", (TOK, D), F32, kind="ExternalOutput").ap()
    perceiver(nc, t, out)
    r = run_bass_kernel_spmd(nc, [arrays], core_ids=[0])
    return r.results[0]["out_0"].reshape(B, SQ, D)
```
